# Optimizing a Trainium2 kernel written in Bass

```python
import numpy as np
import jax
import jax.numpy as jnp

def _softmax(x, axis=-1):
    return jax.nn.softmax(x, axis=axis)

def _gelu(x):
    return jax.nn.gelu(x, approximate=True)

def _silu(x):
    return jax.nn.silu(x)

def _sigmoid(x):
    return jax.nn.sigmoid(x)

def _layernorm(x, axis=-1, eps=1e-05):
    m = jnp.mean(x, axis=axis, keepdims=True)
    v = jnp.var(x, axis=axis, keepdims=True)
    return (x - m) / jnp.sqrt(v + eps)

def _scatter_add(tgt, idx, src, axis=0):
    return tgt.at[idx].add(src)

def _segment_sum(src, seg, n):
    return jax.ops.segment_sum(src, seg, n)
kernel_name = 'mk_adaln_d2_jaxref_r4_fdaeff'

def setup_inputs(seed: int=0):
    np.random.seed(seed)
    _w = jnp.asarray

    def _L0_attn_setup():
        import jax, jax.numpy as jnp
        import numpy as np
        H_HEADS = 8
        WIN = 64

        def _layernorm(x, gamma, beta, eps=1e-05):
            mu = jnp.mean(x, axis=-1, keepdims=True)
            var = jnp.var(x, axis=-1, keepdims=True)
            return (x - mu) * jax.lax.rsqrt(var + eps) * gamma + beta
        key = jax.random.key(seed)
        ks = jax.random.split(key, 8)
        B, S, D = (4, 1024, 256)
        F = 4 * D
        s = 0.02
        return {'x': jax.random.normal(ks[0], (B, S, D), dtype=jnp.float32), 'Wq': jax.random.normal(ks[1], (D, D), dtype=jnp.float32) * s, 'bq': jnp.zeros((D,), jnp.float32), 'Wk': jax.random.normal(ks[2], (D, D), dtype=jnp.float32) * s, 'bk': jnp.zeros((D,), jnp.float32), 'Wv': jax.random.normal(ks[3], (D, D), dtype=jnp.float32) * s, 'bv': jnp.zeros((D,), jnp.float32), 'Wo': jax.random.normal(ks[4], (D, D), dtype=jnp.float32) * s, 'bo': jnp.zeros((D,), jnp.float32), 'gamma': jnp.ones((D,), jnp.float32), 'beta': jnp.zeros((D,), jnp.float32), 'W1': jax.random.normal(ks[5], (D, F), dtype=jnp.float32) * s, 'b1': jnp.zeros((F,), jnp.float32), 'W2': jax.random.normal(ks[6], (F, D), dtype=jnp.float32) * s, 'b2': jnp.zeros((D,), jnp.float32)}
    _L0_attn_in = _L0_attn_setup()

    def _L0_ffn_setup():
        import jax, jax.numpy as jnp
        import numpy as np
        SL, BS, HS, FF, E, TOPK = (512, 2, 256, 1024, 8, 2)
        key = jax.random.key(seed)
        ks = jax.random.split(key, 6)
        T = SL * BS
        x = jax.random.normal(ks[0], (SL, BS, HS), jnp.float32)
        scores = jax.random.uniform(ks[1], (T, E), jnp.float32)
        expert_weights = jax.random.uniform(ks[2], (T, TOPK), jnp.float32)
        expert_indices = jax.random.randint(ks[3], (T, TOPK), 0, E, jnp.int32)
        w1 = jax.random.normal(ks[4], (E, HS, FF), jnp.float32) * (1.0 / np.sqrt(HS))
        w2 = jax.random.normal(ks[5], (E, FF, HS), jnp.float32) * (1.0 / np.sqrt(FF))
        bias = jnp.zeros((HS,), jnp.float32)
        return dict(x=x, scores=scores, expert_weights=expert_weights, expert_indices=expert_indices, w1=w1, w2=w2, bias=bias)
    _L0_ffn_in = _L0_ffn_setup()
    _L0_c = _w((lambda *s: np.random.randn(*s).astype(np.float32) * 0.05)(16, 256))
    _L0_wmod = _w((lambda *s: np.random.randn(*s).astype(np.float32) * 0.05)(256, 6 * 256) * 256 ** (-0.5))

    def _L1_attn_setup():
        import jax, jax.numpy as jnp
        import numpy as np
        NUM_HEADS = 16
        EPS = 1e-06

        def _split_heads(t, h):
            b, s, d = t.shape
            return t.reshape(b, s, h, d // h).transpose(0, 2, 1, 3)
        key = jax.random.key(seed)
        ks = jax.random.split(key, 6)
        b, s, d = (4, 1024, 256)
        scale = 1.0 / np.sqrt(d)
        return {'x': jax.random.normal(ks[0], (b, s, d), dtype=jnp.float32), 'wq': jax.random.normal(ks[1], (d, d), dtype=jnp.float32) * scale, 'wk': jax.random.normal(ks[2], (d, d), dtype=jnp.float32) * scale, 'wv': jax.random.normal(ks[3], (d, d), dtype=jnp.float32) * scale, 'wo': jax.random.normal(ks[4], (d, d), dtype=jnp.float32) * scale, 'bo': jnp.zeros((d,), dtype=jnp.float32)}
    _L1_attn_in = _L1_attn_setup()

    def _L1_ffn_setup():
        import jax, jax.numpy as jnp
        import numpy as np
        D_MODEL = 256
        N_HEADS = 16
        N_KV = 4
        NUM_REP = N_HEADS // N_KV
        HEAD_DIM = D_MODEL // N_HEADS
        N_EXPERTS = 8
        TOP_K = 2
        CAP_FACTOR = 1.25
        EPS_NORM = 1e-06

        def _rmsnorm(x, w):
            var = jnp.mean(x * x, axis=-1, keepdims=True)
            return w * (x * jax.lax.rsqrt(var + EPS_NORM))

        def _gqa(x, qw, qb, kw, kb, vw, vb, ow, ob):
            B, S, D = x.shape
            q = (x @ qw + qb).reshape(B, S, N_HEADS, HEAD_DIM).transpose(0, 2, 1, 3)
            k = (x @ kw + kb).reshape(B, S, N_KV, HEAD_DIM).transpose(0, 2, 1, 3)
            v = (x @ vw + vb).reshape(B, S, N_KV, HEAD_DIM).transpose(0, 2, 1, 3)
            k = jnp.repeat(k, NUM_REP, axis=1)
            v = jnp.repeat(v, NUM_REP, axis=1)
            scores = jnp.einsum('bhqd,bhkd->bhqk', q, k) / np.sqrt(HEAD_DIM).astype(np.float32)
            attn = jax.nn.softmax(scores, axis=-1)
            out = jnp.einsum('bhqk,bhkd->bhqd', attn, v)
            out = out.transpose(0, 2, 1, 3).reshape(B, S, D)
            return out @ ow + ob

        def _moe(x, gate_w, w1, w2):
            B, S, D = x.shape
            T = B * S
            x_flat = x.reshape(T, D)
            capacity = int(CAP_FACTOR * T * TOP_K / N_EXPERTS)
            logits = x_flat @ gate_w
            probs = jax.nn.sigmoid(logits)
            _, sel = jax.lax.top_k(probs, TOP_K)
            w_topk = jnp.take_along_axis(probs, sel, axis=1)
            w_topk = w_topk / (jnp.sum(w_topk, axis=-1, keepdims=True) + 1e-06)
            flat_sel = sel.reshape(-1)
            em = jax.nn.one_hot(flat_sel, N_EXPERTS, dtype=jnp.int32)
            ranks = jnp.take_along_axis(jnp.cumsum(em, axis=0), flat_sel[:, None], axis=1)[:, 0] - 1
            valid = ranks < capacity
            slot = flat_sel * capacity + ranks
            scatter_idx = jnp.where(valid, slot, N_EXPERTS * capacity)
            x_rep = jnp.repeat(x_flat, TOP_K, axis=0)
            padded = jnp.zeros((N_EXPERTS * capacity + 1, D), x.dtype).at[scatter_idx].set(x_rep)
            padded_x = padded[:N_EXPERTS * capacity].reshape(N_EXPERTS, capacity, D)
            h = jax.nn.gelu(jnp.einsum('ecd,edf->ecf', padded_x, w1), approximate=False)
            out_padded = jnp.einsum('ecf,efd->ecd', h, w2).reshape(N_EXPERTS * capacity, D)
            gather_idx = jnp.where(valid, slot, 0)
            out_rep = jnp.where(valid[:, None], out_padded[gather_idx], 0.0)
            out_w = out_rep * w_topk.reshape(-1)[:, None]
            return out_w.reshape(T, TOP_K, D).sum(axis=1).reshape(B, S, D)
        key = jax.random.key(seed)
        ks = jax.random.split(key, 12)
        s = 0.02
        return {'x': jax.random.normal(ks[0], (4, 256, D_MODEL), jnp.float32), 'qw': jax.random.normal(ks[1], (D_MODEL, D_MODEL), jnp.float32) * s, 'qb': jnp.zeros((D_MODEL,), jnp.float32), 'kw': jax.random.normal(ks[2], (D_MODEL, N_KV * HEAD_DIM), jnp.float32) * s, 'kb': jnp.zeros((N_KV * HEAD_DIM,), jnp.float32), 'vw': jax.random.normal(ks[3], (D_MODEL, N_KV * HEAD_DIM), jnp.float32) * s, 'vb': jnp.zeros((N_KV * HEAD_DIM,), jnp.float32), 'ow': jax.random.normal(ks[4], (D_MODEL, D_MODEL), jnp.float32) * s, 'ob': jnp.zeros((D_MODEL,), jnp.float32), 'gate_w': jax.random.normal(ks[5], (D_MODEL, N_EXPERTS), jnp.float32) * s, 'w1': jax.random.normal(ks[6], (N_EXPERTS, D_MODEL, 512), jnp.float32) * s, 'w2': jax.random.normal(ks[7], (N_EXPERTS, 512, D_MODEL), jnp.float32) * s, 'norm1_w': jnp.ones((D_MODEL,), jnp.float32), 'norm2_w': jnp.ones((D_MODEL,), jnp.float32)}
    _L1_ffn_in = _L1_ffn_setup()
    _L1_c = _w((lambda *s: np.random.randn(*s).astype(np.float32) * 0.05)(16, 256))
    _L1_wmod = _w((lambda *s: np.random.randn(*s).astype(np.float32) * 0.05)(256, 6 * 256) * 256 ** (-0.5))
    _d = {'L0_attn_x': _L0_attn_in['x'], 'L0_attn_Wq': _L0_attn_in['Wq'], 'L0_attn_bq': _L0_attn_in['bq'], 'L0_attn_Wk': _L0_attn_in['Wk'], 'L0_attn_bk': _L0_attn_in['bk'], 'L0_attn_Wv': _L0_attn_in['Wv'], 'L0_attn_bv': _L0_attn_in['bv'], 'L0_attn_Wo': _L0_attn_in['Wo'], 'L0_attn_bo': _L0_attn_in['bo'], 'L0_attn_gamma': _L0_attn_in['gamma'], 'L0_attn_beta': _L0_attn_in['beta'], 'L0_attn_W1': _L0_attn_in['W1'], 'L0_attn_b1': _L0_attn_in['b1'], 'L0_attn_W2': _L0_attn_in['W2'], 'L0_attn_b2': _L0_attn_in['b2'], 'L0_ffn_scores': _L0_ffn_in['scores'], 'L0_ffn_expert_weights': _L0_ffn_in['expert_weights'], 'L0_ffn_expert_indices': _L0_ffn_in['expert_indices'], 'L0_ffn_w1': _L0_ffn_in['w1'], 'L0_ffn_w2': _L0_ffn_in['w2'], 'L0_ffn_bias': _L0_ffn_in['bias'], 'L0_c': _L0_c, 'L0_wmod': _L0_wmod, 'L1_attn_wq': _L1_attn_in['wq'], 'L1_attn_wk': _L1_attn_in['wk'], 'L1_attn_wv': _L1_attn_in['wv'], 'L1_attn_wo': _L1_attn_in['wo'], 'L1_attn_bo': _L1_attn_in['bo'], 'L1_ffn_qw': _L1_ffn_in['qw'], 'L1_ffn_qb': _L1_ffn_in['qb'], 'L1_ffn_kw': _L1_ffn_in['kw'], 'L1_ffn_kb': _L1_ffn_in['kb'], 'L1_ffn_vw': _L1_ffn_in['vw'], 'L1_ffn_vb': _L1_ffn_in['vb'], 'L1_ffn_ow': _L1_ffn_in['ow'], 'L1_ffn_ob': _L1_ffn_in['ob'], 'L1_ffn_gate_w': _L1_ffn_in['gate_w'], 'L1_ffn_w1': _L1_ffn_in['w1'], 'L1_ffn_w2': _L1_ffn_in['w2'], 'L1_ffn_norm1_w': _L1_ffn_in['norm1_w'], 'L1_ffn_norm2_w': _L1_ffn_in['norm2_w'], 'L1_c': _L1_c, 'L1_wmod': _L1_wmod}
    _x0 = _d['L0_attn_x']
    _d['L0_attn_x'] = jax.random.normal(jax.random.fold_in(jax.random.key(seed), 1), (16, 512, 256), dtype=_x0.dtype)
    del _x0
    return _d

def reference(L0_attn_x, L0_attn_Wq, L0_attn_bq, L0_attn_Wk, L0_attn_bk, L0_attn_Wv, L0_attn_bv, L0_attn_Wo, L0_attn_bo, L0_attn_gamma, L0_attn_beta, L0_attn_W1, L0_attn_b1, L0_attn_W2, L0_attn_b2, L0_ffn_scores, L0_ffn_expert_weights, L0_ffn_expert_indices, L0_ffn_w1, L0_ffn_w2, L0_ffn_bias, L0_c, L0_wmod, L1_attn_wq, L1_attn_wk, L1_attn_wv, L1_attn_wo, L1_attn_bo, L1_ffn_qw, L1_ffn_qb, L1_ffn_kw, L1_ffn_kb, L1_ffn_vw, L1_ffn_vb, L1_ffn_ow, L1_ffn_ob, L1_ffn_gate_w, L1_ffn_w1, L1_ffn_w2, L1_ffn_norm1_w, L1_ffn_norm2_w, L1_c, L1_wmod):

    def _L0_attn_ref(x, Wq, bq, Wk, bk, Wv, bv, Wo, bo, gamma, beta, W1, b1, W2, b2):
        import jax, jax.numpy as jnp
        import numpy as np
        H_HEADS = 8
        WIN = 64

        def _layernorm(x, gamma, beta, eps=1e-05):
            mu = jnp.mean(x, axis=-1, keepdims=True)
            var = jnp.var(x, axis=-1, keepdims=True)
            return (x - mu) * jax.lax.rsqrt(var + eps) * gamma + beta
        B, S, D = x.shape
        w, H = (WIN, H_HEADS)
        dh = D // H
        pad = -S % w
        if pad:
            x = jnp.pad(x, ((0, 0), (0, pad), (0, 0)))
        mask = jnp.concatenate([jnp.ones((B, S), jnp.float32), jnp.zeros((B, pad), jnp.float32)], axis=1)
        Sp = S + pad
        nc = Sp // w

        def proj(W, b):
            return (x @ W + b).reshape(B, Sp, H, dh).transpose(0, 2, 1, 3).reshape(B, H, nc, w, dh)
        q = proj(Wq, bq)
        k = proj(Wk, bk)
        v = proj(Wv, bv)

        def ext3(t):
            tp = jnp.pad(t, ((0, 0), (0, 0), (1, 1), (0, 0), (0, 0)))
            return jnp.concatenate([tp[:, :, :-2], tp[:, :, 1:-1], tp[:, :, 2:]], axis=3)
        k3 = ext3(k)
        v3 = ext3(v)
        mc = mask.reshape(B, nc, w)
        mp = jnp.pad(mc, ((0, 0), (1, 1), (0, 0)))
        m3 = jnp.concatenate([mp[:, :-2], mp[:, 1:-1], mp[:, 2:]], axis=2)
        qi = jnp.arange(w)
        kj = jnp.arange(3 * w)
        band = jnp.abs(qi[:, None] - (kj[None, :] - w)) <= w
        allow = band[None, None, None, :, :] & (m3[:, None, :, None, :] > 0)
        scale = float(dh) ** (-0.5)
        scores = jnp.einsum('bhcqd,bhckd->bhcqk', q, k3) * scale
        scores = jnp.where(allow, scores, jnp.float32(-1e+30))
        p = jax.nn.softmax(scores, axis=-1)
        o = jnp.einsum('bhcqk,bhckd->bhcqd', p, v3)
        o = o.reshape(B, H, Sp, dh).transpose(0, 2, 1, 3).reshape(B, Sp, D)
        attn = o @ Wo + bo
        x = x + attn
        x = _layernorm(x, gamma, beta)
        h = jax.nn.gelu(x @ W1 + b1, approximate=False)
        x = x + (h @ W2 + b2)
        return x

    def _L0_ffn_ref(x, scores, expert_weights, expert_indices, w1, w2, bias):
        import jax, jax.numpy as jnp
        import numpy as np
        SL, BS, HS, FF, E, TOPK = (512, 2, 256, 1024, 8, 2)
        sl, bs, hs = x.shape
        n_exp = w1.shape[0]
        top_k = expert_indices.shape[-1]
        xf = x.reshape(-1, hs)
        flat_idx = expert_indices.reshape(-1)
        flat_w = expert_weights.reshape(-1)
        order = jnp.argsort(flat_idx)
        tok = order // top_k
        tokens_per_expert = jnp.bincount(flat_idx, length=n_exp).astype(jnp.int32)
        xs = xf[tok]
        h = jax.nn.gelu(jax.lax.ragged_dot(xs, w1, tokens_per_expert), approximate=False)
        ys = jax.lax.ragged_dot(h, w2, tokens_per_expert)
        ys = ys * flat_w[order][:, None]
        out = jnp.zeros_like(xf).at[tok].add(ys)
        return out.reshape(sl, bs, hs) + bias

    def _L1_attn_ref(x, wq, wk, wv, wo, bo):
        import jax, jax.numpy as jnp
        import numpy as np
        NUM_HEADS = 16
        EPS = 1e-06

        def _split_heads(t, h):
            b, s, d = t.shape
            return t.reshape(b, s, h, d // h).transpose(0, 2, 1, 3)
        h = NUM_HEADS
        q = _split_heads(x @ wq.T, h)
        k = _split_heads(x @ wk.T, h)
        v = _split_heads(x @ wv.T, h)
        qf = jax.nn.elu(q) + 1.0
        kf = jax.nn.elu(k) + 1.0
        k_sum = jnp.sum(kf, axis=-2)
        denom = jnp.sum(qf * k_sum[:, :, None, :], axis=-1, keepdims=True) + EPS
        kv = jnp.einsum('bhsd,bhse->bhde', kf, v)
        q_kv = jnp.einsum('bhsd,bhde->bhse', qf, kv)
        out = q_kv / denom
        b, _, s, dh = out.shape
        out = out.transpose(0, 2, 1, 3).reshape(b, s, h * dh)
        return out @ wo.T + bo

    def _L1_ffn_ref(x, qw, qb, kw, kb, vw, vb, ow, ob, gate_w, w1, w2, norm1_w, norm2_w):
        import jax, jax.numpy as jnp
        import numpy as np
        D_MODEL = 256
        N_HEADS = 16
        N_KV = 4
        NUM_REP = N_HEADS // N_KV
        HEAD_DIM = D_MODEL // N_HEADS
        N_EXPERTS = 8
        TOP_K = 2
        CAP_FACTOR = 1.25
        EPS_NORM = 1e-06

        def _rmsnorm(x, w):
            var = jnp.mean(x * x, axis=-1, keepdims=True)
            return w * (x * jax.lax.rsqrt(var + EPS_NORM))

        def _gqa(x, qw, qb, kw, kb, vw, vb, ow, ob):
            B, S, D = x.shape
            q = (x @ qw + qb).reshape(B, S, N_HEADS, HEAD_DIM).transpose(0, 2, 1, 3)
            k = (x @ kw + kb).reshape(B, S, N_KV, HEAD_DIM).transpose(0, 2, 1, 3)
            v = (x @ vw + vb).reshape(B, S, N_KV, HEAD_DIM).transpose(0, 2, 1, 3)
            k = jnp.repeat(k, NUM_REP, axis=1)
            v = jnp.repeat(v, NUM_REP, axis=1)
            scores = jnp.einsum('bhqd,bhkd->bhqk', q, k) / np.sqrt(HEAD_DIM).astype(np.float32)
            attn = jax.nn.softmax(scores, axis=-1)
            out = jnp.einsum('bhqk,bhkd->bhqd', attn, v)
            out = out.transpose(0, 2, 1, 3).reshape(B, S, D)
            return out @ ow + ob

        def _moe(x, gate_w, w1, w2):
            B, S, D = x.shape
            T = B * S
            x_flat = x.reshape(T, D)
            capacity = int(CAP_FACTOR * T * TOP_K / N_EXPERTS)
            logits = x_flat @ gate_w
            probs = jax.nn.sigmoid(logits)
            _, sel = jax.lax.top_k(probs, TOP_K)
            w_topk = jnp.take_along_axis(probs, sel, axis=1)
            w_topk = w_topk / (jnp.sum(w_topk, axis=-1, keepdims=True) + 1e-06)
            flat_sel = sel.reshape(-1)
            em = jax.nn.one_hot(flat_sel, N_EXPERTS, dtype=jnp.int32)
            ranks = jnp.take_along_axis(jnp.cumsum(em, axis=0), flat_sel[:, None], axis=1)[:, 0] - 1
            valid = ranks < capacity
            slot = flat_sel * capacity + ranks
            scatter_idx = jnp.where(valid, slot, N_EXPERTS * capacity)
            x_rep = jnp.repeat(x_flat, TOP_K, axis=0)
            padded = jnp.zeros((N_EXPERTS * capacity + 1, D), x.dtype).at[scatter_idx].set(x_rep)
            padded_x = padded[:N_EXPERTS * capacity].reshape(N_EXPERTS, capacity, D)
            h = jax.nn.gelu(jnp.einsum('ecd,edf->ecf', padded_x, w1), approximate=False)
            out_padded = jnp.einsum('ecf,efd->ecd', h, w2).reshape(N_EXPERTS * capacity, D)
            gather_idx = jnp.where(valid, slot, 0)
            out_rep = jnp.where(valid[:, None], out_padded[gather_idx], 0.0)
            out_w = out_rep * w_topk.reshape(-1)[:, None]
            return out_w.reshape(T, TOP_K, D).sum(axis=1).reshape(B, S, D)
        src = x + _gqa(x, qw, qb, kw, kb, vw, vb, ow, ob)
        src = _rmsnorm(src, norm1_w)
        src = src + _moe(src, gate_w, w1, w2)
        return _rmsnorm(src, norm2_w)
    x = L0_attn_x
    mod = (_silu(L0_c) @ L0_wmod).reshape(L0_c.shape[0], 6, 1, -1)
    sa, ca, ga, sb, cb, gb = (mod[:, 0], mod[:, 1], mod[:, 2], mod[:, 3], mod[:, 4], mod[:, 5])
    ga = (2 * (ga >= 0) - 1) * jnp.maximum(jnp.abs(ga), 0.25)
    gb = (2 * (gb >= 0) - 1) * jnp.maximum(jnp.abs(gb), 0.25)
    h = _layernorm(x, axis=-1) * (1 + ca) + sa
    x = x + ga * _L0_attn_ref(h, L0_attn_Wq, L0_attn_bq, L0_attn_Wk, L0_attn_bk, L0_attn_Wv, L0_attn_bv, L0_attn_Wo, L0_attn_bo, L0_attn_gamma, L0_attn_beta, L0_attn_W1, L0_attn_b1, L0_attn_W2, L0_attn_b2)
    h = _layernorm(x, axis=-1) * (1 + cb) + sb
    x = x + gb * _L0_ffn_ref(h, L0_ffn_scores, L0_ffn_expert_weights, L0_ffn_expert_indices, L0_ffn_w1, L0_ffn_w2, L0_ffn_bias)
    mod = (_silu(L1_c) @ L1_wmod).reshape(L1_c.shape[0], 6, 1, -1)
    sa, ca, ga, sb, cb, gb = (mod[:, 0], mod[:, 1], mod[:, 2], mod[:, 3], mod[:, 4], mod[:, 5])
    ga = (2 * (ga >= 0) - 1) * jnp.maximum(jnp.abs(ga), 0.25)
    gb = (2 * (gb >= 0) - 1) * jnp.maximum(jnp.abs(gb), 0.25)
    h = _layernorm(x, axis=-1) * (1 + ca) + sa
    x = x + ga * _L1_attn_ref(h, L1_attn_wq, L1_attn_wk, L1_attn_wv, L1_attn_wo, L1_attn_bo)
    h = _layernorm(x, axis=-1) * (1 + cb) + sb
    x = x + gb * _L1_ffn_ref(h, L1_ffn_qw, L1_ffn_qb, L1_ffn_kw, L1_ffn_kb, L1_ffn_vw, L1_ffn_vb, L1_ffn_ow, L1_ffn_ob, L1_ffn_gate_w, L1_ffn_w1, L1_ffn_w2, L1_ffn_norm1_w, L1_ffn_norm2_w)
    return x

_drawn_inputs = setup_inputs


def setup_inputs(seed=0):
    import zlib

    import numpy as np

    out = dict(_drawn_inputs(seed))
    spreads = {'L0_attn_bq': (0.0, 0.8),
     'L0_attn_bk': (0.0, 0.8),
     'L0_attn_bv': (0.0, 0.8),
     'L0_attn_bo': (0.0, 0.32),
     'L0_attn_gamma': (1.0, 0.2),
     'L0_attn_beta': (0.0, 0.352),
     'L0_attn_b1': (0.0, 0.8),
     'L0_attn_b2': (0.0, 0.297),
     'L0_ffn_bias': (0.0, 0.305),
     'L1_attn_bo': (0.0, 0.341),
     'L1_ffn_qb': (0.0, 0.8),
     'L1_ffn_kb': (0.0, 0.8),
     'L1_ffn_vb': (0.0, 0.8),
     'L1_ffn_ob': (0.0, 0.374),
     'L1_ffn_norm1_w': (1.0, 0.2),
     'L1_ffn_norm2_w': (1.0, 0.2)}
    factors = {'L0_attn_Wq': 8.0,
     'L0_attn_Wk': 8.0,
     'L0_attn_Wv': 8.0,
     'L0_attn_Wo': 6.506,
     'L1_attn_wq': 8.0,
     'L1_attn_wk': 8.0,
     'L1_attn_wv': 3.379,
     'L1_attn_wo': 3.404,
     'L1_ffn_qw': 8.0,
     'L1_ffn_kw': 8.0,
     'L1_ffn_vw': 8.0,
     'L1_ffn_ow': 6.72,
     'L1_ffn_gate_w': 4.754,
     'L1_ffn_w1': 4.307,
     'L1_ffn_w2': 4.196}
    for name, (base, spread) in spreads.items():
        noise = np.random.default_rng([zlib.crc32(name.encode()), seed]).standard_normal(out[name].shape)
        drawn = base * np.exp(spread * noise) if base else spread * noise
        out[name] = jnp.asarray(drawn.astype(out[name].dtype))
    for name, factor in factors.items():
        out[name] = (out[name] * factor).astype(out[name].dtype)
    return out
```

```python
from contextlib import ExitStack

import concourse.bass as bass
from concourse import mybir

F32 = mybir.dt.float32
BF16 = mybir.dt.bfloat16
I32 = mybir.dt.int32
U32 = mybir.dt.uint32
ACT = mybir.ActivationFunctionType
ALU = mybir.AluOpType
AX = mybir.AxisListType

P = 128
D = 256
C = D // P
B = 16
S = 512
NT = S // P
T = B * S
PAD = 64
SP_ = S + 2 * PAD
LN_EPS = 1e-5
NEG = -1e30

H0, DH0 = 8, 32
SCALE0 = float(DH0) ** -0.5
F0 = 1024
NF0 = F0 // P
E = 8
TOPK = 2
H1, DH1 = 16, 16
HPC1 = P // DH1
EPS_DEN = 1e-6
HQ, HKV, DHQ = 16, 4, 16
REP = HQ // HKV
EPS_NORM = 1e-6
F1 = 512
NF1 = F1 // P
CAP = int(1.25 * T * TOPK / E)
CT = CAP // S
ROWS_MOE0 = 1024
RSQRT_MAGIC = float(0x5F3759DF)


class Steps:

    def __init__(self, eng, sem, base, per):
        self.eng, self.sem, self.base, self.per, self.n = eng, sem, base, per, 0

    def __call__(self, ins):
        ins.then_inc(self.sem, 1)
        self.n += 1

    def settle(self):
        self.eng.wait_ge(self.sem, self.base + self.n)

    def close(self):
        assert self.n == self.per, (self.n, self.per)


def bank(m, i):
    return m.psum[:, i, :]


def tile_maker(nc, ctx):

    def sb(name, shape, dtype=F32):
        return ctx.enter_context(nc.sbuf_tensor(name, shape, dtype))

    return sb


def allocate(nc, ctx):

    class Memory:
        pass

    m = Memory()

    sb = tile_maker(nc, ctx)
    m.waits_taken = ctx.enter_context(nc.semaphore("waits_taken"))
    m.psum = ctx.enter_context(nc.psum_tensor("psum", [P, 8, 512], F32))
    m.x = sb("x", [P, T // P * D])
    m.ident = sb("ident", [P, P])
    m.ident_bf = sb("ident_bf", [P, P], BF16)
    m.band_mask = sb("band_mask", [P, 3, 2, D], BF16)
    m.ones_col = sb("ones_col", [P, 1])
    m.mod_cols0 = sb("mod_cols0", [P, 4, C, B])
    m.mod_cols1 = sb("mod_cols1", [P, 4, C, B])
    m.gate_rows = sb("gate_rows", [P, 4, D])
    m.gather_idx = sb("gather_idx", [P, T // P * TOPK], U32)
    m.gather_wt = sb("gather_wt", [P, T // P * TOPK])
    m.bn = sb("bn", [P, NT, 6])
    m.meanvar = sb("meanvar", [P, NT, 2])
    m.var_eps = sb("var_eps", [P, NT])
    m.newton = sb("newton", [P, NT])
    m.rstd = sb("rstd", [P, NT])
    m.xn = sb("xn", [P, NT, D])
    return m


def take_wait(eng, m):
    eng.sem_inc(m.waits_taken, 1)


def emit_rsqrt(dve, step, m, out, var, eps):
    a, h = m.var_eps[:, :], m.newton[:, :]
    step(dve.tensor_scalar(a, var, eps, None, ALU.add))
    step.settle()
    step(dve.tensor_scalar(out.bitcast(I32), a.bitcast(I32), -0.5, RSQRT_MAGIC, ALU.mult, ALU.add))
    step.settle()
    for _ in range(3):
        step(dve.scalar_tensor_tensor(out=h, in0=out, scalar=-0.5, in1=out, op0=ALU.mult, op1=ALU.mult))
        step.settle()
        step(dve.tensor_tensor(h, h, a, ALU.mult))
        step.settle()
        step(dve.scalar_tensor_tensor(out=out, in0=h, scalar=1.5, in1=out, op0=ALU.add, op1=ALU.mult))
        step.settle()


def emit_layernorm(dve, step, m, tiles, ready, tile_wait=None, free_wait=None):
    for t in range(NT):
        if tile_wait:
            tile_wait(t)
        step(dve.bn_stats(m.bn[:, t, :], tiles[t]))
    step.settle()
    take_wait(dve, m)
    for t in range(NT):
        step(dve.bn_aggr(m.meanvar[:, t, :], m.bn[:, t, :]))
    step.settle()
    emit_rsqrt(dve, step, m, m.rstd[:, :], m.meanvar[:, :, 1], LN_EPS)
    if free_wait:
        free_wait()
    for t in range(NT):
        dve.tensor_scalar(m.xn[:, t, :], tiles[t], m.meanvar[:, t, 0:1], m.rstd[:, t:t + 1],
                          ALU.subtract, ALU.mult).then_inc(ready, 1)


LN_STEPS = 2 * NT + 11


def emit_rms_scale(dve, step, m, tiles, eps, tile_wait=None):
    for t in range(NT):
        if tile_wait:
            tile_wait(t)
        step(dve.bn_stats(m.bn[:, t, :], tiles[t]))
    step.settle()
    take_wait(dve, m)
    for t in range(NT):
        step(dve.bn_aggr(m.meanvar[:, t, :], m.bn[:, t, :]))
    step.settle()
    step(dve.tensor_tensor(m.meanvar[:, :, 0], m.meanvar[:, :, 0], m.meanvar[:, :, 0], ALU.mult))
    step.settle()
    step(dve.tensor_tensor(m.meanvar[:, :, 1], m.meanvar[:, :, 1], m.meanvar[:, :, 0], ALU.add))
    step.settle()
    emit_rsqrt(dve, step, m, m.rstd[:, :], m.meanvar[:, :, 1], eps)


RMS_STEPS = LN_STEPS + 2


def emit_transpose_tiles(pe, m, src, banks, wait, done):
    for t in range(NT):
        wait(t)
        for c in range(C):
            mm = pe.transpose(bank(m, banks[c])[:, t * P:(t + 1) * P], src[:, t, c * P:(c + 1) * P], m.ident[:, :])
    mm.then_inc(done, 1)


def setup_block(nc, m, I, mods_dram):
    ctx = ExitStack()
    with nc.cleanup_on_exit(), ctx:
        def sb(name, shape, dtype=F32):
            return ctx.enter_context(nc.sbuf_tensor(name, shape, dtype))

        def sem(name):
            return nc.alloc_semaphore(name=name)

        cond = sb("cond", [B, 2, D])
        wmod = sb("wmod", [P, 2, C, 6 * D])
        expc = sb("expc", [B, 2, D])
        silu = sb("silu", [B, 2, D])
        condT = sb("condT", [P, 2, C, B])
        mod = sb("mod", [B, 2, 6, D])
        sign = sb("sign", [B, 2, 2, D])
        rows = sb("rows", [B, 2, 4, D])
        bias_rows = sb("bias_rows", [B, 3, D])
        cond_in = sem("cond_in")
        wmod_in = [sem("wmod_in0"), sem("wmod_in1")]
        zeroed = sem("zeroed")
        constants = sem("constants")
        exp_done = sem("exp_done")
        step_s = sem("setup_steps")
        silu_ready = sem("silu_ready")
        condT_done = sem("condT_done")
        condT_ready = sem("condT_ready")
        mod_done = sem("mod_done")
        mod_ready = sem("mod_ready")
        rows_ready = sem("rows_ready")
        cols_done = sem("cols_done")
        rows_out = sem("rows_out")
        NBLK = 6 * D // 512
        block = ctx.enter_context(nc.Block())

        @block.sync
        def _(sp):
            for layer in (0, 1):
                sp.dma_start(cond[:, layer, :], I[f"L{layer}_c"]).then_inc(cond_in, 16)
            for i, n in enumerate(("L0_attn_b2", "L0_ffn_bias", "L1_attn_bo")):
                sp.dma_start(bias_rows[:, i, :], I[n].partition_broadcast(B)).then_inc(cond_in, 16)
            for layer in (0, 1):
                sp.wait_ge(rows_ready, 2 * (layer + 1))
                sp.dma_start(mods_dram[layer], rows[:, layer, :, :]).then_inc(rows_out, 16)
            sp.wait_ge(rows_out, 32)

        @block.gpsimd
        def _(pool):
            pool.memset(m.ident[:, :], 0.0).then_inc(zeroed, 1)
            pool.memset(m.ident_bf[:, :], 0.0).then_inc(zeroed, 1)
            pool.memset(m.band_mask[:, :, :, :], 0.0).then_inc(zeroed, 1)
            pool.memset(m.ones_col[:, :], 1.0).then_inc(constants, 1)
            pool.wait_ge(zeroed, 3)
            for eye in (m.ident, m.ident_bf):
                pool.affine_select(out=eye[:, :], in_=eye[:, :], compare_op=ALU.not_equal, fill=1.0, base=0,
                                   pattern=[[-1, P]], channel_multiplier=1).then_inc(constants, 1)
            w = m.band_mask[:, :, :, :].rearrange("p v r j -> p (v r) j")
            pool.affine_select(out=w, in_=w, compare_op=ALU.is_ge, fill=NEG, base=0, pattern=[[0, 6], [1, D]],
                               channel_multiplier=-1).then_inc(zeroed, 1)
            pool.wait_ge(zeroed, 4)
            pool.affine_select(out=w, in_=w, compare_op=ALU.is_ge, fill=NEG, base=2 * PAD, pattern=[[0, 6], [-1, D]],
                               channel_multiplier=1).then_inc(zeroed, 1)
            pool.wait_ge(zeroed, 5)
            pool.affine_select(out=m.band_mask[:, 0, :, :], in_=m.band_mask[:, 0, :, :], compare_op=ALU.is_ge,
                               fill=NEG, base=-PAD, pattern=[[0, 2], [1, D]], channel_multiplier=0)\
                .then_inc(constants, 1)
            pool.affine_select(out=m.band_mask[:, 2, :, :], in_=m.band_mask[:, 2, :, :], compare_op=ALU.is_ge,
                               fill=NEG, base=PAD + P - 1, pattern=[[0, 2], [-1, D]], channel_multiplier=0)\
                .then_inc(constants, 1)

        @block.scalar
        def _(act):
            for layer in (0, 1):
                act.dma_start(wmod[:, layer, :, :], I[f"L{layer}_wmod"].rearrange("(c p) n -> p c n", p=P))\
                    .then_inc(wmod_in[layer], 16)
            act.wait_ge(cond_in, 16 * 5)
            act.activation(expc[:, :, :], cond[:, :, :], ACT.Exp, scale=-1.0).then_inc(exp_done, 1)

        @block.vector
        def _(dve):
            step = Steps(dve, step_s, 0, 0)
            dve.wait_ge(exp_done, 1)
            step(dve.tensor_scalar(expc[:, :, :], expc[:, :, :], 1.0, None, ALU.add))
            step.settle()
            step(dve.reciprocal(expc[:, :, :], expc[:, :, :]))
            step.settle()
            dve.tensor_tensor(silu[:, :, :], cond[:, :, :], expc[:, :, :], ALU.mult).then_inc(silu_ready, 1)
            dve.wait_ge(condT_done, 1)
            dve.tensor_copy(condT[:, :, :, :].rearrange("p l c b -> p (l c b)"), bank(m, 7)[:, 0:2 * C * B])\
                .then_inc(condT_ready, 1)
            for layer in (0, 1):
                dve.wait_ge(mod_done, NBLK * (layer + 1))
                for n in range(NBLK):
                    step(dve.tensor_copy(mod[:, layer, 2 * n:2 * n + 2, :].rearrange("b s d -> b (s d)"),
                                         bank(m, NBLK * layer + n)[0:B, :]))
                step.settle()
                step(dve.tensor_scalar(mod[:, layer, 1:5:3, :], mod[:, layer, 1:5:3, :], 1.0, None, ALU.add))
                gates = mod[:, layer, 2:6:3, :]
                step(dve.tensor_scalar(sign[:, layer, :, :], gates, 0.0, None, ALU.is_ge))
                step.settle()
                step(dve.tensor_scalar(sign[:, layer, :, :], sign[:, layer, :, :], 2.0, -1.0, ALU.mult, ALU.add))
                step.settle()
                step(dve.tensor_tensor(gates, gates, sign[:, layer, :, :], ALU.mult))
                step.settle()
                step(dve.tensor_scalar(gates, gates, 0.25, None, ALU.max))
                step.settle()
                step(dve.tensor_tensor(rows[:, layer, 0:3:2, :], gates, sign[:, layer, :, :], ALU.mult))
                step.settle()
                if layer == 0:
                    dve.tensor_tensor(rows[:, 0, 1, :], rows[:, 0, 0, :], bias_rows[:, 0, :], ALU.mult)\
                        .then_inc(rows_ready, 1)
                    dve.tensor_tensor(rows[:, 0, 3, :], rows[:, 0, 2, :], bias_rows[:, 1, :], ALU.mult)\
                        .then_inc(rows_ready, 1)
                else:
                    dve.tensor_tensor(rows[:, 1, 1, :], rows[:, 1, 0, :], bias_rows[:, 2, :], ALU.mult)\
                        .then_inc(rows_ready, 1)
                    dve.memset(rows[:, 1, 3, :], 0.0).then_inc(rows_ready, 1)
            for layer in (0, 1):
                dve.wait_ge(cols_done, layer + 1)
                dve.tensor_copy((m.mod_cols0, m.mod_cols1)[layer][:, :, :, :].rearrange("p s c b -> p (s c b)"),
                                bank(m, 6 + layer)[:, 0:4 * C * B]).then_inc(mod_ready, 1)

        @block.tensor
        def _(pe):
            pe.wait_ge(constants, 5)
            pe.wait_ge(silu_ready, 1)
            for layer in (0, 1):
                for c in range(C):
                    j = (layer * C + c) * B
                    mm = pe.transpose(bank(m, 7)[:, j:j + B], silu[:, layer, c * P:(c + 1) * P], m.ident[0:B, 0:B])
            mm.then_inc(condT_done, 1)
            pe.wait_ge(condT_ready, 1)
            for layer in (0, 1):
                pe.wait_ge(wmod_in[layer], 16)
                for n in range(NBLK):
                    for c in range(C):
                        mm = pe.matmul(bank(m, NBLK * layer + n)[0:B, :], condT[:, layer, c, :],
                                       wmod[:, layer, c, 512 * n:512 * (n + 1)], start=(c == 0), stop=(c == C - 1))
                    mm.then_inc(mod_done, 1)
            for layer in (0, 1):
                pe.wait_ge(rows_ready, 2 * (layer + 1))
                for i, slot in enumerate((0, 1, 3, 4)):
                    for c in range(C):
                        j = (i * C + c) * B
                        mm = pe.transpose(bank(m, 6 + layer)[:, j:j + B], mod[:, layer, slot, c * P:(c + 1) * P],
                                          m.ident[0:B, 0:B])
                mm.then_inc(cols_done, 1)


VBANKS = 3


def local_attention_block(nc, m, I, mods_dram):
    ctx = ExitStack()
    with nc.cleanup_on_exit(), ctx:
        def sem(name):
            return nc.alloc_semaphore(name=name)

        sb = tile_maker(nc, ctx)
        m.wq0, m.wk0, m.wv0, m.wo0 = (sb(n, [P, C, D]) for n in ("wq0", "wk0", "wv0", "wo0"))
        m.bq0, m.bk0, m.gamma0, m.beta0 = (sb(n, [P, C]) for n in ("bq0", "bk0", "gamma0", "beta0"))
        m.b1_0 = sb("b1_0", [P, NF0])
        m.bv0_rows = sb("bv0_rows", [P, D])
        m.bo0_rows = sb("bo0_rows", [P, D])
        w1 = sb("w1_0", [P, C, F0])
        w2 = sb("w2_0", [P, NF0, D])
        m.hT = sb("hT", [P, C, SP_])
        m.qT = sb("qT", [P, C, S])
        m.kT = sb("kT", [P, C, SP_])
        m.v_ones = sb("v_ones", [P, NT + 1, H0, DH0 + 1])
        m.negmax = sb("negmax", [P, 2, H0])
        m.bias_exp = sb("bias_exp", [P, 2, H0])
        m.probs = sb("probs", [P, 2, H0, 2 * P])
        m.probsT = sb("probsT", [P, 2, H0, 2, P])
        m.recip = sb("recip", [P, 2, H0])
        m.attn = sb("attn", [P, 2, D])
        m.attnT = sb("attnT", [P, 2, C, P])
        m.resid = sb("resid", [P, NT, D])
        m.x2T = sb("x2T", [P, C, S])
        m.actT = sb("actT", [P, NF0, S])
        m.scaled = sb("scaled", [P, NT, D])
        zeroed = sem("a_zeroed")
        x_first = sem("a_x_first")
        x_rest = sem("a_x_rest")
        w_in = sem("a_w_in")
        wmlp_in = sem("a_wmlp_in")
        rows_in = sem("a_rows_in")
        norm_s = sem("a_first_norm_steps")
        attention_s = sem("a_attention_steps")
        norm2_s = sem("a_second_norm_steps")
        xn_ready = sem("a_xn_ready")
        hT_done = sem("a_hT_done")
        hT_act = sem("a_hT_act")
        hT_dve = sem("a_hT_dve")
        q_done = sem("a_q_done")
        k_done = sem("a_k_done")
        v_done = sem("a_v_done")
        q_ready = sem("a_q_ready")
        k_ready = sem("a_k_ready")
        v_ready = sem("a_v_ready")
        s_done = sem("a_scores_done")
        max_ready = sem("a_max_ready")
        p_ready = sem("a_probs_ready")
        pT_done = sem("a_probsT_done")
        pT_act = sem("a_probsT_act")
        pT_dve = sem("a_probsT_dve")
        o_done = sem("a_attn_done")
        o_ready = sem("a_attn_ready")
        oT_done = sem("a_attnT_done")
        oT_ready = sem("a_attnT_ready")
        r_done = sem("a_resid_done")
        r_ready = sem("a_resid_ready")
        rn_ready = sem("a_resid_norm_ready")
        x2_done = sem("a_x2T_done")
        x2_act = sem("a_x2T_act")
        x2_dve = sem("a_x2T_dve")
        up_done = sem("a_up_done")
        gelu_ready = sem("a_gelu_ready")
        y_done = sem("a_y_done")
        scaled_ready = sem("a_scaled_ready")
        x_ready = sem("a_x_ready")
        bias_added = sem("a_bias_added")
        block = ctx.enter_context(nc.Block())

        def x_tile(b, t):
            return m.x[:, bass.ds(b * (NT * D) + t * D, D)]

        def load_rows(sp, b):
            sp.dma_start(m.gate_rows[:, :, :], mods_dram[0, bass.ds(b, 1), :, :].rearrange("a s d -> (a s) d")
                         .partition_broadcast(P)).then_inc(rows_in, 16)

        @block.sync
        def _(sp):
            xv = I["L0_attn_x"].rearrange("b (t p) d -> b p t d", p=P)
            xs = m.x[:, :].rearrange("p (b t d) -> p b t d", b=B, d=D)
            sp.dma_start(xs[:, 0, :, :], xv[0]).then_inc(x_first, 16)
            for tile, k in ((m.wq0, "Wq"), (m.wk0, "Wk"), (m.wv0, "Wv"), (m.wo0, "Wo")):
                sp.dma_start(tile[:, :, :], I[f"L0_attn_{k}"].rearrange("(c p) n -> p c n", p=P))\
                    .then_inc(w_in, 16)
            for tile, k in ((m.bq0, "bq"), (m.bk0, "bk"), (m.gamma0, "gamma"), (m.beta0, "beta")):
                sp.dma_start(tile[:, :], I[f"L0_attn_{k}"].rearrange("(c p) -> p c", p=P),
                             allow_slow_non_contiguous=True)\
                    .then_inc(w_in, 16)
            sp.dma_start(m.b1_0[:, :], I["L0_attn_b1"].rearrange("(c p) -> p c", p=P),
                         allow_slow_non_contiguous=True).then_inc(w_in, 16)
            sp.dma_start(m.bv0_rows[:, :], I["L0_attn_bv"].partition_broadcast(P)).then_inc(w_in, 16)
            sp.dma_start(m.bo0_rows[:, :], I["L0_attn_bo"].partition_broadcast(P)).then_inc(w_in, 16)
            sp.dma_start(w1[:, :, :], I["L0_attn_W1"].rearrange("(c p) f -> p c f", p=P)).then_inc(wmlp_in, 16)
            sp.dma_start(w2[:, :, :], I["L0_attn_W2"].rearrange("(f p) d -> p f d", p=P)).then_inc(wmlp_in, 16)
            load_rows(sp, 0)
            for b in range(1, B):
                sp.dma_start(xs[:, b, :, :], xv[b]).then_inc(x_rest, 16)
            with sp.Fori(1, B) as b:
                sp.wait_ge(scaled_ready, b * NT)
                sp.wait_ge(bias_added, b)
                load_rows(sp, b)

        @block.gpsimd
        def _(pool):
            pool.memset(m.hT[:, :, :], 0.0).then_inc(zeroed, 1)
            pool.memset(m.kT[:, :, :], 0.0).then_inc(zeroed, 1)
            pool.memset(m.v_ones[:, :, :, :], 1.0).then_inc(zeroed, 1)
            with pool.Fori(0, B) as b:
                pool.wait_ge(xn_ready, b * NT + NT)
                pool.wait_ge(rows_in, b * 16 + 16)
                take_wait(pool, m)
                xb = m.x[:, bass.ds(b * (NT * D), NT * D)].rearrange("p (t d) -> p t d", t=NT)
                pool.tensor_tensor(xb, xb, m.gate_rows[:, 1:2, :].to_broadcast([P, NT, D]), ALU.add)\
                    .then_inc(bias_added, 1)

        @block.scalar
        def _(act):
            act.wait_ge(w_in, 16 * 11)
            act.wait_ge(zeroed, 3)

            def inputs(b):
                act.wait_ge(hT_done, b + 1)
                act.activation(m.hT[:, 0, PAD:PAD + S], bank(m, 0), ACT.Identity,
                               bias=m.mod_cols0[:, 0, 0, bass.ds(b, 1)], scale=m.mod_cols0[:, 1, 0, bass.ds(b, 1)])\
                    .then_inc(hT_act, 1)
                for c in range(C):
                    act.wait_ge(q_done, b * C + c + 1)
                    act.activation(m.qT[:, c, :], bank(m, c), ACT.Identity, bias=m.bq0[:, c:c + 1])\
                        .then_inc(q_ready, 1)

            def attention(b):
                def exps(t):
                    act.wait_ge(max_ready, b * NT + t + 1)
                    if t >= 2:
                        act.wait_ge(pT_done, b * (4 * NT) + 4 * (t - 1))
                    for j in range(4):
                        for i, h in enumerate((j, j + 4)):
                            ins = act.activation(m.probs[:, t % 2, h, :],
                                                 bank(m, 4 * (t % 2) + j)[:, i * 2 * P:(i + 1) * 2 * P],
                                                 ACT.Exp, bias=m.bias_exp[:, t % 2, h:h + 1], scale=SCALE0)
                        ins.then_inc(p_ready, 1)

                def copy_probsT(t):
                    if t >= 2:
                        act.wait_ge(o_done, b * NT + t - 1)
                    for j in (0, 2):
                        act.wait_ge(pT_done, b * (4 * NT) + 4 * t + j + 1)
                        act.activation(m.probsT[:, t % 2, j:8:4, :, :],
                                       bank(m, 4 * (t % 2) + j).rearrange("p (i k q) -> p i k q", i=2, k=2),
                                       ACT.Copy).then_inc(pT_act, 1)

                def copy_attnT(t):
                    act.wait_ge(oT_done, b * NT + t + 1)
                    act.activation(m.attnT[:, t % 2, :, :].rearrange("p c q -> p (c q)"),
                                   bank(m, 4 * (t % 2) + 1)[:, 0:D], ACT.Copy).then_inc(oT_ready, 1)

                exps(0)
                copy_probsT(0)
                exps(1)
                copy_probsT(1)
                copy_attnT(0)
                copy_attnT(1)
                exps(2)
                copy_probsT(2)
                exps(3)
                copy_probsT(3)
                copy_attnT(2)
                copy_attnT(3)

            def mlp(b):
                act.wait_ge(x2_done, b + 1)
                act.activation(m.x2T[:, 0, :], bank(m, 0), ACT.Identity, bias=m.beta0[:, 0:1],
                               scale=m.gamma0[:, 0:1]).then_inc(x2_act, 1)
                for f in range(NF0):
                    act.wait_ge(up_done, b * NF0 + f + 1)
                    act.activation(m.actT[:, f, :], bank(m, 2 + f % 6), ACT.Gelu, bias=m.b1_0[:, f:f + 1])\
                        .then_inc(gelu_ready, 1)

            inputs(0)
            with act.Fori(0, B - 1) as b:
                attention(b)
                inputs(b + 1)
                mlp(b)
            attention(B - 1)
            mlp(B - 1)

        @block.vector
        def _(dve):
            dve.wait_ge(w_in, 16 * 11)
            dve.wait_ge(zeroed, 3)
            dve.wait_ge(x_first, 16)

            def first_norm(b):
                step = Steps(dve, norm_s, b * LN_STEPS, LN_STEPS)
                emit_layernorm(dve, step, m, [x_tile(b, t) for t in range(NT)], xn_ready)
                step.close()

            def modulate(b):
                dve.wait_ge(hT_done, b + 1)
                dve.tensor_scalar(m.hT[:, 1, PAD:PAD + S], bank(m, 1), m.mod_cols0[:, 1, 1, bass.ds(b, 1)],
                                  m.mod_cols0[:, 0, 1, bass.ds(b, 1)], ALU.mult, ALU.add).then_inc(hT_dve, 1)

            def inputs(b):
                for c in range(C):
                    dve.wait_ge(k_done, b * C + c + 1)
                    dve.tensor_scalar(m.kT[:, c, PAD:PAD + S], bank(m, 2 + c), m.bk0[:, c:c + 1], None, ALU.add)\
                        .then_inc(k_ready, 1)
                for i in range(VBANKS):
                    n = min(2, NT + 1 - 2 * i)
                    dve.wait_ge(v_done, b * VBANKS + i + 1)
                    dve.tensor_tensor(m.v_ones[:, 2 * i:2 * i + n, :, 0:DH0],
                                      bank(m, 4 + i)[:, 0:n * D].rearrange("p (j h d) -> p j h d", j=n, h=H0),
                                      m.bv0_rows[:, :].rearrange("p (j h d) -> p j h d", j=1, h=H0)
                                      .to_broadcast([P, n, H0, DH0]), ALU.add).then_inc(v_ready, 1)

            def attention(b):
                step = Steps(dve, attention_s, b * (2 * NT), 2 * NT)

                def row_max(t):
                    dve.wait_ge(s_done, b * NT + t + 1)
                    if t >= 2:
                        dve.wait_ge(p_ready, b * (4 * NT) + 4 * (t - 1))
                    step(dve.tensor_reduce(m.negmax[:, t % 2, :].rearrange("p (i j) -> p j i", i=2),
                                           m.psum[:, 4 * (t % 2):4 * (t % 2) + 4, :]
                                           .rearrange("p j (i k) -> p j i k", i=2), AX.X, ALU.max, negate=True))
                    step.settle()
                    dve.tensor_scalar(m.bias_exp[:, t % 2, :], m.negmax[:, t % 2, :], SCALE0, None, ALU.mult)\
                        .then_inc(max_ready, 1)

                def copy_probsT(t):
                    if t >= 2:
                        dve.wait_ge(o_done, b * NT + t - 1)
                    for j in (1, 3):
                        dve.wait_ge(pT_done, b * (4 * NT) + 4 * t + j + 1)
                        dve.tensor_copy(m.probsT[:, t % 2, j:8:4, :, :],
                                        bank(m, 4 * (t % 2) + j).rearrange("p (i k q) -> p i k q", i=2, k=2))\
                            .then_inc(pT_dve, 1)

                def normalise(t):
                    dve.wait_ge(o_done, b * NT + t + 1)
                    o = bank(m, 4 * (t % 2))[:, 0:H0 * (DH0 + 1)].rearrange("p (h d) -> p h d", h=H0)
                    step(dve.reciprocal(m.recip[:, t % 2, :], o[:, :, DH0]))
                    step.settle()
                    if t >= 2:
                        dve.wait_ge(oT_done, b * NT + t - 1)
                    dve.tensor_tensor(m.attn[:, t % 2, :].rearrange("p (h d) -> p h d", h=H0), o[:, :, 0:DH0],
                                      m.recip[:, t % 2, :].rearrange("p (h a) -> p h a", a=1)
                                      .to_broadcast([P, H0, DH0]), ALU.mult).then_inc(o_ready, 1)

                def residual(t):
                    dve.wait_ge(r_done, b * NT + t + 1)
                    dve.tensor_tensor(m.resid[:, t, :], bank(m, 4 * (t % 2) + 2)[:, 0:D], m.bo0_rows[:, :], ALU.add)\
                        .then_inc(r_ready, 1)

                row_max(0)
                row_max(1)
                copy_probsT(0)
                normalise(0)
                copy_probsT(1)
                normalise(1)
                residual(0)
                row_max(2)
                residual(1)
                row_max(3)
                copy_probsT(2)
                normalise(2)
                copy_probsT(3)
                normalise(3)
                residual(2)
                residual(3)
                step.close()

            def second_norm(b):
                step = Steps(dve, norm2_s, b * LN_STEPS, LN_STEPS)
                emit_layernorm(dve, step, m, [m.resid[:, t, :] for t in range(NT)], rn_ready,
                               lambda t: dve.wait_ge(r_ready, b * NT + t + 1))
                step.close()

            def mlp_input(b):
                dve.wait_ge(x2_done, b + 1)
                dve.tensor_scalar(m.x2T[:, 1, :], bank(m, 1), m.gamma0[:, 1:2], m.beta0[:, 1:2], ALU.mult, ALU.add)\
                    .then_inc(x2_dve, 1)

            def residual_stream(b):
                dve.wait_ge(rows_in, b * 16 + 16)
                dve.wait_ge(bias_added, b + 1)
                for t in range(NT):
                    dve.wait_ge(y_done, b * NT + t + 1)
                    dve.tensor_tensor(m.scaled[:, t, :], bank(m, (0, 1, 4, 5)[t])[:, 0:D], m.gate_rows[:, 0, :],
                                      ALU.mult).then_inc(scaled_ready, 1)
                    dve.wait_ge(scaled_ready, b * NT + t + 1)
                    dve.tensor_tensor(x_tile(b, t), x_tile(b, t), m.scaled[:, t, :], ALU.add).then_inc(x_ready, 1)

            def turn(b, norm_next):
                attention(b)
                modulate(b + 1)
                second_norm(b)
                inputs(b + 1)
                mlp_input(b)
                if norm_next:
                    first_norm(b + 2)
                residual_stream(b)

            first_norm(0)
            dve.wait_ge(x_rest, 16 * (B - 1))
            modulate(0)
            first_norm(1)
            inputs(0)
            with dve.Fori(0, B - 2) as b:
                turn(b, True)
            turn(B - 2, False)
            attention(B - 1)
            second_norm(B - 1)
            mlp_input(B - 1)
            residual_stream(B - 1)

        @block.tensor
        def _(pe):
            pe.wait_ge(w_in, 16 * 11)

            def inputs(b, first=False):
                emit_transpose_tiles(pe, m, m.xn, (0, 1), lambda t: pe.wait_ge(xn_ready, b * NT + t + 1), hT_done)
                pe.wait_ge(hT_act, b + 1)
                pe.wait_ge(hT_dve, b + 1)
                for w, at, done in ((m.wq0, 0, q_done), (m.wk0, 2, k_done)):
                    if at and not first:
                        pe.wait_ge(r_ready, b * NT)
                    for o in range(C):
                        for c in range(C):
                            mm = pe.matmul(bank(m, at + o), w[:, c, o * P:(o + 1) * P], m.hT[:, c, PAD:PAD + S],
                                           start=(c == 0), stop=(c == C - 1))
                        mm.then_inc(done, 1)
                for j in range(NT + 1):
                    for c in range(C):
                        mm = pe.matmul(bank(m, 4 + j // 2)[:, (j % 2) * D:(j % 2 + 1) * D],
                                       m.hT[:, c, j * P:(j + 1) * P], m.wv0[:, c, :], start=(c == 0), stop=(c == C - 1))
                    if j % 2 or j == NT:
                        mm.then_inc(v_done, 1)

            def attention(b):
                def scores(t):
                    if t == 0:
                        pe.wait_ge(q_ready, b * C + C)
                        pe.wait_ge(k_ready, b * C + C)
                    elif t == 1:
                        pe.wait_ge(v_ready, b * VBANKS + VBANKS)
                    else:
                        pe.wait_ge(r_ready, b * NT + t - 1)
                    variant = 0 if t == 0 else 2 if t == NT - 1 else 1
                    for j in range(4):
                        pe.matmul(bank(m, 4 * (t % 2) + j), m.ident_bf[:, :],
                                  m.band_mask[:, variant, :, :].rearrange("p r k -> p (r k)"), start=True, stop=False,
                                  skip_group_check=True)
                    for i in range(2):
                        for j in range(4):
                            mm = pe.matmul(bank(m, 4 * (t % 2) + j)[:, i * 2 * P:(i + 1) * 2 * P],
                                           m.qT[32 * j:32 * j + DH0, i, t * P:(t + 1) * P],
                                           m.kT[32 * j:32 * j + DH0, i, t * P:(t + 2) * P], start=False, stop=True,
                                           skip_group_check=True)
                    mm.then_inc(s_done, 1)

                def transpose_probs(t):
                    for j in range(4):
                        pe.wait_ge(p_ready, b * (4 * NT) + 4 * t + j + 1)
                        for i in range(2):
                            for k in range(2):
                                mm = pe.transpose(bank(m, 4 * (t % 2) + j)[:, (2 * i + k) * P:(2 * i + k + 1) * P],
                                                  m.probs[:, t % 2, j + 4 * i, k * P:(k + 1) * P], m.ident[:, :])
                        mm.then_inc(pT_done, 1)

                def weigh_values(t):
                    pe.wait_ge(pT_act, b * (2 * NT) + 2 * t + 2)
                    pe.wait_ge(pT_dve, b * (2 * NT) + 2 * t + 2)
                    for h in range(H0):
                        for k in range(2):
                            mm = pe.matmul(bank(m, 4 * (t % 2))[:, h * (DH0 + 1):(h + 1) * (DH0 + 1)],
                                           m.probsT[:, t % 2, h, k, :], m.v_ones[:, t + k, h, :],
                                           start=(k == 0), stop=(k == 1))
                    mm.then_inc(o_done, 1)

                def transpose_attn(t):
                    pe.wait_ge(o_ready, b * NT + t + 1)
                    for c in range(C):
                        mm = pe.transpose(bank(m, 4 * (t % 2) + 1)[:, c * P:(c + 1) * P],
                                          m.attn[:, t % 2, c * P:(c + 1) * P], m.ident[:, :])
                    mm.then_inc(oT_done, 1)

                def project(t):
                    pe.wait_ge(oT_ready, b * NT + t + 1)
                    out = bank(m, 4 * (t % 2) + 2)
                    for c in range(C):
                        pe.matmul(out[:, 0:D], m.attnT[:, t % 2, c, :], m.wo0[:, c, :], start=(c == 0), stop=False,
                                  skip_group_check=True)
                    for c in range(C):
                        mm = pe.matmul(out[:, c * P:(c + 1) * P], m.hT[:, c, PAD + t * P:PAD + (t + 1) * P],
                                       m.ident[:, :], start=False, stop=True, skip_group_check=True)
                    mm.then_inc(r_done, 1)

                scores(0)
                scores(1)
                transpose_probs(0)
                weigh_values(0)
                transpose_probs(1)
                transpose_attn(0)
                weigh_values(1)
                project(0)
                transpose_attn(1)
                scores(2)
                project(1)
                scores(3)
                transpose_probs(2)
                weigh_values(2)
                transpose_probs(3)
                transpose_attn(2)
                weigh_values(3)
                project(2)
                transpose_attn(3)
                project(3)

            def mlp(b, latest):
                pe.wait_ge(q_ready, latest * C + C)
                emit_transpose_tiles(pe, m, m.xn, (0, 1), lambda t: pe.wait_ge(rn_ready, b * NT + t + 1), x2_done)
                pe.wait_ge(x2_act, b + 1)
                pe.wait_ge(x2_dve, b + 1)
                pe.wait_ge(wmlp_in, 32)
                pe.wait_ge(r_ready, b * NT + NT)
                pe.wait_ge(k_ready, latest * C + C)
                pe.wait_ge(v_ready, latest * VBANKS + VBANKS)
                for f in range(NF0):
                    if f >= 6:
                        pe.wait_ge(gelu_ready, b * NF0 + f - 5)
                    for c in range(C):
                        mm = pe.matmul(bank(m, 2 + f % 6), w1[:, c, f * P:(f + 1) * P], m.x2T[:, c, :],
                                       start=(c == 0), stop=(c == C - 1))
                    mm.then_inc(up_done, 1)
                for t in range(NT):
                    out = bank(m, (0, 1, 4, 5)[t])
                    for f in range(NF0):
                        if t == 0 or f == NF0 - 1:
                            pe.wait_ge(gelu_ready, b * NF0 + f + 1)
                        pe.matmul(out[:, 0:D], m.actT[:, f, t * P:(t + 1) * P], w2[:, f, :], start=(f == 0),
                                  stop=False, skip_group_check=True)
                    for c in range(C):
                        mm = pe.matmul(out[:, c * P:(c + 1) * P], m.x2T[:, c, t * P:(t + 1) * P], m.ident[:, :],
                                       start=False, stop=True, skip_group_check=True)
                    mm.then_inc(y_done, 1)
                pe.wait_ge(scaled_ready, b * NT + NT)

            inputs(0, first=True)
            with pe.Fori(0, B - 1) as b:
                attention(b)
                inputs(b + 1)
                mlp(b, b + 1)
            attention(B - 1)
            mlp(B - 1, B - 1)

def routed_experts_block(nc, m, I, mods_dram, padded_dram):
    NG = ROWS_MOE0 // S
    NTL = ROWS_MOE0 // P
    ZR = 8
    U = 2 * NG
    ctx = ExitStack()
    with ctx:
        def sem(name):
            return ctx.enter_context(nc.semaphore(name))

        sb = tile_maker(nc, ctx)
        m.h0T = sb("h0T", [P, C, ROWS_MOE0])
        w1 = sb("w1_e", [P, 2, C, F0])
        w2 = sb("w2_e", [P, 2, NF0, D])
        actT = sb("actT_e", [P, 2, NF0, S])
        acc = sb("acc", [P, NTL, D])
        idx = sb("idx", [P, NTL, TOPK], I32)
        idx_f = sb("idx_f", [P, NTL, TOPK])
        wts = sb("wts", [P, NTL, TOPK])
        expert_i = sb("expert_i", [P, E], I32)
        expert_f = sb("expert_f", [P, E])
        hit = sb("hit", [P, TOPK, E, NTL])
        wt = sb("wt", [P, E * NTL])
        rows2 = sb("rows2", [P, NG, 4, D])
        zeros = sb("zeros", [P, ZR * D])
        zeros_ready = sem("b_zeros_ready")
        zero_filled = sem("b_zero_filled")
        route_in = sem("b_route_in")
        rows_in = sem("b_rows_in")
        rows2_in = sem("b_rows2_in")
        w_in = [sem(f"b_w_in{u}") for u in range(2)]
        iota_ready = sem("b_iota_ready")
        dve_s = sem("b_dve_steps")
        xn_ready = sem("b_xn_ready")
        hT_done = sem("b_hT_done")
        hT_act = sem("b_hT_act")
        hT_dve = sem("b_hT_dve")
        up_done = sem("b_up_done")
        gelu_ready = sem("b_gelu_ready")
        y_done = sem("b_y_done")
        acc_ready = sem("b_acc_ready")
        bias_added = sem("b_bias_added")
        x_ready = sem("b_x_ready")
        block = ctx.enter_context(nc.Block())
        STEPS_BEFORE = 2 * LN_STEPS + 7

        def load_rows(sp, b):
            sp.dma_start(m.gate_rows[:, :, :], mods_dram[0, bass.ds(b, 1), :, :].rearrange("a s d -> (a s) d")
                         .partition_broadcast(P)).then_inc(rows_in, 16)

        @block.sync
        def _(sp):
            def load_expert(e, u):
                sp.dma_start(w1[:, u, :, :], I["L0_ffn_w1"][bass.ds(e, 1), :, :]
                             .rearrange("e (c p) f -> p (e c) f", p=P)).then_inc(w_in[u], 16)
                sp.dma_start(w2[:, u, :, :], I["L0_ffn_w2"][bass.ds(e, 1), :, :]
                             .rearrange("e (f p) d -> p (e f) d", p=P)).then_inc(w_in[u], 16)

            sp.dma_start(idx[:, :, :], I["L0_ffn_expert_indices"].rearrange("(t p) k -> p t k", p=P))\
                .then_inc(route_in, 16)
            sp.dma_start(wts[:, :, :], I["L0_ffn_expert_weights"].rearrange("(t p) k -> p t k", p=P))\
                .then_inc(route_in, 16)
            load_expert(0, 0)
            load_expert(1, 1)
            for g in range(NG):
                sp.dma_start(rows2[:, g, :, :], mods_dram[0, g, :, :].partition_broadcast(P)).then_inc(rows2_in, 16)
            load_rows(sp, 0)
            with sp.Fori(1, B) as b:
                sp.wait_ge(bias_added, b)
                load_rows(sp, b)
            sp.wait_ge(zero_filled, 16 * (E * CAP // (P * ZR)))
            with sp.Fori(1, E // 2) as i:
                for u in range(2):
                    sp.wait_ge(y_done, (i - 1) * (U * NT) + (u + 1) * NG * NT)
                    load_expert(2 * i + u, u)

        @block.gpsimd
        def _(pool):
            pool.memset(zeros[:, :], 0.0).then_inc(zeros_ready, 1)
            pool.iota(expert_i[:, :], [[1, E]], base=0, channel_multiplier=0).then_inc(iota_ready, 1)
            pool.wait_ge(xn_ready, NG * NT)
            with pool.Fori(0, B) as b:
                pool.wait_ge(rows_in, b * 16 + 16)
                take_wait(pool, m)
                xb = m.x[:, bass.ds(b * (NT * D), NT * D)].rearrange("p (t d) -> p t d", t=NT)
                pool.tensor_tensor(xb, xb, m.gate_rows[:, 3:4, :].to_broadcast([P, NT, D]), ALU.add)\
                    .then_inc(bias_added, 1)

        @block.scalar
        def _(act):
            act.wait_ge(zeros_ready, 1)
            for r in range(0, E * CAP, P * ZR):
                act.dma_start(padded_dram[r:r + P * ZR, :].rearrange("(p r) d -> p (r d)", p=P), zeros[:, :])\
                    .then_inc(zero_filled, 16)
            for g in range(NG):
                act.wait_ge(hT_done, g + 1)
                act.activation(m.h0T[:, 0, g * S:(g + 1) * S], bank(m, 2 * g), ACT.Identity,
                               bias=m.mod_cols0[:, 2, 0, g:g + 1], scale=m.mod_cols0[:, 3, 0, g:g + 1])\
                    .then_inc(hT_act, 1)
            with act.Fori(0, E // 2) as i:
                for u in range(U):
                    if u >= 2:
                        act.wait_ge(y_done, i * (U * NT) + (u - 1) * NT)
                    for f in range(NF0):
                        act.wait_ge(up_done, i * (U * NF0) + u * NF0 + f + 1)
                        act.activation(actT[:, u % 2, f, :], bank(m, f % 4), ACT.Gelu).then_inc(gelu_ready, 1)

        @block.vector
        def _(dve):
            step = Steps(dve, dve_s, 0, STEPS_BEFORE)
            for g in range(NG):
                emit_layernorm(dve, step, m, [m.x[:, (g * NT + t) * D:(g * NT + t + 1) * D] for t in range(NT)],
                               xn_ready, None, (lambda: dve.wait_ge(hT_done, 1)) if g else None)
            for g in range(NG):
                dve.wait_ge(hT_done, g + 1)
                dve.tensor_scalar(m.h0T[:, 1, g * S:(g + 1) * S], bank(m, 2 * g + 1), m.mod_cols0[:, 3, 1, g:g + 1],
                                  m.mod_cols0[:, 2, 1, g:g + 1], ALU.mult, ALU.add).then_inc(hT_dve, 1)
            step(dve.memset(acc[:, :, :], 0.0))
            dve.wait_ge(route_in, 32)
            dve.wait_ge(iota_ready, 1)
            step(dve.tensor_copy(idx_f[:, :, :], idx[:, :, :]))
            step(dve.tensor_copy(expert_f[:, :], expert_i[:, :]))
            step.settle()
            for k in range(TOPK):
                step(dve.tensor_tensor(hit[:, k, :, :],
                                       expert_f[:, :].rearrange("p (e t) -> p e t", t=1).to_broadcast([P, E, NTL]),
                                       idx_f[:, :, k].rearrange("p (e t) -> p e t", e=1).to_broadcast([P, E, NTL]),
                                       ALU.is_equal))
            step.settle()
            for k in range(TOPK):
                step(dve.tensor_tensor(hit[:, k, :, :], hit[:, k, :, :],
                                       wts[:, :, k].rearrange("p (e t) -> p e t", e=1).to_broadcast([P, E, NTL]),
                                       ALU.mult))
            step.settle()
            dve.tensor_tensor(wt[:, :], hit[:, 0, :, :].rearrange("p e t -> p (e t)"),
                              hit[:, 1, :, :].rearrange("p e t -> p (e t)"), ALU.add).then_inc(acc_ready, 1)
            dve.wait_ge(acc_ready, 1)
            with dve.Fori(0, E // 2) as i:
                for u in range(U):
                    for t in range(NT):
                        tile = (u % NG) * NT + t
                        dve.wait_ge(y_done, i * (U * NT) + u * NT + t + 1)
                        dve.scalar_tensor_tensor(out=acc[:, tile, :], in0=bank(m, 4 + t)[:, 0:D],
                                                 scalar=wt[:, bass.ds((2 * i + u // NG) * NTL + tile, 1)],
                                                 in1=acc[:, tile, :], op0=ALU.mult, op1=ALU.add)\
                            .then_inc(acc_ready, 1)
            dve.wait_ge(acc_ready, 1 + (E // 2) * U * NT)
            dve.wait_ge(rows2_in, 16 * NG)
            for g in range(NG):
                a = acc[:, g * NT:(g + 1) * NT, :]
                step(dve.tensor_tensor(a, a, rows2[:, g, 2:3, :].to_broadcast([P, NT, D]), ALU.mult))
            step.settle()
            dve.wait_ge(bias_added, B)
            dve.tensor_tensor(m.x[:, 0:NTL * D], m.x[:, 0:NTL * D], acc[:, :, :].rearrange("p t d -> p (t d)"),
                              ALU.add).then_inc(x_ready, 1)

        @block.tensor
        def _(pe):
            for g in range(NG):
                emit_transpose_tiles(pe, m, m.xn, (2 * g, 2 * g + 1),
                                     lambda t: pe.wait_ge(xn_ready, g * NT + t + 1), hT_done)
            pe.wait_ge(hT_act, NG)
            pe.wait_ge(hT_dve, NG)
            with pe.Fori(0, E // 2) as i:
                def up(u):
                    if u % NG == 0:
                        pe.wait_ge(w_in[u // NG], i * 32 + 32)
                    for f in range(NF0):
                        if u or f >= 4:
                            pe.wait_ge(gelu_ready, i * (U * NF0) + u * NF0 + f - 3)
                        for c in range(C):
                            mm = pe.matmul(bank(m, f % 4), w1[:, u // NG, c, f * P:(f + 1) * P],
                                           m.h0T[:, c, (u % NG) * S:(u % NG + 1) * S],
                                           start=(c == 0), stop=(c == C - 1))
                        mm.then_inc(up_done, 1)

                def down(u):
                    pe.wait_ge(gelu_ready, i * (U * NF0) + (u + 1) * NF0)
                    for t in range(NT):
                        if u:
                            pe.wait_ge(acc_ready, i * (U * NT) + (u - 1) * NT + t + 2)
                        for f in range(NF0):
                            mm = pe.matmul(bank(m, 4 + t)[:, 0:D], actT[:, u % 2, f, t * P:(t + 1) * P],
                                           w2[:, u // NG, f, :], start=(f == 0), stop=(f == NF0 - 1))
                        mm.then_inc(y_done, 1)

                up(0)
                for u in range(1, U):
                    up(u)
                    down(u - 1)
                down(U - 1)
                pe.wait_ge(acc_ready, i * (U * NT) + U * NT + 1)


Q_PARTS = (0, 0, 1, 0, 1, 2)
K_PARTS = (0, 1, 0, 2, 1, 0)
NSLOT = len(Q_PARTS)
K_SCORE = NSLOT * DHQ
K_FULL = K_SCORE + 3
INVALID = float(1 << 20)
DKV = HKV * DHQ
VW = 32


def mixer_block(nc, m, I, mods_dram, qk_dram, padded_dram, src_dram):
    ctx = ExitStack()
    with ctx:
        def sem(name):
            return ctx.enter_context(nc.semaphore("c_" + name))

        sb = tile_maker(nc, ctx)
        wq = sb("wq1", [P, C, D])
        wkv = sb("wkv1", [P, C, 2 * D])
        wo = sb("wo1", [P, C, D])
        qw = sb("qw", [P, C, D])
        kw = sb("kw", [P, C, DKV])
        vw = sb("vw", [P, C, DKV])
        ow = sb("ow", [P, C, D])
        gate_w = sb("gate_w", [P, C, E])
        qb = sb("qb", [P, C])
        kb = sb("kb", [DKV, 1])
        vb = sb("vb_rows", [P, DKV])
        ob = sb("ob_rows", [P, D])
        n1w = sb("n1w_rows", [P, D])
        block_mask = sb("block_mask", [P, HPC1, DH1])
        head_mask = sb("head_mask", [P, HPC1])
        before = sb("before", [P, P], BF16)
        ones_bf = sb("ones_bf", [P, P], BF16)
        expert_i = sb("expert_i1", [P, E], I32)
        expert_f = sb("expert_f1", [P, E])
        first_slot = sb("first_slot", [P, E])
        hT = sb("hT1", [P, C, S])
        q_exp = sb("q_exp", [P, C, S])
        q_relu = sb("q_relu", [P, C, S])
        k_exp = sb("k_exp", [P, NT, D])
        k_relu = sb("k_relu", [P, NT, D])
        v_one = sb("v_one", [P, NT, C, P + 1])
        kv_bd = sb("kv_bd", [P, C, P + HPC1])
        den = sb("den1", [P, NT, H1])
        o1 = sb("o1", [P, NT, D])
        o1T = sb("o1T", [P, 2, C, P])
        scaled = sb("scaled1", [P, NT, D])
        q_part = sb("q_part", [P, 3, C, S], BF16)
        k_part = sb("k_part", [DKV, 3, S], BF16)
        q_rest = sb("q_rest", [P, C, S])
        k_rest = sb("k_rest", [DKV, S])
        q_stack = sb("q_stack", [K_FULL, HQ, S], BF16)
        k_stack = sb("k_stack", [K_FULL, HKV, S], BF16)
        v_tile = sb("v_tile", [P, NT, HKV, VW])
        negmax = sb("negmax1", [P, NT, HQ])
        max_rest = sb("max_rest", [P, NT, HQ])
        max_part = sb("max_part", [P, HKV, NT, REP, 3], BF16)
        maxT = sb("maxT", [3 * REP, HKV, S], BF16)
        pT = sb("pT", [P, 3, 2, S])
        oraw = sb("oraw", [P, HKV, S])
        osum = sb("osum", [P, NT, HQ])
        resid = sb("resid1", [P, NT, D])
        src = sb("src", [P, NT, D])
        probs = sb("router_probs", [P, NT, E])
        top = sb("top", [P, NT, E])
        top_i = sb("top_i", [P, NT, E], U32)
        sel = sb("sel", [P, NT, TOPK])
        wsum = sb("wsum", [P, NT, 1])
        chosen = sb("chosen", [P, TOPK, NT, E])
        load = sb("load", [P, NT, E], BF16)
        load_before = sb("load_before", [P, NT + 1, E], BF16)
        slots_e = sb("slots_e", [P, NT, E])
        over = sb("over", [P, NT, E])
        slot_k = sb("slot_k", [P, NT, TOPK])
        valid = sb("valid", [P, NT, TOPK])
        wk = sb("wk", [P, NT, TOPK])
        scatter_idx = sb("scatter_idx", [P, NT, TOPK], U32)

        w_in = sem("w_in")
        consts = sem("consts")
        masks = sem("masks")
        rows_in = sem("rows_in")
        norm_s = sem("first_norm_steps")
        linear_s = sem("linear_steps")
        inputs_s = sem("inputs_steps")
        grouped_s = sem("grouped_steps")
        route_s = sem("route_steps")
        xn_ready = sem("xn_ready")
        hT_done = sem("hT_done")
        hT_act = sem("hT_act")
        hT_dve = sem("hT_dve")
        q_done = sem("q_done")
        kv_done = sem("kv_done")
        q_min = sem("q_min_ready")
        k_min = sem("k_min_ready")
        q_act = sem("q_act")
        k_act = sem("k_act")
        qf_ready = sem("qf_ready")
        kf_ready = sem("kf_ready")
        gram_done = sem("gram_done")
        kvbd_ready = sem("kvbd_ready")
        n_done = sem("numer_done")
        o1_ready = sem("o1_ready")
        o1T_done = sem("o1T_done")
        o1T_ready = sem("o1T_ready")
        p1_done = sem("proj1_done")
        bias_added = sem("bias_added")
        scaled_ready = sem("scaled_ready")
        x_ready = sem("x_ready")
        xn2_ready = sem("xn2_ready")
        h2_done = sem("h2_done")
        h2_act = sem("h2_act")
        h2_dve = sem("h2_dve")
        qk_done = sem("qk_done")
        v_done = sem("v_done")
        part0 = sem("part0_ready")
        rest = sem("rest_ready")
        part1 = sem("part1_ready")
        part2 = sem("part2_ready")
        v_ready = sem("v_ready")
        parts_out = sem("parts_out")
        stack_in = sem("stack_in")
        s_done = sem("max_scores_done")
        max_read = sem("max_read")
        maxp_ready = sem("max_parts_ready")
        maxT_done = sem("maxT_done")
        maxT_ready = sem("maxT_ready")
        max_in = [sem(f"max_rows_in{g}") for g in range(HKV)]
        sT_done = sem("scoresT_done")
        pT_ready = sem("probsT_ready")
        pv_done = sem("pv_done")
        oraw_ready = sem("oraw_ready")
        ot_done = sem("ot_done")
        o2_ready = sem("o2_ready")
        o2T_done = sem("o2T_done")
        o2T_ready = sem("o2T_ready")
        r_done = sem("resid_done")
        r_ready = sem("resid_ready")
        src_ready = sem("src_ready")
        srcT_done = sem("srcT_done")
        srcT_ready = sem("srcT_ready")
        logits_done = sem("logits_done")
        lexp_ready = sem("logits_exp_ready")
        load_ready = sem("load_ready")
        rank_done = sem("rank_done")
        sidx_ready = sem("scatter_idx_ready")
        scattered = sem("scattered")
        src_out = sem("src_out")
        src_free = sem("src_free")
        ROUTER_STEPS = 29
        GROUPED_STEPS = 3 * HKV + NT
        ROUTE_STEPS = RMS_STEPS + ROUTER_STEPS
        NW = 15
        block = ctx.enter_context(nc.Block())

        def x_tile(b, t):
            return m.x[:, bass.ds(b * (NT * D) + t * D, D)]

        def load_rows(sp, b):
            sp.dma_start(m.gate_rows[:, :, :], mods_dram[1, bass.ds(b, 1), :, :].rearrange("a s d -> (a s) d")
                         .partition_broadcast(P)).then_inc(rows_in, 16)

        @block.sync
        def _(sp):
            for tile, name in ((wq, "L1_attn_wq"), (wo, "L1_attn_wo"), (qw, "L1_ffn_qw"), (kw, "L1_ffn_kw"),
                               (vw, "L1_ffn_vw"), (ow, "L1_ffn_ow"), (gate_w, "L1_ffn_gate_w")):
                sp.dma_start(tile[:, :, :], I[name].rearrange("(c p) n -> p c n", p=P)).then_inc(w_in, 16)
            for i, name in enumerate(("L1_attn_wk", "L1_attn_wv")):
                sp.dma_start(wkv[:, :, i * D:(i + 1) * D], I[name].rearrange("(c p) n -> p c n", p=P))\
                    .then_inc(w_in, 16)
            sp.dma_start(qb[:, :], I["L1_ffn_qb"].rearrange("(c p) -> p c", p=P), allow_slow_non_contiguous=True)\
                .then_inc(w_in, 16)
            sp.dma_start(kb[:, :], I["L1_ffn_kb"].rearrange("(p a) -> p a", a=1)).then_inc(w_in, 16)
            for tile, name in ((vb, "L1_ffn_vb"), (ob, "L1_ffn_ob"), (n1w, "L1_ffn_norm1_w")):
                sp.dma_start(tile[:, :], I[name].partition_broadcast(P)).then_inc(w_in, 16)
            load_rows(sp, 0)

            def parts(b):
                sp.wait_ge(part2, b * (C + 1) + C + 1)
                for j in range(3):
                    sp.dma_start(qk_dram[j, 0:D, :].rearrange("(c p) n -> p c n", p=P), q_part[:, j, :, :])\
                        .then_inc(parts_out, 16)
                    sp.dma_start(qk_dram[j, D:D + DKV, :], k_part[:, j, :]).then_inc(parts_out, 16)
                sp.wait_ge(parts_out, b * 96 + 96)
                for s in range(NSLOT):
                    sp.dma_start(q_stack[s * DHQ:(s + 1) * DHQ, :, :],
                                 qk_dram[Q_PARTS[s], 0:D, :].rearrange("(h d) n -> d h n", d=DHQ))\
                        .then_inc(stack_in, 16)
                    sp.dma_start(k_stack[s * DHQ:(s + 1) * DHQ, :, :],
                                 qk_dram[K_PARTS[s], D:D + DKV, :].rearrange("(h d) n -> d h n", d=DHQ))\
                        .then_inc(stack_in, 16)

            def max_rows(b):
                for g in range(HKV):
                    sp.wait_ge(maxT_ready, b * HKV + g + 1)
                    for h in range(REP):
                        sp.dma_start(q_stack[K_SCORE:K_FULL, REP * g + h, :], maxT[3 * h:3 * h + 3, g, :])\
                            .then_inc(max_in[g], 16)

            def store_src(b):
                sp.wait_ge(src_ready, b * NT + NT)
                sp.dma_start(src_dram[bass.ds(b * S, S), :].rearrange("(t p) d -> p t d", p=P), src[:, :, :])\
                    .then_inc(src_out, 16)

            parts(0)
            with sp.Fori(1, B) as b:
                sp.wait_ge(scaled_ready, b * NT)
                take_wait(sp, m)
                sp.wait_ge(bias_added, b)
                load_rows(sp, b)
                max_rows(b - 1)
                parts(b)
                store_src(b - 1)
            max_rows(B - 1)
            store_src(B - 1)

        @block.gpsimd
        def _(pool):
            pool.memset(head_mask[:, :], 1.0).then_inc(masks, 1)
            pool.memset(block_mask[:, :, :], 1.0).then_inc(masks, 1)
            pool.memset(before[:, :], 1.0).then_inc(masks, 1)
            pool.memset(ones_bf[:, :], 1.0).then_inc(consts, 1)
            pool.memset(v_one[:, :, :, :], 1.0).then_inc(consts, 1)
            pool.memset(v_tile[:, :, :, :], 0.0).then_inc(masks, 1)
            pool.memset(load_before[:, :, :], 0.0).then_inc(consts, 1)
            pool.iota(expert_i[:, :], [[1, E]], base=0, channel_multiplier=0).then_inc(consts, 1)
            pool.wait_ge(masks, 4)
            pool.memset(v_tile[:, :, :, DHQ:DHQ + 1], 1.0).then_inc(consts, 1)
            pool.affine_select(out=head_mask[:, :], in_=head_mask[:, :], compare_op=ALU.is_ge, fill=0.0, base=0,
                               pattern=[[-DH1, HPC1]], channel_multiplier=1).then_inc(masks, 1)
            pool.affine_select(out=block_mask[:, :, :], in_=block_mask[:, :, :], compare_op=ALU.is_ge, fill=0.0,
                               base=0, pattern=[[-DH1, HPC1], [0, DH1]], channel_multiplier=1).then_inc(masks, 1)
            pool.affine_select(out=before[:, :], in_=before[:, :], compare_op=ALU.is_gt, fill=0.0, base=0,
                               pattern=[[1, P]], channel_multiplier=-1).then_inc(consts, 1)
            pool.wait_ge(masks, 6)
            pool.affine_select(out=head_mask[:, :], in_=head_mask[:, :], compare_op=ALU.is_ge, fill=0.0,
                               base=DH1 - 1, pattern=[[DH1, HPC1]], channel_multiplier=-1).then_inc(consts, 1)
            pool.affine_select(out=block_mask[:, :, :], in_=block_mask[:, :, :], compare_op=ALU.is_ge, fill=0.0,
                               base=DH1 - 1, pattern=[[DH1, HPC1], [0, DH1]], channel_multiplier=-1)\
                .then_inc(consts, 1)

            def add_bias(b):
                pool.wait_ge(xn_ready, b * NT + NT)
                pool.wait_ge(rows_in, b * 16 + 16)
                take_wait(pool, m)
                xb = m.x[:, bass.ds(b * (NT * D), NT * D)].rearrange("p (t d) -> p t d", t=NT)
                pool.tensor_tensor(xb, xb, m.gate_rows[:, 1:2, :].to_broadcast([P, NT, D]), ALU.add)\
                    .then_inc(bias_added, 1)

            def scatter(b):
                pool.wait_ge(sidx_ready, b + 1)
                take_wait(pool, m)
                for t in range(NT):
                    for k in range(TOPK):
                        pool.indirect_dma_start(padded_dram, bass.IndirectOffsetOnAxis(ap=scatter_idx[:, t, k:k + 1], axis=0),
                                                src[:, t, :], None, bounds_check=E * CAP - 1, oob_is_err=False)\
                            .then_inc(scattered, 16)
                pool.wait_ge(scattered, (b + 1) * (NT * TOPK * 16))
                take_wait(pool, m)
                pool.wait_ge(src_out, (b + 1) * 16)
                pool.sem_inc(src_free, 1)

            add_bias(0)
            with pool.Fori(1, B) as b:
                add_bias(b)
                scatter(b - 1)
            scatter(B - 1)

        @block.scalar
        def _(act):
            act.wait_ge(w_in, 16 * (NW - 1))
            act.wait_ge(consts, 9)

            def linear_attention(b):
                act.wait_ge(hT_done, b + 1)
                act.activation(hT[:, 0, :], bank(m, 0), ACT.Identity, bias=m.mod_cols1[:, 0, 0, bass.ds(b, 1)],
                               scale=m.mod_cols1[:, 1, 0, bass.ds(b, 1)]).then_inc(hT_act, 1)
                for c in range(C):
                    act.wait_ge(q_min, b * C + c + 1)
                    act.activation(q_exp[:, c, :], q_exp[:, c, :], ACT.Exp).then_inc(q_act, 1)
                    act.activation(q_relu[:, c, :], bank(m, 2 + c), ACT.Relu).then_inc(q_act, 1)
                for t in range(NT):
                    act.wait_ge(k_min, b * NT + t + 1)
                    act.activation(k_exp[:, t, :], k_exp[:, t, :], ACT.Exp).then_inc(k_act, 1)
                    act.activation(k_relu[:, t, :], bank(m, 4 + t)[:, 0:D], ACT.Relu).then_inc(k_act, 1)
                    act.activation(v_one[:, t, :, 0:P], bank(m, 4 + t)[:, D:2 * D].rearrange("p (c n) -> p c n", c=C),
                                   ACT.Copy).then_inc(k_act, 1)
                for t in range(NT):
                    act.wait_ge(o1T_done, b * NT + t + 1)
                    if t >= 2:
                        act.wait_ge(p1_done, b * NT + t - 1)
                    act.activation(o1T[:, t % 2, :, :].rearrange("p c n -> p (c n)"), bank(m, 2 + t % 2)[:, 0:D],
                                   ACT.Copy).then_inc(o1T_ready, 1)

            def grouped_inputs(b):
                act.wait_ge(h2_done, b + 1)
                act.activation(hT[:, 0, :], bank(m, 6), ACT.Identity, bias=m.mod_cols1[:, 2, 0, bass.ds(b, 1)],
                               scale=m.mod_cols1[:, 3, 0, bass.ds(b, 1)]).then_inc(h2_act, 1)
                for i in range(C + 1):
                    act.wait_ge(qk_done, b * (C + 1) + i + 1)
                    if i < C:
                        act.activation(q_part[:, 0, i, :], bank(m, i), ACT.Identity, bias=qb[:, i:i + 1])\
                            .then_inc(part0, 1)
                    else:
                        act.activation(k_part[:, 0, :], bank(m, 2)[0:DKV, :], ACT.Identity, bias=kb[:, 0:1])\
                            .then_inc(part0, 1)
                for i in range(C + 1):
                    act.wait_ge(rest, b * (C + 1) + i + 1)
                    if i < C:
                        act.activation(q_part[:, 1, i, :], q_rest[:, i, :], ACT.Copy).then_inc(part1, 1)
                    else:
                        act.activation(k_part[:, 1, :], k_rest[:, :], ACT.Copy).then_inc(part1, 1)

            def grouped_attention(b):
                for u in range(32):
                    act.wait_ge(sT_done, b * 32 + u + 1)
                    if u >= 3:
                        act.wait_ge(pv_done, b * 32 + u - 2)
                    act.activation(pT[:, u % 3, :, :], m.psum[:, 2 + 2 * (u % 2):4 + 2 * (u % 2), :], ACT.Exp,
                                   scale=float(DHQ) ** -0.5).then_inc(pT_ready, 1)
                for t in range(NT):
                    act.wait_ge(o2T_done, b * NT + t + 1)
                    if t >= 2:
                        act.wait_ge(r_done, b * NT + t - 1)
                    act.activation(o1T[:, t % 2, :, :].rearrange("p c n -> p (c n)"), bank(m, 4 + t % 2)[:, 0:D],
                                   ACT.Copy).then_inc(o2T_ready, 1)

            def route(b):
                act.wait_ge(srcT_done, b + 1)
                for c in range(C):
                    act.activation(q_exp[:, c, :], bank(m, 4 + c), ACT.Copy).then_inc(srcT_ready, 1)
                act.wait_ge(logits_done, b + 1)
                act.activation(probs[:, :, :].rearrange("p t e -> p (t e)"), bank(m, 6)[:, 0:NT * E], ACT.Exp,
                               scale=-1.0).then_inc(lexp_ready, 1)

            linear_attention(0)
            grouped_inputs(0)
            with act.Fori(1, B) as b:
                grouped_attention(b - 1)
                linear_attention(b)
                grouped_inputs(b)
                route(b - 1)
            grouped_attention(B - 1)
            route(B - 1)

        @block.vector
        def _(dve):
            dve.wait_ge(w_in, 16 * (NW - 1))
            dve.memset(k_stack[K_SCORE:K_FULL, :, :], 1.0).then_inc(consts, 1)
            dve.wait_ge(consts, 9)
            dve.tensor_copy(expert_f[:, :], expert_i[:, :]).then_inc(masks, 1)
            dve.wait_ge(masks, 7)
            dve.tensor_scalar(first_slot[:, :], expert_f[:, :], float(CAP), None, ALU.mult)\
                .then_inc(src_free, 1)

            def first_norm(b):
                step = Steps(dve, norm_s, b * LN_STEPS, LN_STEPS)
                emit_layernorm(dve, step, m, [x_tile(b, t) for t in range(NT)], xn_ready)
                step.close()

            def linear_attention(b):
                step = Steps(dve, linear_s, b * (2 * NT), 2 * NT)
                dve.wait_ge(hT_done, b + 1)
                dve.tensor_scalar(hT[:, 1, :], bank(m, 1), m.mod_cols1[:, 1, 1, bass.ds(b, 1)],
                                  m.mod_cols1[:, 0, 1, bass.ds(b, 1)], ALU.mult, ALU.add).then_inc(hT_dve, 1)
                for c in range(C):
                    dve.wait_ge(q_done, b * C + c + 1)
                    dve.tensor_scalar(q_exp[:, c, :], bank(m, 2 + c), 0.0, None, ALU.min).then_inc(q_min, 1)
                for t in range(NT):
                    dve.wait_ge(kv_done, b * NT + t + 1)
                    dve.tensor_scalar(k_exp[:, t, :], bank(m, 4 + t)[:, 0:D], 0.0, None, ALU.min).then_inc(k_min, 1)
                for c in range(C):
                    dve.wait_ge(q_act, b * (2 * C) + 2 * c + 2)
                    dve.tensor_tensor(q_exp[:, c, :], q_exp[:, c, :], q_relu[:, c, :], ALU.add).then_inc(qf_ready, 1)
                for t in range(NT):
                    dve.wait_ge(k_act, b * (3 * NT) + 3 * t + 3)
                    dve.tensor_tensor(k_exp[:, t, :], k_exp[:, t, :], k_relu[:, t, :], ALU.add).then_inc(kf_ready, 1)
                for c in range(C):
                    dve.wait_ge(gram_done, b * C + c + 1)
                    dve.tensor_tensor(kv_bd[:, c, 0:P], bank(m, c)[:, 0:P],
                                      block_mask[:, :, :].rearrange("p h d -> p (h d)"), ALU.mult)\
                        .then_inc(kvbd_ready, 1)
                    dve.tensor_tensor(kv_bd[:, c, P:P + HPC1], head_mask[:, :],
                                      bank(m, c)[:, P:P + 1].to_broadcast([P, HPC1]), ALU.mult)\
                        .then_inc(kvbd_ready, 1)
                for t in range(NT):
                    dve.wait_ge(n_done, b * NT + t + 1)
                    nd = bank(m, 4 + t)[:, 0:C * (P + HPC1)].rearrange("p (c n) -> p c n", c=C)
                    step(dve.tensor_scalar(den[:, t, :].rearrange("p (c h) -> p c h", c=C), nd[:, :, P:P + HPC1],
                                           EPS_DEN, None, ALU.add))
                    step.settle()
                    step(dve.reciprocal(den[:, t, :], den[:, t, :]))
                    step.settle()
                    for c in range(C):
                        ins = dve.tensor_tensor(o1[:, t, c * P:(c + 1) * P].rearrange("p (h d) -> p h d", h=HPC1),
                                                nd[:, c, 0:P].rearrange("p (h d) -> p h d", h=HPC1),
                                                den[:, t, c * HPC1:(c + 1) * HPC1].rearrange("p (h a) -> p h a", a=1)
                                                .to_broadcast([P, HPC1, DH1]), ALU.mult)
                        ins.then_inc(o1_ready, 1)
                dve.wait_ge(bias_added, b + 1)
                for t in range(NT):
                    dve.wait_ge(p1_done, b * NT + t + 1)
                    dve.tensor_tensor(scaled[:, t, :], bank(m, t % 2)[:, 0:D], m.gate_rows[:, 0, :], ALU.mult)\
                        .then_inc(scaled_ready, 1)
                    dve.wait_ge(scaled_ready, b * NT + t + 1)
                    dve.tensor_tensor(x_tile(b, t), x_tile(b, t), scaled[:, t, :], ALU.add).then_inc(x_ready, 1)
                step.close()

            def grouped_inputs(b):
                step = Steps(dve, inputs_s, b * LN_STEPS, LN_STEPS)
                emit_layernorm(dve, step, m, [x_tile(b, t) for t in range(NT)], xn2_ready,
                               lambda t: t == 0 and (dve.wait_ge(x_ready, b * NT + NT), take_wait(dve, m)))
                dve.wait_ge(h2_done, b + 1)
                dve.tensor_scalar(hT[:, 1, :], bank(m, 7), m.mod_cols1[:, 3, 1, bass.ds(b, 1)],
                                  m.mod_cols1[:, 2, 1, bass.ds(b, 1)], ALU.mult, ALU.add).then_inc(h2_dve, 1)
                for i in range(C + 1):
                    dve.wait_ge(part0, b * (C + 1) + i + 1)
                    if i < C:
                        dve.scalar_tensor_tensor(out=q_rest[:, i, :], in0=bank(m, i), scalar=qb[:, i:i + 1],
                                                 in1=q_part[:, 0, i, :], op0=ALU.add, op1=ALU.subtract)\
                            .then_inc(rest, 1)
                    else:
                        dve.scalar_tensor_tensor(out=k_rest[:, :], in0=bank(m, 2)[0:DKV, :], scalar=kb[:, 0:1],
                                                 in1=k_part[:, 0, :], op0=ALU.add, op1=ALU.subtract)\
                            .then_inc(rest, 1)
                for i in range(C + 1):
                    dve.wait_ge(part1, b * (C + 1) + i + 1)
                    if i < C:
                        dve.tensor_tensor(q_part[:, 2, i, :], q_rest[:, i, :], q_part[:, 1, i, :], ALU.subtract)\
                            .then_inc(part2, 1)
                    else:
                        dve.tensor_tensor(k_part[:, 2, :], k_rest[:, :], k_part[:, 1, :], ALU.subtract)\
                            .then_inc(part2, 1)
                dve.wait_ge(v_done, b + 1)
                dve.tensor_tensor(v_tile[:, :, :, 0:DHQ],
                                  bank(m, 3)[:, 0:NT * DKV].rearrange("p (t g d) -> p t g d", t=NT, g=HKV),
                                  vb[:, :].rearrange("p (t g d) -> p t g d", t=1, g=HKV)
                                  .to_broadcast([P, NT, HKV, DHQ]), ALU.add).then_inc(v_ready, 1)
                step.close()

            def grouped_attention(b, last=False):
                step = Steps(dve, grouped_s, b * GROUPED_STEPS, GROUPED_STEPS)

                def row_max(g, k):
                    n = 16 * g + k
                    dve.wait_ge(s_done, b * 64 + n + 1)
                    dve.tensor_reduce(negmax[:, k // 4, REP * g + k % 4:REP * g + k % 4 + 1], bank(m, n % 2), AX.X,
                                      ALU.max, negate=True).then_inc(max_read, 1)

                def cut_max(g):
                    dve.wait_ge(max_read, b * 64 + 16 * g + 16)
                    part, head = max_part[:, g, :, :, :], slice(REP * g, REP * (g + 1))
                    step(dve.tensor_copy(part[:, :, :, 0], negmax[:, :, head]))
                    step.settle()
                    step(dve.tensor_tensor(max_rest[:, :, head], negmax[:, :, head], part[:, :, :, 0], ALU.subtract))
                    step.settle()
                    step(dve.tensor_copy(part[:, :, :, 1], max_rest[:, :, head]))
                    step.settle()
                    dve.tensor_tensor(part[:, :, :, 2], max_rest[:, :, head], part[:, :, :, 1], ALU.subtract)\
                        .then_inc(maxp_ready, 1)

                def copy_max(g):
                    dve.wait_ge(maxT_done, b * HKV + g + 1)
                    dve.tensor_copy(maxT[:, g, :], bank(m, 6 + g % 2).bitcast(BF16)[0:3 * REP, 0:S])\
                        .then_inc(maxT_ready, 1)

                def copy_weighed(g):
                    dve.wait_ge(pv_done, b * 32 + 8 * (g + 1))
                    dve.tensor_copy(oraw[:, g, :], bank(m, 6 + g % 2)).then_inc(oraw_ready, 1)

                for k in range(16):
                    row_max(0, k)
                cut_max(0)
                for k in range(16):
                    row_max(1, k)
                    if k == 3:
                        copy_max(0)
                for g in range(HKV):
                    if g:
                        copy_weighed(g - 1)
                    if g + 1 < HKV:
                        cut_max(g + 1)
                    for k in range(16):
                        if g + 2 < HKV:
                            row_max(g + 2, k)
                        if k == 3 and g + 1 < HKV:
                            copy_max(g + 1)
                    if g == HKV - 2 and not last:
                        first_norm(b + 1)
                copy_weighed(HKV - 1)
                for t in range(NT):
                    dve.wait_ge(ot_done, b * NT + t + 1)
                    o = bank(m, t).rearrange("p (h w) -> p h w", w=VW)
                    step(dve.reciprocal(osum[:, t, :], o[:, :, DHQ]))
                    step.settle()
                    dve.tensor_tensor(o1[:, t, :].rearrange("p (h d) -> p h d", h=HQ), o[:, :, 0:DHQ],
                                      osum[:, t, :].rearrange("p (h a) -> p h a", a=1).to_broadcast([P, HQ, DHQ]),
                                      ALU.mult).then_inc(o2_ready, 1)
                for t in range(NT):
                    dve.wait_ge(r_done, b * NT + t + 1)
                    dve.tensor_tensor(resid[:, t, :], bank(m, 6 + t % 2)[:, 0:D], ob[:, :], ALU.add)\
                        .then_inc(r_ready, 1)
                step.close()

            def route(b):
                step = Steps(dve, route_s, b * ROUTE_STEPS, ROUTE_STEPS)
                emit_rms_scale(dve, step, m, [resid[:, t, :] for t in range(NT)], EPS_NORM,
                               lambda t: dve.wait_ge(r_ready, b * NT + t + 1))
                dve.wait_ge(src_free, b + 1)
                for t in range(NT):
                    dve.scalar_tensor_tensor(out=src[:, t, :], in0=resid[:, t, :], scalar=m.rstd[:, t:t + 1],
                                             in1=n1w[:, :], op0=ALU.mult, op1=ALU.mult).then_inc(src_ready, 1)
                dve.wait_ge(lexp_ready, b + 1)
                step(dve.tensor_scalar(probs[:, :, :], probs[:, :, :], 1.0, None, ALU.add))
                step.settle()
                step(dve.reciprocal(probs[:, :, :], probs[:, :, :]))
                step.settle()
                take_wait(dve, m)
                step(dve.tensor_copy(load_before[:, 0, :], load_before[:, NT, :]))
                for t in range(NT):
                    step(dve.max(top[:, t, :], probs[:, t, :]))
                step.settle()
                take_wait(dve, m)
                step(dve.tensor_tensor(wsum[:, :, :], top[:, :, 0:1], top[:, :, 1:2], ALU.add))
                for t in range(NT):
                    step(dve.max_index(top_i[:, t, :], top[:, t, :], probs[:, t, :]))
                step.settle()
                step(dve.tensor_copy(sel[:, :, :], top_i[:, :, 0:TOPK]))
                step(dve.tensor_scalar(wsum[:, :, :], wsum[:, :, :], 1e-6, None, ALU.add))
                step.settle()
                step(dve.reciprocal(wsum[:, :, :], wsum[:, :, :]))
                for k in range(TOPK):
                    step(dve.tensor_tensor(chosen[:, k, :, :],
                                           expert_f[:, :].rearrange("p (t e) -> p t e", t=1).to_broadcast([P, NT, E]),
                                           sel[:, :, k:k + 1].to_broadcast([P, NT, E]), ALU.is_equal))
                step.settle()
                step(dve.tensor_tensor(load[:, :, :], chosen[:, 0, :, :], chosen[:, 1, :, :], ALU.add))
                step(dve.tensor_tensor(wk[:, :, :], top[:, :, 0:TOPK], wsum[:, :, :].to_broadcast([P, NT, TOPK]),
                                       ALU.mult))
                step.settle()
                for t in range(NT):
                    dve.tensor_tensor(load_before[:, t + 1, :], load_before[:, t, :], load[:, t, :], ALU.add)\
                        .then_inc(load_ready, 1)
                    dve.wait_ge(load_ready, b * NT + t + 1)
                dve.wait_ge(rank_done, b + 1)
                rank = bank(m, 7)[:, 0:NT * E].rearrange("p (t e) -> p t e", t=NT)
                step(dve.tensor_scalar(over[:, :, :], rank, float(CAP), INVALID, ALU.is_ge, ALU.mult))
                step(dve.tensor_tensor(slots_e[:, :, :], rank, first_slot[:, :].rearrange("p (t e) -> p t e", t=1)
                                       .to_broadcast([P, NT, E]), ALU.add))
                step.settle()
                step(dve.tensor_tensor(slots_e[:, :, :], slots_e[:, :, :], over[:, :, :], ALU.add))
                step.settle()
                for k in range(TOPK):
                    step(dve.tensor_tensor(chosen[:, k, :, :], chosen[:, k, :, :], slots_e[:, :, :], ALU.mult))
                step.settle()
                for k in range(TOPK):
                    step(dve.tensor_reduce(slot_k[:, :, k], chosen[:, k, :, :], AX.X, ALU.add))
                step.settle()
                step(dve.tensor_scalar(valid[:, :, :], slot_k[:, :, :], INVALID, None, ALU.is_lt))
                dve.tensor_copy(scatter_idx[:, :, :], slot_k[:, :, :]).then_inc(sidx_ready, 1)
                step.settle()
                at = bass.ds(b * (NT * TOPK), NT * TOPK)
                step(dve.tensor_tensor(m.gather_idx[:, at], slot_k[:, :, :].rearrange("p t k -> p (t k)"),
                                       valid[:, :, :].rearrange("p t k -> p (t k)"), ALU.mult))
                step(dve.tensor_tensor(m.gather_wt[:, at], wk[:, :, :].rearrange("p t k -> p (t k)"),
                                       valid[:, :, :].rearrange("p t k -> p (t k)"), ALU.mult))
                step.close()

            first_norm(0)
            linear_attention(0)
            grouped_inputs(0)
            with dve.Fori(1, B) as b:
                grouped_attention(b - 1)
                linear_attention(b)
                grouped_inputs(b)
                route(b - 1)
            grouped_attention(B - 1, last=True)
            route(B - 1)

        @block.tensor
        def _(pe):
            pe.wait_ge(w_in, 16 * (NW - 1))
            pe.wait_ge(consts, 9)

            def linear_attention(b):
                emit_transpose_tiles(pe, m, m.xn, (0, 1), lambda t: pe.wait_ge(xn_ready, b * NT + t + 1), hT_done)
                pe.wait_ge(hT_act, b + 1)
                pe.wait_ge(hT_dve, b + 1)
                for o in range(C):
                    for c in range(C):
                        mm = pe.matmul(bank(m, 2 + o), wq[:, c, o * P:(o + 1) * P], hT[:, c, :],
                                       start=(c == 0), stop=(c == C - 1))
                    mm.then_inc(q_done, 1)
                for t in range(NT):
                    for c in range(C):
                        mm = pe.matmul(bank(m, 4 + t), hT[:, c, t * P:(t + 1) * P], wkv[:, c, :],
                                       start=(c == 0), stop=(c == C - 1))
                    mm.then_inc(kv_done, 1)
                pe.wait_ge(kf_ready, b * NT + NT)
                for c in range(C):
                    for t in range(NT):
                        mm = pe.matmul(bank(m, c)[:, 0:P + 1], k_exp[:, t, c * P:(c + 1) * P], v_one[:, t, c, :],
                                       start=(t == 0), stop=(t == NT - 1))
                    mm.then_inc(gram_done, 1)
                pe.wait_ge(qf_ready, b * C + C)
                pe.wait_ge(kvbd_ready, b * (2 * C) + 2 * C)
                for t in range(NT):
                    for c in range(C):
                        mm = pe.matmul(bank(m, 4 + t)[:, c * (P + HPC1):(c + 1) * (P + HPC1)],
                                       q_exp[:, c, t * P:(t + 1) * P], kv_bd[:, c, :], start=True, stop=True)
                    mm.then_inc(n_done, 1)

                def transpose1(t):
                    pe.wait_ge(o1_ready, b * (C * NT) + C * t + C)
                    if t >= 2:
                        pe.wait_ge(o1T_ready, b * NT + t - 1)
                    for c in range(C):
                        mm = pe.transpose(bank(m, 2 + t % 2)[:, c * P:(c + 1) * P], o1[:, t, c * P:(c + 1) * P],
                                          m.ident[:, :])
                    mm.then_inc(o1T_done, 1)

                def project1(t):
                    pe.wait_ge(o1T_ready, b * NT + t + 1)
                    if t >= 2:
                        pe.wait_ge(scaled_ready, b * NT + t - 1)
                    for c in range(C):
                        mm = pe.matmul(bank(m, t % 2)[:, 0:D], o1T[:, t % 2, c, :], wo[:, c, :],
                                       start=(c == 0), stop=(c == C - 1))
                    mm.then_inc(p1_done, 1)

                transpose1(0)
                for t in range(1, NT):
                    transpose1(t)
                    project1(t - 1)
                project1(NT - 1)

            def grouped_inputs(b):
                emit_transpose_tiles(pe, m, m.xn, (6, 7), lambda t: pe.wait_ge(xn2_ready, b * NT + t + 1), h2_done)
                pe.wait_ge(h2_act, b + 1)
                pe.wait_ge(h2_dve, b + 1)
                for o in range(C + 1):
                    for c in range(C):
                        if o < C:
                            mm = pe.matmul(bank(m, o), qw[:, c, o * P:(o + 1) * P], hT[:, c, :],
                                           start=(c == 0), stop=(c == C - 1))
                        else:
                            mm = pe.matmul(bank(m, 2)[0:DKV, :], kw[:, c, :], hT[:, c, :],
                                           start=(c == 0), stop=(c == C - 1))
                    mm.then_inc(qk_done, 1)
                for t in range(NT):
                    for c in range(C):
                        mm = pe.matmul(bank(m, 3)[:, t * DKV:(t + 1) * DKV], hT[:, c, t * P:(t + 1) * P], vw[:, c, :],
                                       start=(c == 0), stop=(c == C - 1))
                mm.then_inc(v_done, 1)

            def grouped_attention(b):
                pe.wait_ge(rest, b * (C + 1) + C + 1)
                pe.wait_ge(v_ready, b + 1)
                pe.wait_ge(stack_in, b * (32 * NSLOT) + 32 * NSLOT)
                def max_scores(g, k):
                    n = 16 * g + k
                    if n >= 2:
                        pe.wait_ge(max_read, b * 64 + n - 1)
                    pe.matmul(bank(m, n % 2), q_stack[0:K_SCORE, REP * g + k % 4, (k // 4) * P:(k // 4 + 1) * P],
                              k_stack[0:K_SCORE, g, :], start=True, stop=True).then_inc(s_done, 1)

                def transpose_max(g):
                    if g >= 2:
                        pe.wait_ge(oraw_ready, b * HKV + g - 1)
                        take_wait(pe, m)
                    pe.wait_ge(maxp_ready, b * HKV + g + 1)
                    take_wait(pe, m)
                    for t in range(NT):
                        mm = pe.transpose(bank(m, 6 + g % 2).bitcast(BF16)[0:3 * REP, t * P:(t + 1) * P],
                                          max_part[:, g, t, :, :].rearrange("p h j -> p (h j)"), m.ident_bf[:, :])
                    mm.then_inc(maxT_done, 1)

                def unit(u):
                    return u // 8, (u // 4) % 2, u % 4

                def scoresT(u):
                    g, pair, kc = unit(u)
                    if u % 8 == 0:
                        pe.wait_ge(max_in[g], b * (16 * REP) + 16 * REP)
                    if u >= 2:
                        pe.wait_ge(pT_ready, b * 32 + u - 1)
                    for j in range(2):
                        mm = pe.matmul(bank(m, 2 + 2 * (u % 2) + j), k_stack[:, g, kc * P:(kc + 1) * P],
                                       q_stack[:, REP * g + 2 * pair + j, :], start=True, stop=True)
                    mm.then_inc(sT_done, 1)

                def weigh(u):
                    g, pair, kc = unit(u)
                    pe.wait_ge(pT_ready, b * 32 + u + 1)
                    for j in range(2):
                        q0 = 32 * (2 * pair + j)
                        mm = pe.matmul(bank(m, 6 + g % 2)[q0:q0 + VW, :], v_tile[:, kc, g, :], pT[:, u % 3, j, :],
                                       start=(kc == 0), stop=(kc == NT - 1))
                    mm.then_inc(pv_done, 1)

                for k in range(16):
                    max_scores(0, k)
                for k in range(16):
                    max_scores(1, k)
                    if k == 3:
                        transpose_max(0)
                scoresT(0)
                for g in range(HKV):
                    for i in range(8):
                        u = 8 * g + i
                        if u + 1 < 32:
                            scoresT(u + 1)
                        weigh(u)
                        if g + 2 < HKV:
                            max_scores(g + 2, 2 * i)
                            max_scores(g + 2, 2 * i + 1)
                        if i == 1 and g + 1 < HKV:
                            transpose_max(g + 1)

                pe.wait_ge(oraw_ready, b * HKV + HKV)
                for t in range(NT):
                    for g in range(HKV):
                        mm = pe.transpose(bank(m, t)[:, g * P:(g + 1) * P], oraw[:, g, t * P:(t + 1) * P],
                                          m.ident[:, :])
                    mm.then_inc(ot_done, 1)

                def transpose2(t):
                    pe.wait_ge(o2_ready, b * NT + t + 1)
                    if t >= 2:
                        pe.wait_ge(o2T_ready, b * NT + t - 1)
                    for c in range(C):
                        mm = pe.transpose(bank(m, 4 + t % 2)[:, c * P:(c + 1) * P], o1[:, t, c * P:(c + 1) * P],
                                          m.ident[:, :])
                    mm.then_inc(o2T_done, 1)

                def project2(t):
                    pe.wait_ge(o2T_ready, b * NT + t + 1)
                    if t >= 2:
                        pe.wait_ge(r_ready, b * NT + t - 1)
                    out = bank(m, 6 + t % 2)
                    for c in range(C):
                        pe.matmul(out[:, 0:D], o1T[:, t % 2, c, :], ow[:, c, :], start=(c == 0), stop=False,
                                  skip_group_check=True)
                    for c in range(C):
                        mm = pe.matmul(out[:, c * P:(c + 1) * P], hT[:, c, t * P:(t + 1) * P], m.ident[:, :],
                                       start=False, stop=True, skip_group_check=True)
                    mm.then_inc(r_done, 1)

                transpose2(0)
                for t in range(1, NT):
                    transpose2(t)
                    project2(t - 1)
                project2(NT - 1)

            def route(b):
                emit_transpose_tiles(pe, m, src, (4, 5), lambda t: pe.wait_ge(src_ready, b * NT + t + 1), srcT_done)
                pe.wait_ge(srcT_ready, b * C + C)
                for t in range(NT):
                    for c in range(C):
                        mm = pe.matmul(bank(m, 6)[:, t * E:(t + 1) * E], q_exp[:, c, t * P:(t + 1) * P],
                                       gate_w[:, c, :], start=(c == 0), stop=(c == C - 1))
                mm.then_inc(logits_done, 1)
                pe.wait_ge(load_ready, b * NT + NT)
                for t in range(NT):
                    pe.matmul(bank(m, 7)[:, t * E:(t + 1) * E], before[:, :], load[:, t, :], start=True, stop=False)
                    mm = pe.matmul(bank(m, 7)[:, t * E:(t + 1) * E], ones_bf[:, :], load_before[:, t, :],
                                   start=False, stop=True)
                mm.then_inc(rank_done, 1)

            linear_attention(0)
            grouped_inputs(0)
            with pe.Fori(1, B) as b:
                grouped_attention(b - 1)
                linear_attention(b)
                grouped_inputs(b)
                route(b - 1)
            grouped_attention(B - 1)
            route(B - 1)


def experts_block(nc, m, I, padded_dram, expert_out):
    U = 2 * CT
    ctx = ExitStack()
    with ctx:
        def sem(name):
            return ctx.enter_context(nc.semaphore("d_" + name))

        sb = tile_maker(nc, ctx)
        w1 = sb("w1_x", [P, 2, C, F1])
        w2 = sb("w2_x", [P, 2, NF1, D])
        xe = sb("xe", [P, 2, NT, D])
        xT = sb("xT_x", [P, C, S])
        actT = sb("actT_x", [P, NF1, S])
        ye = sb("ye", [P, 2, NT, D])
        w_in = [sem(f"w_in{u}") for u in range(2)]
        x_in = [sem(f"x_in{u}") for u in range(2)]
        stored = [sem(f"stored{u}") for u in range(2)]
        xT_done = sem("xT_done")
        xT_act = sem("xT_act")
        xT_dve = sem("xT_dve")
        up_done = sem("up_done")
        gelu_ready = sem("gelu_ready")
        y_done = sem("y_done")
        ye_ready = sem("ye_ready")
        ye_free = sem("ye_free")
        block = ctx.enter_context(nc.Block())

        @block.sync
        def _(sp):
            def load_expert(e, slot):
                sp.dma_start(w1[:, slot, :, :], I["L1_ffn_w1"][bass.ds(e, 1), :, :]
                             .rearrange("e (c p) f -> p (e c) f", p=P)).then_inc(w_in[slot], 16)
                sp.dma_start(w2[:, slot, :, :], I["L1_ffn_w2"][bass.ds(e, 1), :, :]
                             .rearrange("e (f p) d -> p (e f) d", p=P)).then_inc(w_in[slot], 16)

            def load_rows(i, u):
                sp.dma_start(xe[:, u % 2, :, :], padded_dram[bass.ds((i * U + u) * S, S), :]
                             .rearrange("(t p) d -> p t d", p=P)).then_inc(x_in[u % 2], 16)

            def store_rows(i, u):
                sp.wait_ge(ye_ready, i * (2 * U) + 2 * u + 2)
                sp.dma_start(expert_out[bass.ds((i * U + u) * S, S), :].rearrange("(t p) d -> p t d", p=P),
                             ye[:, u % 2, :, :]).then_inc(stored[u % 2], 16)

            def turn(i, last):
                for u in range(U):
                    if not (last and u + 2 >= U):
                        sp.wait_ge(xT_done, i * U + u + 1)
                        load_rows(i, u + 2)
                    if u:
                        store_rows(i, u - 1)
                    if u == CT and not last:
                        load_expert(2 * i + 2, 0)
                store_rows(i, U - 1)
                if not last:
                    load_expert(2 * i + 3, 1)

            load_rows(0, 0)
            load_expert(0, 0)
            load_rows(0, 1)
            load_expert(1, 1)
            with sp.Fori(0, E // 2 - 1) as i:
                turn(i, False)
            turn(E // 2 - 1, True)

        @block.gpsimd
        def _(pool):
            pool.sem_inc(ye_free, 2)
            with pool.Fori(0, E // 2) as i:
                for u in range(U):
                    pool.wait_ge(stored[u % 2], i * (16 * CT) + 16 * (u // 2) + 16)
                    pool.sem_inc(ye_free, 1)

        @block.scalar
        def _(act):
            with act.Fori(0, E // 2) as i:
                def evacuate(u):
                    act.wait_ge(xT_done, i * U + u + 1)
                    act.activation(xT[:, 0, :], bank(m, 0), ACT.Copy).then_inc(xT_act, 1)

                evacuate(0)
                for u in range(U):
                    for f in range(NF1):
                        act.wait_ge(up_done, i * (U * NF1) + u * NF1 + f + 1)
                        act.activation(actT[:, f, :], bank(m, 2 + f), ACT.Gelu).then_inc(gelu_ready, 1)
                    if u + 1 < U:
                        evacuate(u + 1)

        @block.vector
        def _(dve):
            with dve.Fori(0, E // 2) as i:
                def evacuate(u):
                    dve.wait_ge(xT_done, i * U + u + 1)
                    dve.tensor_copy(xT[:, 1, :], bank(m, 1)).then_inc(xT_dve, 1)

                evacuate(0)
                for u in range(U):
                    if u + 1 < U:
                        evacuate(u + 1)
                    dve.wait_ge(ye_free, i * U + u + 1)
                    take_wait(dve, m)
                    for h in range(2):
                        dve.wait_ge(y_done, i * (2 * U) + 2 * u + h + 1)
                        dve.tensor_copy(ye[:, u % 2, 2 * h:2 * h + 2, :].rearrange("p t d -> p (t d)"),
                                        bank(m, 6 + h)).then_inc(ye_ready, 1)

        @block.tensor
        def _(pe):
            with pe.Fori(0, E // 2) as i:
                def transpose(u):
                    pe.wait_ge(x_in[u % 2], i * (16 * CT) + 16 * (u // 2) + 16)
                    for t in range(NT):
                        for c in range(C):
                            mm = pe.transpose(bank(m, c)[:, t * P:(t + 1) * P], xe[:, u % 2, t, c * P:(c + 1) * P],
                                              m.ident[:, :])
                    mm.then_inc(xT_done, 1)

                def up(u):
                    pe.wait_ge(xT_act, i * U + u + 1)
                    pe.wait_ge(xT_dve, i * U + u + 1)
                    if u % CT == 0:
                        pe.wait_ge(w_in[u // CT], i * 32 + 32)
                    for f in range(NF1):
                        for c in range(C):
                            mm = pe.matmul(bank(m, 2 + f), w1[:, u // CT, c, f * P:(f + 1) * P], xT[:, c, :],
                                           start=(c == 0), stop=(c == C - 1))
                        mm.then_inc(up_done, 1)

                def down(u):
                    pe.wait_ge(gelu_ready, i * (U * NF1) + (u + 1) * NF1)
                    for h in range(2):
                        if u:
                            pe.wait_ge(ye_ready, i * (2 * U) + 2 * u - 1 + h)
                        for t in range(2 * h, 2 * h + 2):
                            for f in range(NF1):
                                mm = pe.matmul(bank(m, 6 + h)[:, (t % 2) * D:(t % 2 + 1) * D],
                                               actT[:, f, t * P:(t + 1) * P], w2[:, u // CT, f, :],
                                               start=(f == 0), stop=(f == NF1 - 1))
                        mm.then_inc(y_done, 1)

                transpose(0)
                for u in range(U):
                    up(u)
                    if u + 1 < U:
                        transpose(u + 1)
                    down(u)
                pe.wait_ge(ye_ready, i * (2 * U) + 2 * U)
                take_wait(pe, m)


def combine_block(nc, m, I, mods_dram, src_dram, expert_out, out):
    ctx = ExitStack()
    with ctx:
        def sem(name):
            return ctx.enter_context(nc.semaphore("e_" + name))

        sb = tile_maker(nc, ctx)
        src = sb("src_e", [P, 2, NT, D])
        gate2 = sb("gate2", [P, 2, D])
        n2w = sb("n2w_rows", [P, D])
        idx_b = sb("idx_b", [P, 2, NT * TOPK], U32)
        got = sb("got", [P, 2, NT, TOPK, D])
        y = sb("y_e", [P, NT, D])
        part = sb("part_e", [P, NT, D])
        z = sb("z_e", [P, NT, D])
        n2w_in = sem("n2w_in")
        src_in = [sem(f"src_in{u}") for u in range(2)]
        gathered = [sem(f"gathered{u}") for u in range(2)]
        idx_ready = sem("idx_ready")
        used = sem("buffers_free")
        dve_s = sem("dve_steps")
        x_ready = sem("x_ready")
        stored = sem("stored")
        block = ctx.enter_context(nc.Block())
        PER = 2 * NT + 1 + NT + RMS_STEPS
        CHUNK = NT * D

        @block.sync
        def _(sp):
            sp.dma_start(n2w[:, :], I["L1_ffn_norm2_w"].partition_broadcast(P)).then_inc(n2w_in, 16)
            with sp.Fori(0, B // 2) as i:
                for u in range(2):
                    sp.wait_ge(used, 2 * i + u + 1)
                    sp.dma_start(src[:, u, :, :], src_dram[bass.ds((2 * i + u) * S, S), :]
                                 .rearrange("(t p) d -> p t d", p=P)).then_inc(src_in[u], 16)
                    sp.dma_start(gate2[:, u, :], mods_dram[1, bass.ds(2 * i + u, 1), 2:3, :]
                                 .rearrange("a s d -> (a s d)").partition_broadcast(P)).then_inc(src_in[u], 16)

        @block.gpsimd
        def _(pool):
            with pool.Fori(0, B // 2) as i:
                for u in range(2):
                    pool.wait_ge(used, 2 * i + u + 1)
                    take_wait(pool, m)
                    pool.tensor_copy(idx_b[:, u, :], m.gather_idx[:, bass.ds((2 * i + u) * (NT * TOPK), NT * TOPK)])\
                        .then_inc(idx_ready, 1)
                    pool.wait_ge(idx_ready, 2 * i + u + 1)
                    take_wait(pool, m)
                    for t in range(NT):
                        for k in range(TOPK):
                            at = idx_b[:, u, t * TOPK + k:t * TOPK + k + 1]
                            pool.indirect_dma_start(got[:, u, t, k, :], None, expert_out,
                                                    bass.IndirectOffsetOnAxis(ap=at, axis=0),
                                                    bounds_check=E * CAP - 1, oob_is_err=False)\
                                .then_inc(gathered[u], 16)

        @block.scalar
        def _(act):
            with act.Fori(0, B) as b:
                act.wait_ge(x_ready, b + 1)
                act.dma_start(out[bass.ds(b, 1), :, :].rearrange("b (t p) d -> p (b t) d", p=P),
                              m.x[:, bass.ds(b * CHUNK, CHUNK)].rearrange("p (t d) -> p t d", t=NT))\
                    .then_inc(stored, 16)
            act.wait_ge(stored, 16 * B)

        @block.vector
        def _(dve):
            dve.sem_inc(used, 2)
            dve.wait_ge(n2w_in, 16)
            with dve.Fori(0, B // 2) as i:
                for u in range(2):
                    n = 2 * i + u
                    step = Steps(dve, dve_s, n * PER, PER)
                    dve.wait_ge(src_in[u], i * 32 + 32)
                    take_wait(dve, m)
                    step(dve.tensor_tensor(gate2[:, u, :], gate2[:, u, :], n2w[:, :], ALU.mult))
                    dve.wait_ge(gathered[u], i * (16 * NT * TOPK) + 16 * NT * TOPK)
                    take_wait(dve, m)

                    def weight(t, k):
                        return m.gather_wt[:, bass.ds(n * (NT * TOPK) + t * TOPK + k, 1)]

                    for t in range(NT):
                        step(dve.scalar_tensor_tensor(out=part[:, t, :], in0=got[:, u, t, 0, :], scalar=weight(t, 0),
                                                      in1=src[:, u, t, :], op0=ALU.mult, op1=ALU.add))
                    step.settle()
                    take_wait(dve, m)
                    for t in range(NT):
                        step(dve.scalar_tensor_tensor(out=y[:, t, :], in0=got[:, u, t, 1, :], scalar=weight(t, 1),
                                                      in1=part[:, t, :], op0=ALU.mult, op1=ALU.add))
                    step.settle()
                    take_wait(dve, m)
                    emit_rms_scale(dve, step, m, [y[:, t, :] for t in range(NT)], EPS_NORM)
                    for t in range(NT):
                        step(dve.scalar_tensor_tensor(out=z[:, t, :], in0=y[:, t, :], scalar=m.rstd[:, t:t + 1],
                                                      in1=gate2[:, u, :], op0=ALU.mult, op1=ALU.mult))
                    step.settle()
                    dve.sem_inc(used, 1)
                    xb = m.x[:, bass.ds(n * CHUNK, CHUNK)]
                    dve.tensor_tensor(xb, xb, z[:, :, :].rearrange("p t d -> p (t d)"), ALU.add).then_inc(x_ready, 1)
                    step.close()


def build_program(nc, I, out):
    mods_dram = nc.dram_tensor("mods", (2, B, 4, D), F32, kind="Internal").ap()
    qk_dram = nc.dram_tensor("qk_parts", (3, D + DKV, S), BF16, kind="Internal").ap()
    padded_dram = nc.dram_tensor("padded", (E * CAP, D), F32, kind="Internal").ap()
    expert_out = nc.dram_tensor("expert_out", (E * CAP, D), F32, kind="Internal").ap()
    src_dram = nc.dram_tensor("src_rows", (T, D), F32, kind="Internal").ap()
    ctx = ExitStack()
    with ctx:
        m = allocate(nc, ctx)
        setup_block(nc, m, I, mods_dram)
        local_attention_block(nc, m, I, mods_dram)
        routed_experts_block(nc, m, I, mods_dram, padded_dram)
        mixer_block(nc, m, I, mods_dram, qk_dram, padded_dram, src_dram)
        experts_block(nc, m, I, padded_dram, expert_out)
        combine_block(nc, m, I, mods_dram, src_dram, expert_out, out)


_TRANSPOSED = ("L1_attn_wq", "L1_attn_wk", "L1_attn_wv", "L1_attn_wo")


def kernel(**inputs):
    import numpy as _np
    import concourse.bacc as _bacc
    from concourse import mybir as _mybir
    from concourse.bass_utils import run_bass_kernel_spmd as _run

    nc = _bacc.Bacc("TRN2", target_bir_lowering=False, num_devices=1)
    arrays, aps = {}, {}
    for name, a in inputs.items():
        a = _np.asarray(a)
        a = _np.ascontiguousarray(a.T if name in _TRANSPOSED else a)
        arrays[f"in_{name}_dram"] = a
        aps[name] = nc.dram_tensor(f"in_{name}_dram", a.shape, _mybir.dt.from_np(a.dtype), kind="ExternalInput").ap()
    out = nc.dram_tensor("out_0_dram", (B, S, D), F32, kind="ExternalOutput").ap()
    build_program(nc, aps, out)
    r = _run(nc, [arrays], core_ids=[0])
    return r.results[0]["out_0_dram"]
```

```python
from contextlib import ExitStack

import concourse.bass as bass
from concourse import mybir

F32 = mybir.dt.float32
BF16 = mybir.dt.bfloat16
I32 = mybir.dt.int32
U32 = mybir.dt.uint32
ACT = mybir.ActivationFunctionType
ALU = mybir.AluOpType
AX = mybir.AxisListType

P = 128
D = 256
C = D // P
B = 16
S = 512
NT = S // P
T = B * S
PAD = 64
SP_ = S + 2 * PAD
LN_EPS = 1e-5
NEG = -1e30

H0, DH0 = 8, 32
SCALE0 = float(DH0) ** -0.5
F0 = 1024
NF0 = F0 // P
E = 8
TOPK = 2
H1, DH1 = 16, 16
HPC1 = P // DH1
EPS_DEN = 1e-6
HQ, HKV, DHQ = 16, 4, 16
REP = HQ // HKV
EPS_NORM = 1e-6
F1 = 512
NF1 = F1 // P
CAP = int(1.25 * T * TOPK / E)
CT = CAP // S
ROWS_MOE0 = 1024
RSQRT_MAGIC = float(0x5F3759DF)


Q_PARTS = (0, 0, 1, 0, 1, 2)
K_PARTS = (0, 1, 0, 2, 1, 0)
NSLOT = len(Q_PARTS)
K_SCORE = NSLOT * DHQ
K_FULL = K_SCORE + 3
INVALID = float(1 << 20)
DKV = HKV * DHQ
VW = 32


class Steps:

    def __init__(self, eng, sem, base, per):
        self.eng, self.sem, self.base, self.per, self.n = eng, sem, base, per, 0

    def __call__(self, ins):
        ins.then_inc(self.sem, 1)
        self.n += 1

    def settle(self):
        self.eng.wait_ge(self.sem, self.base + self.n)

    def close(self):
        assert self.n == self.per, (self.n, self.per)


def bank(m, i):
    return m.psum[:, i, :]


def tile_maker(nc, ctx):

    def sb(name, shape, dtype=F32):
        return ctx.enter_context(nc.sbuf_tensor(name, shape, dtype))

    return sb


def allocate(nc, ctx):

    class Memory:
        pass

    m = Memory()

    sb = tile_maker(nc, ctx)
    m.waits_taken = ctx.enter_context(nc.semaphore("waits_taken"))
    m.x_first = ctx.enter_context(nc.semaphore("x_first"))
    m.x_rest = ctx.enter_context(nc.semaphore("x_rest"))
    m.mixer_w_in = ctx.enter_context(nc.semaphore("mixer_w_in"))
    m.psum = ctx.enter_context(nc.psum_tensor("psum", [P, 8, 512], F32))
    m.x = sb("x", [P, T // P * D])
    m.ident = sb("ident", [P, P])
    m.ident_bf = sb("ident_bf", [P, P], BF16)
    m.band_mask = sb("band_mask", [P, 3, 2, D], BF16)
    m.ones_col = sb("ones_col", [P, 1])
    m.mod_cols0 = sb("mod_cols0", [P, 4, C, B])
    m.mod_cols1 = sb("mod_cols1", [P, 4, C, B])
    m.gate_rows = sb("gate_rows", [P, 4, D])
    m.gather_idx = sb("gather_idx", [P, T // P * TOPK], U32)
    m.gather_wt = sb("gather_wt", [P, T // P * TOPK])
    m.wq1 = sb("wq1", [P, C, D])
    m.wkv1 = sb("wkv1", [P, C, 2 * D])
    m.wo1 = sb("wo1", [P, C, D])
    m.qw = sb("qw", [P, C, D])
    m.kw = sb("kw", [P, C, DKV])
    m.vw = sb("vw", [P, C, DKV])
    m.ow = sb("ow", [P, C, D])
    m.gate_w = sb("gate_w", [P, C, E])
    m.qb = sb("qb", [P, C])
    m.kb = sb("kb", [DKV, 1])
    m.vb = sb("vb_rows", [P, DKV])
    m.ob = sb("ob_rows", [P, D])
    m.n1w = sb("n1w_rows", [P, D])
    m.bn = sb("bn", [P, 2 * NT, 6])
    m.meanvar = sb("meanvar", [P, 2 * NT, 2])
    m.var_eps = sb("var_eps", [P, 2 * NT])
    m.newton = sb("newton", [P, 2 * NT])
    m.rstd = sb("rstd", [P, 2 * NT])
    m.xn = sb("xn", [P, NT, D])
    return m


def take_wait(eng, m):
    eng.sem_inc(m.waits_taken, 1)


def emit_rsqrt(dve, step, m, out, var, eps, n):
    a, h = m.var_eps[:, 0:n], m.newton[:, 0:n]
    step(dve.tensor_scalar(a, var, eps, None, ALU.add))
    step.settle()
    step(dve.tensor_scalar(out.bitcast(I32), a.bitcast(I32), -0.5, RSQRT_MAGIC, ALU.mult, ALU.add))
    step.settle()
    for _ in range(3):
        step(dve.scalar_tensor_tensor(out=h, in0=out, scalar=-0.5, in1=out, op0=ALU.mult, op1=ALU.mult))
        step.settle()
        step(dve.tensor_tensor(h, h, a, ALU.mult))
        step.settle()
        step(dve.scalar_tensor_tensor(out=out, in0=h, scalar=1.5, in1=out, op0=ALU.add, op1=ALU.mult))
        step.settle()


def emit_layernorm(dve, step, m, tiles, ready, tile_wait=None, free_wait=None, out=None):
    for t in range(NT):
        if tile_wait:
            tile_wait(t)
        step(dve.bn_stats(m.bn[:, t, :], tiles[t]))
    step.settle()
    take_wait(dve, m)
    for t in range(NT):
        step(dve.bn_aggr(m.meanvar[:, t, :], m.bn[:, t, :]))
    step.settle()
    emit_rsqrt(dve, step, m, m.rstd[:, 0:NT], m.meanvar[:, 0:NT, 1], LN_EPS, NT)
    if free_wait:
        free_wait()
    for t in range(NT):
        dve.tensor_scalar((out or m.xn)[:, t, :], tiles[t], m.meanvar[:, t, 0:1], m.rstd[:, t:t + 1],
                          ALU.subtract, ALU.mult).then_inc(ready, 1)


LN_STEPS = 2 * NT + 11


def emit_rms_scale(dve, step, m, tiles, eps, tile_wait=None):
    n = len(tiles)
    for t in range(n):
        if tile_wait:
            tile_wait(t)
        step(dve.bn_stats(m.bn[:, t, :], tiles[t]))
    step.settle()
    take_wait(dve, m)
    for t in range(n):
        step(dve.bn_aggr(m.meanvar[:, t, :], m.bn[:, t, :]))
    step.settle()
    step(dve.tensor_tensor(m.meanvar[:, 0:n, 0], m.meanvar[:, 0:n, 0], m.meanvar[:, 0:n, 0], ALU.mult))
    step.settle()
    step(dve.tensor_tensor(m.meanvar[:, 0:n, 1], m.meanvar[:, 0:n, 1], m.meanvar[:, 0:n, 0], ALU.add))
    step.settle()
    emit_rsqrt(dve, step, m, m.rstd[:, 0:n], m.meanvar[:, 0:n, 1], eps, n)


RMS_STEPS = LN_STEPS + 2


def emit_transpose_tiles(pe, m, src, banks, wait, done):
    for t in range(NT):
        wait(t)
        for c in range(C):
            mm = pe.transpose(bank(m, banks[c])[:, t * P:(t + 1) * P], src[:, t, c * P:(c + 1) * P], m.ident[:, :])
    mm.then_inc(done, 1)


def setup_block(nc, m, I, mods_dram):
    ctx = ExitStack()
    with nc.cleanup_on_exit(), ctx:
        def sb(name, shape, dtype=F32):
            return ctx.enter_context(nc.sbuf_tensor(name, shape, dtype))

        def sem(name):
            return nc.alloc_semaphore(name=name)

        cond = sb("cond", [B, 2, D])
        wmod = sb("wmod", [P, 2, C, 6 * D])
        expc = sb("expc", [B, 2, D])
        silu = sb("silu", [B, 2, D])
        condT = sb("condT", [P, 2, C, B])
        mod = sb("mod", [B, 2, 6, D])
        sign = sb("sign", [B, 2, 2, D])
        rows = sb("rows", [B, 2, 4, D])
        bias_rows = sb("bias_rows", [B, 3, D])
        cond_in = sem("cond_in")
        wmod_in = [sem("wmod_in0"), sem("wmod_in1")]
        zeroed = sem("zeroed")
        constants = sem("constants")
        exp_done = sem("exp_done")
        step_s = sem("setup_steps")
        silu_ready = sem("silu_ready")
        condT_done = sem("condT_done")
        condT_ready = sem("condT_ready")
        mod_done = sem("mod_done")
        mod_ready = sem("mod_ready")
        rows_ready = sem("rows_ready")
        cols_done = sem("cols_done")
        rows_out = sem("rows_out")
        NBLK = 6 * D // 512
        block = ctx.enter_context(nc.Block())

        @block.sync
        def _(sp):
            for layer in (0, 1):
                sp.dma_start(cond[:, layer, :], I[f"L{layer}_c"]).then_inc(cond_in, 16)
            for i, n in enumerate(("L0_attn_b2", "L0_ffn_bias", "L1_attn_bo")):
                sp.dma_start(bias_rows[:, i, :], I[n].partition_broadcast(B)).then_inc(cond_in, 16)
            xv = I["L0_attn_x"].rearrange("b (t p) d -> b p t d", p=P)
            xs = m.x[:, :].rearrange("p (b t d) -> p b t d", b=B, d=D)
            for b in range(B):
                sp.dma_start(xs[:, b, :, :], xv[b]).then_inc(m.x_first if b < 2 else m.x_rest, 16)
            for layer in (0, 1):
                sp.wait_ge(rows_ready, 2 * (layer + 1))
                sp.dma_start(mods_dram[layer], rows[:, layer, :, :]).then_inc(rows_out, 16)
            sp.wait_ge(rows_out, 32)

        @block.gpsimd
        def _(pool):
            pool.memset(m.ident[:, :], 0.0).then_inc(zeroed, 1)
            pool.memset(m.ident_bf[:, :], 0.0).then_inc(zeroed, 1)
            pool.memset(m.band_mask[:, :, :, :], 0.0).then_inc(zeroed, 1)
            pool.memset(m.ones_col[:, :], 1.0).then_inc(constants, 1)
            pool.wait_ge(zeroed, 3)
            for eye in (m.ident, m.ident_bf):
                pool.affine_select(out=eye[:, :], in_=eye[:, :], compare_op=ALU.not_equal, fill=1.0, base=0,
                                   pattern=[[-1, P]], channel_multiplier=1).then_inc(constants, 1)
            w = m.band_mask[:, :, :, :].rearrange("p v r j -> p (v r) j")
            pool.affine_select(out=w, in_=w, compare_op=ALU.is_ge, fill=NEG, base=0, pattern=[[0, 6], [1, D]],
                               channel_multiplier=-1).then_inc(zeroed, 1)
            pool.wait_ge(zeroed, 4)
            pool.affine_select(out=w, in_=w, compare_op=ALU.is_ge, fill=NEG, base=2 * PAD, pattern=[[0, 6], [-1, D]],
                               channel_multiplier=1).then_inc(zeroed, 1)
            pool.wait_ge(zeroed, 5)
            pool.affine_select(out=m.band_mask[:, 0, :, :], in_=m.band_mask[:, 0, :, :], compare_op=ALU.is_ge,
                               fill=NEG, base=-PAD, pattern=[[0, 2], [1, D]], channel_multiplier=0)\
                .then_inc(constants, 1)
            pool.affine_select(out=m.band_mask[:, 2, :, :], in_=m.band_mask[:, 2, :, :], compare_op=ALU.is_ge,
                               fill=NEG, base=PAD + P - 1, pattern=[[0, 2], [-1, D]], channel_multiplier=0)\
                .then_inc(constants, 1)

        @block.scalar
        def _(act):
            for layer in (0, 1):
                act.dma_start(wmod[:, layer, :, :], I[f"L{layer}_wmod"].rearrange("(c p) n -> p c n", p=P))\
                    .then_inc(wmod_in[layer], 16)
            act.wait_ge(cond_in, 16 * 5)
            act.activation(expc[:, :, :], cond[:, :, :], ACT.Exp, scale=-1.0).then_inc(exp_done, 1)

        @block.vector
        def _(dve):
            step = Steps(dve, step_s, 0, 0)
            dve.wait_ge(exp_done, 1)
            step(dve.tensor_scalar(expc[:, :, :], expc[:, :, :], 1.0, None, ALU.add))
            step.settle()
            step(dve.reciprocal(expc[:, :, :], expc[:, :, :]))
            step.settle()
            dve.tensor_tensor(silu[:, :, :], cond[:, :, :], expc[:, :, :], ALU.mult).then_inc(silu_ready, 1)
            dve.wait_ge(condT_done, 1)
            dve.tensor_copy(condT[:, :, :, :].rearrange("p l c b -> p (l c b)"), bank(m, 7)[:, 0:2 * C * B])\
                .then_inc(condT_ready, 1)
            for layer in (0, 1):
                dve.wait_ge(mod_done, NBLK * (layer + 1))
                for n in range(NBLK):
                    step(dve.tensor_copy(mod[:, layer, 2 * n:2 * n + 2, :].rearrange("b s d -> b (s d)"),
                                         bank(m, NBLK * layer + n)[0:B, :]))
                step.settle()
                step(dve.tensor_scalar(mod[:, layer, 1:5:3, :], mod[:, layer, 1:5:3, :], 1.0, None, ALU.add))
                gates = mod[:, layer, 2:6:3, :]
                step(dve.tensor_scalar(sign[:, layer, :, :], gates, 0.0, None, ALU.is_ge))
                step.settle()
                step(dve.tensor_scalar(sign[:, layer, :, :], sign[:, layer, :, :], 2.0, -1.0, ALU.mult, ALU.add))
                step.settle()
                step(dve.tensor_tensor(gates, gates, sign[:, layer, :, :], ALU.mult))
                step.settle()
                step(dve.tensor_scalar(gates, gates, 0.25, None, ALU.max))
                step.settle()
                step(dve.tensor_tensor(rows[:, layer, 0:3:2, :], gates, sign[:, layer, :, :], ALU.mult))
                step.settle()
                if layer == 0:
                    dve.tensor_tensor(rows[:, 0, 1, :], rows[:, 0, 0, :], bias_rows[:, 0, :], ALU.mult)\
                        .then_inc(rows_ready, 1)
                    dve.tensor_tensor(rows[:, 0, 3, :], rows[:, 0, 2, :], bias_rows[:, 1, :], ALU.mult)\
                        .then_inc(rows_ready, 1)
                else:
                    dve.tensor_tensor(rows[:, 1, 1, :], rows[:, 1, 0, :], bias_rows[:, 2, :], ALU.mult)\
                        .then_inc(rows_ready, 1)
                    dve.memset(rows[:, 1, 3, :], 0.0).then_inc(rows_ready, 1)
            for layer in (0, 1):
                dve.wait_ge(cols_done, layer + 1)
                dve.tensor_copy((m.mod_cols0, m.mod_cols1)[layer][:, :, :, :].rearrange("p s c b -> p (s c b)"),
                                bank(m, 6 + layer)[:, 0:4 * C * B]).then_inc(mod_ready, 1)

        @block.tensor
        def _(pe):
            pe.wait_ge(constants, 5)
            pe.wait_ge(silu_ready, 1)
            for layer in (0, 1):
                for c in range(C):
                    j = (layer * C + c) * B
                    mm = pe.transpose(bank(m, 7)[:, j:j + B], silu[:, layer, c * P:(c + 1) * P], m.ident[0:B, 0:B])
            mm.then_inc(condT_done, 1)
            pe.wait_ge(condT_ready, 1)
            for layer in (0, 1):
                pe.wait_ge(wmod_in[layer], 16)
                for n in range(NBLK):
                    for c in range(C):
                        mm = pe.matmul(bank(m, NBLK * layer + n)[0:B, :], condT[:, layer, c, :],
                                       wmod[:, layer, c, 512 * n:512 * (n + 1)], start=(c == 0), stop=(c == C - 1))
                    mm.then_inc(mod_done, 1)
            for layer in (0, 1):
                pe.wait_ge(rows_ready, 2 * (layer + 1))
                for i, slot in enumerate((0, 1, 3, 4)):
                    for c in range(C):
                        j = (i * C + c) * B
                        mm = pe.transpose(bank(m, 6 + layer)[:, j:j + B], mod[:, layer, slot, c * P:(c + 1) * P],
                                          m.ident[0:B, 0:B])
                mm.then_inc(cols_done, 1)


VBANKS = 3


def local_attention_block(nc, m, I, mods_dram, padded_dram):
    ctx = ExitStack()
    with nc.cleanup_on_exit(), ctx:
        def sem(name):
            return nc.alloc_semaphore(name=name)

        sb = tile_maker(nc, ctx)
        m.wq0, m.wk0, m.wv0, m.wo0 = (sb(n, [P, C, D]) for n in ("wq0", "wk0", "wv0", "wo0"))
        m.bq0, m.bk0, m.gamma0, m.beta0 = (sb(n, [P, C]) for n in ("bq0", "bk0", "gamma0", "beta0"))
        m.b1_0 = sb("b1_0", [P, NF0])
        m.bv0_rows = sb("bv0_rows", [P, D])
        m.bo0_rows = sb("bo0_rows", [P, D])
        w1 = sb("w1_0", [P, C, F0])
        w2 = sb("w2_0", [P, NF0, D])
        m.hT = sb("hT", [P, C, SP_])
        m.qT = sb("qT", [P, C, S])
        m.kT = sb("kT", [P, C, SP_])
        m.v_ones = sb("v_ones", [P, NT + 1, H0, DH0 + 1])
        m.negmax = sb("negmax", [P, 2, H0])
        m.bias_exp = sb("bias_exp", [P, 2, H0])
        m.probs = sb("probs", [P, 2, H0, 2 * P])
        m.probsT = sb("probsT", [P, 2, H0, 2, P])
        m.recip = sb("recip", [P, 2, H0])
        m.attn = sb("attn", [P, 2, D])
        m.attnT = sb("attnT", [P, 2, C, P])
        m.resid = sb("resid", [P, NT, D])
        m.x2T = sb("x2T", [P, C, S])
        m.actT = sb("actT", [P, NF0, S])
        m.scaled = sb("scaled", [P, NT, D])
        ZR = 4
        zeros = sb("zeros", [P, ZR * D])
        zeros_ready = sem("a_zeros_ready")
        zero_filled = sem("a_zero_filled")
        zeroed = sem("a_zeroed")
        w_in = sem("a_w_in")
        wmlp_in = sem("a_wmlp_in")
        rows_in = sem("a_rows_in")
        norm_s = sem("a_first_norm_steps")
        attention_s = sem("a_attention_steps")
        norm2_s = sem("a_second_norm_steps")
        xn_ready = sem("a_xn_ready")
        hT_done = sem("a_hT_done")
        hT_act = sem("a_hT_act")
        hT_dve = sem("a_hT_dve")
        q_done = sem("a_q_done")
        k_done = sem("a_k_done")
        v_done = sem("a_v_done")
        q_ready = sem("a_q_ready")
        k_ready = sem("a_k_ready")
        v_ready = sem("a_v_ready")
        s_done = sem("a_scores_done")
        max_ready = sem("a_max_ready")
        p_ready = sem("a_probs_ready")
        pT_done = sem("a_probsT_done")
        pT_act = sem("a_probsT_act")
        pT_dve = sem("a_probsT_dve")
        o_done = sem("a_attn_done")
        o_ready = sem("a_attn_ready")
        oT_done = sem("a_attnT_done")
        oT_ready = sem("a_attnT_ready")
        r_done = sem("a_resid_done")
        r_ready = sem("a_resid_ready")
        rn_ready = sem("a_resid_norm_ready")
        x2_done = sem("a_x2T_done")
        x2_act = sem("a_x2T_act")
        x2_dve = sem("a_x2T_dve")
        up_done = sem("a_up_done")
        gelu_ready = sem("a_gelu_ready")
        y_done = sem("a_y_done")
        scaled_ready = sem("a_scaled_ready")
        x_ready = sem("a_x_ready")
        bias_added = sem("a_bias_added")
        block = ctx.enter_context(nc.Block())

        def x_tile(b, t):
            return m.x[:, bass.ds(b * (NT * D) + t * D, D)]

        def load_rows(sp, b):
            sp.dma_start(m.gate_rows[:, :, :], mods_dram[0, bass.ds(b, 1), :, :].rearrange("a s d -> (a s) d")
                         .partition_broadcast(P)).then_inc(rows_in, 16)

        @block.sync
        def _(sp):
            for tile, k in ((m.wq0, "Wq"), (m.wk0, "Wk"), (m.wv0, "Wv"), (m.wo0, "Wo")):
                sp.dma_start(tile[:, :, :], I[f"L0_attn_{k}"].rearrange("(c p) n -> p c n", p=P))\
                    .then_inc(w_in, 16)
            for tile, k in ((m.bq0, "bq"), (m.bk0, "bk"), (m.gamma0, "gamma"), (m.beta0, "beta")):
                sp.dma_start(tile[:, :], I[f"L0_attn_{k}"].rearrange("(c p) -> p c", p=P),
                             allow_slow_non_contiguous=True)\
                    .then_inc(w_in, 16)
            sp.dma_start(m.b1_0[:, :], I["L0_attn_b1"].rearrange("(c p) -> p c", p=P),
                         allow_slow_non_contiguous=True).then_inc(w_in, 16)
            sp.dma_start(m.bv0_rows[:, :], I["L0_attn_bv"].partition_broadcast(P)).then_inc(w_in, 16)
            sp.dma_start(m.bo0_rows[:, :], I["L0_attn_bo"].partition_broadcast(P)).then_inc(w_in, 16)
            sp.dma_start(w1[:, :, :], I["L0_attn_W1"].rearrange("(c p) f -> p c f", p=P)).then_inc(wmlp_in, 16)
            sp.dma_start(w2[:, :, :], I["L0_attn_W2"].rearrange("(f p) d -> p f d", p=P)).then_inc(wmlp_in, 16)
            load_rows(sp, 0)
            with sp.Fori(1, B) as b:
                sp.wait_ge(scaled_ready, b * NT)
                sp.wait_ge(bias_added, b)
                load_rows(sp, b)

        @block.gpsimd
        def _(pool):
            pool.memset(m.hT[:, :, :], 0.0).then_inc(zeroed, 1)
            pool.memset(m.kT[:, :, :], 0.0).then_inc(zeroed, 1)
            pool.memset(m.v_ones[:, :, :, :], 1.0).then_inc(zeroed, 1)
            pool.memset(zeros[:, :], 0.0).then_inc(zeros_ready, 1)
            with pool.Fori(0, B) as b:
                pool.wait_ge(xn_ready, b * NT + NT)
                pool.wait_ge(rows_in, b * 16 + 16)
                take_wait(pool, m)
                xb = m.x[:, bass.ds(b * (NT * D), NT * D)].rearrange("p (t d) -> p t d", t=NT)
                pool.tensor_tensor(xb, xb, m.gate_rows[:, 1:2, :].to_broadcast([P, NT, D]), ALU.add)\
                    .then_inc(bias_added, 1)

        @block.scalar
        def _(act):
            act.wait_ge(w_in, 16 * 11)
            act.wait_ge(zeroed, 3)

            def inputs(b):
                act.wait_ge(hT_done, b + 1)
                act.activation(m.hT[:, 0, PAD:PAD + S], bank(m, 0), ACT.Identity,
                               bias=m.mod_cols0[:, 0, 0, bass.ds(b, 1)], scale=m.mod_cols0[:, 1, 0, bass.ds(b, 1)])\
                    .then_inc(hT_act, 1)
                for c in range(C):
                    act.wait_ge(q_done, b * C + c + 1)
                    act.activation(m.qT[:, c, :], bank(m, c), ACT.Identity, bias=m.bq0[:, c:c + 1])\
                        .then_inc(q_ready, 1)

            def attention(b):
                def exps(t):
                    act.wait_ge(max_ready, b * NT + t + 1)
                    if t >= 2:
                        act.wait_ge(pT_done, b * (4 * NT) + 4 * (t - 1))
                    for j in range(4):
                        for i, h in enumerate((j, j + 4)):
                            ins = act.activation(m.probs[:, t % 2, h, :],
                                                 bank(m, 4 * (t % 2) + j)[:, i * 2 * P:(i + 1) * 2 * P],
                                                 ACT.Exp, bias=m.bias_exp[:, t % 2, h:h + 1], scale=SCALE0)
                        ins.then_inc(p_ready, 1)

                def copy_probsT(t):
                    if t >= 2:
                        act.wait_ge(o_done, b * NT + t - 1)
                    for j in (0, 2):
                        act.wait_ge(pT_done, b * (4 * NT) + 4 * t + j + 1)
                        act.activation(m.probsT[:, t % 2, j:8:4, :, :],
                                       bank(m, 4 * (t % 2) + j).rearrange("p (i k q) -> p i k q", i=2, k=2),
                                       ACT.Copy).then_inc(pT_act, 1)

                def copy_attnT(t):
                    act.wait_ge(oT_done, b * NT + t + 1)
                    act.activation(m.attnT[:, t % 2, :, :].rearrange("p c q -> p (c q)"),
                                   bank(m, 4 * (t % 2) + 1)[:, 0:D], ACT.Copy).then_inc(oT_ready, 1)

                exps(0)
                copy_probsT(0)
                exps(1)
                copy_probsT(1)
                copy_attnT(0)
                copy_attnT(1)
                exps(2)
                copy_probsT(2)
                exps(3)
                copy_probsT(3)
                copy_attnT(2)
                copy_attnT(3)

            def mlp(b):
                act.wait_ge(x2_done, b + 1)
                act.activation(m.x2T[:, 0, :], bank(m, 0), ACT.Identity, bias=m.beta0[:, 0:1],
                               scale=m.gamma0[:, 0:1]).then_inc(x2_act, 1)
                for f in range(NF0):
                    act.wait_ge(up_done, b * NF0 + f + 1)
                    act.activation(m.actT[:, f, :], bank(m, 2 + f % 6), ACT.Gelu, bias=m.b1_0[:, f:f + 1])\
                        .then_inc(gelu_ready, 1)

            inputs(0)
            act.wait_ge(zeros_ready, 1)
            for r in range(0, E * CAP, P * ZR):
                act.dma_start(padded_dram[r:r + P * ZR, :].rearrange("(p r) d -> p (r d)", p=P), zeros[:, :])\
                    .then_inc(zero_filled, 16)
            with act.Fori(0, B - 1) as b:
                attention(b)
                inputs(b + 1)
                mlp(b)
            attention(B - 1)
            mlp(B - 1)
            act.wait_ge(zero_filled, 16 * (E * CAP // (P * ZR)))

        @block.vector
        def _(dve):
            dve.wait_ge(w_in, 16 * 11)
            dve.wait_ge(zeroed, 3)
            dve.wait_ge(m.x_first, 32)

            def first_norm(b):
                step = Steps(dve, norm_s, b * LN_STEPS, LN_STEPS)
                emit_layernorm(dve, step, m, [x_tile(b, t) for t in range(NT)], xn_ready)
                step.close()

            def modulate(b):
                dve.wait_ge(hT_done, b + 1)
                dve.tensor_scalar(m.hT[:, 1, PAD:PAD + S], bank(m, 1), m.mod_cols0[:, 1, 1, bass.ds(b, 1)],
                                  m.mod_cols0[:, 0, 1, bass.ds(b, 1)], ALU.mult, ALU.add).then_inc(hT_dve, 1)

            def inputs(b):
                for c in range(C):
                    dve.wait_ge(k_done, b * C + c + 1)
                    dve.tensor_scalar(m.kT[:, c, PAD:PAD + S], bank(m, 2 + c), m.bk0[:, c:c + 1], None, ALU.add)\
                        .then_inc(k_ready, 1)
                for i in range(VBANKS):
                    n = min(2, NT + 1 - 2 * i)
                    dve.wait_ge(v_done, b * VBANKS + i + 1)
                    dve.tensor_tensor(m.v_ones[:, 2 * i:2 * i + n, :, 0:DH0],
                                      bank(m, 4 + i)[:, 0:n * D].rearrange("p (j h d) -> p j h d", j=n, h=H0),
                                      m.bv0_rows[:, :].rearrange("p (j h d) -> p j h d", j=1, h=H0)
                                      .to_broadcast([P, n, H0, DH0]), ALU.add).then_inc(v_ready, 1)

            def attention(b):
                step = Steps(dve, attention_s, b * (2 * NT), 2 * NT)

                def row_max(t):
                    dve.wait_ge(s_done, b * NT + t + 1)
                    if t >= 2:
                        dve.wait_ge(p_ready, b * (4 * NT) + 4 * (t - 1))
                    step(dve.tensor_reduce(m.negmax[:, t % 2, :].rearrange("p (i j) -> p j i", i=2),
                                           m.psum[:, 4 * (t % 2):4 * (t % 2) + 4, :]
                                           .rearrange("p j (i k) -> p j i k", i=2), AX.X, ALU.max, negate=True))
                    step.settle()
                    dve.tensor_scalar(m.bias_exp[:, t % 2, :], m.negmax[:, t % 2, :], SCALE0, None, ALU.mult)\
                        .then_inc(max_ready, 1)

                def copy_probsT(t):
                    if t >= 2:
                        dve.wait_ge(o_done, b * NT + t - 1)
                    for j in (1, 3):
                        dve.wait_ge(pT_done, b * (4 * NT) + 4 * t + j + 1)
                        dve.tensor_copy(m.probsT[:, t % 2, j:8:4, :, :],
                                        bank(m, 4 * (t % 2) + j).rearrange("p (i k q) -> p i k q", i=2, k=2))\
                            .then_inc(pT_dve, 1)

                def normalise(t):
                    dve.wait_ge(o_done, b * NT + t + 1)
                    o = bank(m, 4 * (t % 2))[:, 0:H0 * (DH0 + 1)].rearrange("p (h d) -> p h d", h=H0)
                    step(dve.reciprocal(m.recip[:, t % 2, :], o[:, :, DH0]))
                    step.settle()
                    if t >= 2:
                        dve.wait_ge(oT_done, b * NT + t - 1)
                    dve.tensor_tensor(m.attn[:, t % 2, :].rearrange("p (h d) -> p h d", h=H0), o[:, :, 0:DH0],
                                      m.recip[:, t % 2, :].rearrange("p (h a) -> p h a", a=1)
                                      .to_broadcast([P, H0, DH0]), ALU.mult).then_inc(o_ready, 1)

                def residual(t):
                    dve.wait_ge(r_done, b * NT + t + 1)
                    dve.tensor_tensor(m.resid[:, t, :], bank(m, 4 * (t % 2) + 2)[:, 0:D], m.bo0_rows[:, :], ALU.add)\
                        .then_inc(r_ready, 1)

                row_max(0)
                row_max(1)
                copy_probsT(0)
                normalise(0)
                copy_probsT(1)
                normalise(1)
                residual(0)
                residual(1)
                row_max(2)
                row_max(3)
                copy_probsT(2)
                normalise(2)
                copy_probsT(3)
                normalise(3)
                residual(2)
                residual(3)
                step.close()

            def second_norm(b):
                step = Steps(dve, norm2_s, b * LN_STEPS, LN_STEPS)
                emit_layernorm(dve, step, m, [m.resid[:, t, :] for t in range(NT)], rn_ready,
                               lambda t: dve.wait_ge(r_ready, b * NT + t + 1))
                step.close()

            def mlp_input(b):
                dve.wait_ge(x2_done, b + 1)
                dve.tensor_scalar(m.x2T[:, 1, :], bank(m, 1), m.gamma0[:, 1:2], m.beta0[:, 1:2], ALU.mult, ALU.add)\
                    .then_inc(x2_dve, 1)

            def residual_stream(b):
                dve.wait_ge(rows_in, b * 16 + 16)
                dve.wait_ge(bias_added, b + 1)
                for t in range(NT):
                    dve.wait_ge(y_done, b * NT + t + 1)
                    dve.tensor_tensor(m.scaled[:, t, :], bank(m, (0, 1, 4, 5)[t])[:, 0:D], m.gate_rows[:, 0, :],
                                      ALU.mult).then_inc(scaled_ready, 1)
                    dve.wait_ge(scaled_ready, b * NT + t + 1)
                    dve.tensor_tensor(x_tile(b, t), x_tile(b, t), m.scaled[:, t, :], ALU.add).then_inc(x_ready, 1)

            def turn(b, norm_next):
                attention(b)
                modulate(b + 1)
                second_norm(b)
                inputs(b + 1)
                mlp_input(b)
                if norm_next:
                    first_norm(b + 2)
                residual_stream(b)

            first_norm(0)
            modulate(0)
            first_norm(1)
            inputs(0)
            dve.wait_ge(m.x_rest, 16 * (B - 2))
            with dve.Fori(0, B - 2) as b:
                turn(b, True)
            turn(B - 2, False)
            attention(B - 1)
            second_norm(B - 1)
            mlp_input(B - 1)
            residual_stream(B - 1)

        @block.tensor
        def _(pe):
            pe.wait_ge(w_in, 16 * 11)

            def inputs(b, first=False):
                emit_transpose_tiles(pe, m, m.xn, (0, 1), lambda t: pe.wait_ge(xn_ready, b * NT + t + 1), hT_done)
                pe.wait_ge(hT_act, b + 1)
                pe.wait_ge(hT_dve, b + 1)
                for w, at, done in ((m.wq0, 0, q_done), (m.wk0, 2, k_done)):
                    if at and not first:
                        pe.wait_ge(r_ready, b * NT)
                    for o in range(C):
                        for c in range(C):
                            mm = pe.matmul(bank(m, at + o), w[:, c, o * P:(o + 1) * P], m.hT[:, c, PAD:PAD + S],
                                           start=(c == 0), stop=(c == C - 1))
                        mm.then_inc(done, 1)
                for j in range(NT + 1):
                    for c in range(C):
                        mm = pe.matmul(bank(m, 4 + j // 2)[:, (j % 2) * D:(j % 2 + 1) * D],
                                       m.hT[:, c, j * P:(j + 1) * P], m.wv0[:, c, :], start=(c == 0), stop=(c == C - 1))
                    if j % 2 or j == NT:
                        mm.then_inc(v_done, 1)

            def attention(b):
                def scores(t):
                    if t == 0:
                        pe.wait_ge(q_ready, b * C + C)
                        pe.wait_ge(k_ready, b * C + C)
                    elif t == 1:
                        pe.wait_ge(v_ready, b * VBANKS + VBANKS)
                    else:
                        pe.wait_ge(r_ready, b * NT + t - 1)
                    variant = 0 if t == 0 else 2 if t == NT - 1 else 1
                    for j in range(4):
                        pe.matmul(bank(m, 4 * (t % 2) + j), m.ident_bf[:, :],
                                  m.band_mask[:, variant, :, :].rearrange("p r k -> p (r k)"), start=True, stop=False,
                                  skip_group_check=True)
                    for i in range(2):
                        for j in range(4):
                            mm = pe.matmul(bank(m, 4 * (t % 2) + j)[:, i * 2 * P:(i + 1) * 2 * P],
                                           m.qT[32 * j:32 * j + DH0, i, t * P:(t + 1) * P],
                                           m.kT[32 * j:32 * j + DH0, i, t * P:(t + 2) * P], start=False, stop=True,
                                           skip_group_check=True)
                    mm.then_inc(s_done, 1)

                def transpose_probs(t):
                    for j in range(4):
                        pe.wait_ge(p_ready, b * (4 * NT) + 4 * t + j + 1)
                        for i in range(2):
                            for k in range(2):
                                mm = pe.transpose(bank(m, 4 * (t % 2) + j)[:, (2 * i + k) * P:(2 * i + k + 1) * P],
                                                  m.probs[:, t % 2, j + 4 * i, k * P:(k + 1) * P], m.ident[:, :])
                        mm.then_inc(pT_done, 1)

                def weigh_values(t):
                    pe.wait_ge(pT_act, b * (2 * NT) + 2 * t + 2)
                    pe.wait_ge(pT_dve, b * (2 * NT) + 2 * t + 2)
                    for h in range(H0):
                        for k in range(2):
                            mm = pe.matmul(bank(m, 4 * (t % 2))[:, h * (DH0 + 1):(h + 1) * (DH0 + 1)],
                                           m.probsT[:, t % 2, h, k, :], m.v_ones[:, t + k, h, :],
                                           start=(k == 0), stop=(k == 1))
                    mm.then_inc(o_done, 1)

                def transpose_attn(t):
                    pe.wait_ge(o_ready, b * NT + t + 1)
                    for c in range(C):
                        mm = pe.transpose(bank(m, 4 * (t % 2) + 1)[:, c * P:(c + 1) * P],
                                          m.attn[:, t % 2, c * P:(c + 1) * P], m.ident[:, :])
                    mm.then_inc(oT_done, 1)

                def project(t):
                    pe.wait_ge(oT_ready, b * NT + t + 1)
                    out = bank(m, 4 * (t % 2) + 2)
                    for c in range(C):
                        pe.matmul(out[:, 0:D], m.attnT[:, t % 2, c, :], m.wo0[:, c, :], start=(c == 0), stop=False,
                                  skip_group_check=True)
                    for c in range(C):
                        mm = pe.matmul(out[:, c * P:(c + 1) * P], m.hT[:, c, PAD + t * P:PAD + (t + 1) * P],
                                       m.ident[:, :], start=False, stop=True, skip_group_check=True)
                    mm.then_inc(r_done, 1)

                scores(0)
                scores(1)
                transpose_probs(0)
                weigh_values(0)
                transpose_probs(1)
                transpose_attn(0)
                weigh_values(1)
                project(0)
                transpose_attn(1)
                scores(2)
                project(1)
                scores(3)
                transpose_probs(2)
                weigh_values(2)
                transpose_probs(3)
                transpose_attn(2)
                weigh_values(3)
                project(2)
                transpose_attn(3)
                project(3)

            def mlp(b, latest):
                pe.wait_ge(q_ready, latest * C + C)
                emit_transpose_tiles(pe, m, m.xn, (0, 1), lambda t: pe.wait_ge(rn_ready, b * NT + t + 1), x2_done)
                pe.wait_ge(x2_act, b + 1)
                pe.wait_ge(x2_dve, b + 1)
                pe.wait_ge(wmlp_in, 32)
                pe.wait_ge(r_ready, b * NT + NT)
                pe.wait_ge(k_ready, latest * C + C)
                pe.wait_ge(v_ready, latest * VBANKS + VBANKS)
                for f in range(NF0):
                    if f >= 6:
                        pe.wait_ge(gelu_ready, b * NF0 + f - 5)
                    for c in range(C):
                        mm = pe.matmul(bank(m, 2 + f % 6), w1[:, c, f * P:(f + 1) * P], m.x2T[:, c, :],
                                       start=(c == 0), stop=(c == C - 1))
                    mm.then_inc(up_done, 1)
                for t in range(NT):
                    out = bank(m, (0, 1, 4, 5)[t])
                    for f in range(NF0):
                        if t == 0 or f == NF0 - 1:
                            pe.wait_ge(gelu_ready, b * NF0 + f + 1)
                        pe.matmul(out[:, 0:D], m.actT[:, f, t * P:(t + 1) * P], w2[:, f, :], start=(f == 0),
                                  stop=False, skip_group_check=True)
                    for c in range(C):
                        mm = pe.matmul(out[:, c * P:(c + 1) * P], m.x2T[:, c, t * P:(t + 1) * P], m.ident[:, :],
                                       start=False, stop=True, skip_group_check=True)
                    mm.then_inc(y_done, 1)
                pe.wait_ge(scaled_ready, b * NT + NT)

            inputs(0, first=True)
            with pe.Fori(0, B - 1) as b:
                attention(b)
                inputs(b + 1)
                mlp(b, b + 1)
            attention(B - 1)
            mlp(B - 1, B - 1)

def routed_experts_block(nc, m, I, mods_dram):
    NG = ROWS_MOE0 // S
    NTL = ROWS_MOE0 // P
    U = 2 * NG
    ctx = ExitStack()
    with ctx:
        def sem(name):
            return ctx.enter_context(nc.semaphore(name))

        sb = tile_maker(nc, ctx)
        m.h0T = sb("h0T", [P, C, ROWS_MOE0])
        w1 = sb("w1_e", [P, 2, C, F0])
        w2 = sb("w2_e", [P, 2, NF0, D])
        actT = sb("actT_e", [P, 2, NF0, S])
        acc = sb("acc", [P, NTL, D])
        idx = sb("idx", [P, NTL, TOPK], I32)
        idx_f = sb("idx_f", [P, NTL, TOPK])
        wts = sb("wts", [P, NTL, TOPK])
        expert_i = sb("expert_i", [P, E], I32)
        expert_f = sb("expert_f", [P, E])
        hit = sb("hit", [P, TOPK, E, NTL])
        wt = sb("wt", [P, E * NTL])
        rows2 = sb("rows2", [P, NG, 4, D])
        route_in = sem("b_route_in")
        rows_in = sem("b_rows_in")
        rows2_in = sem("b_rows2_in")
        w_in = [sem(f"b_w_in{u}") for u in range(2)]
        iota_ready = sem("b_iota_ready")
        dve_s = sem("b_dve_steps")
        xn_ready = sem("b_xn_ready")
        hT_done = sem("b_hT_done")
        hT_act = sem("b_hT_act")
        hT_dve = sem("b_hT_dve")
        up_done = sem("b_up_done")
        gelu_ready = sem("b_gelu_ready")
        y_done = sem("b_y_done")
        acc_ready = sem("b_acc_ready")
        bias_added = sem("b_bias_added")
        x_ready = sem("b_x_ready")
        block = ctx.enter_context(nc.Block())
        STEPS_BEFORE = 2 * LN_STEPS + 7

        def load_rows(sp, b):
            sp.dma_start(m.gate_rows[:, :, :], mods_dram[0, bass.ds(b, 1), :, :].rearrange("a s d -> (a s) d")
                         .partition_broadcast(P)).then_inc(rows_in, 16)

        @block.sync
        def _(sp):
            def load_expert(e, u):
                sp.dma_start(w1[:, u, :, :], I["L0_ffn_w1"][bass.ds(e, 1), :, :]
                             .rearrange("e (c p) f -> p (e c) f", p=P)).then_inc(w_in[u], 16)
                sp.dma_start(w2[:, u, :, :], I["L0_ffn_w2"][bass.ds(e, 1), :, :]
                             .rearrange("e (f p) d -> p (e f) d", p=P)).then_inc(w_in[u], 16)

            sp.dma_start(idx[:, :, :], I["L0_ffn_expert_indices"].rearrange("(t p) k -> p t k", p=P))\
                .then_inc(route_in, 16)
            sp.dma_start(wts[:, :, :], I["L0_ffn_expert_weights"].rearrange("(t p) k -> p t k", p=P))\
                .then_inc(route_in, 16)
            load_expert(0, 0)
            load_expert(1, 1)
            for g in range(NG):
                sp.dma_start(rows2[:, g, :, :], mods_dram[0, g, :, :].partition_broadcast(P)).then_inc(rows2_in, 16)
            for tile, name in ((m.wq1, "L1_attn_wq"), (m.wo1, "L1_attn_wo"), (m.qw, "L1_ffn_qw"), (m.kw, "L1_ffn_kw"),
                               (m.vw, "L1_ffn_vw"), (m.ow, "L1_ffn_ow"), (m.gate_w, "L1_ffn_gate_w")):
                sp.dma_start(tile[:, :, :], I[name].rearrange("(c p) n -> p c n", p=P)).then_inc(m.mixer_w_in, 16)
            for i, name in enumerate(("L1_attn_wk", "L1_attn_wv")):
                sp.dma_start(m.wkv1[:, :, i * D:(i + 1) * D], I[name].rearrange("(c p) n -> p c n", p=P))\
                    .then_inc(m.mixer_w_in, 16)
            sp.dma_start(m.qb[:, :], I["L1_ffn_qb"].rearrange("(c p) -> p c", p=P), allow_slow_non_contiguous=True)\
                .then_inc(m.mixer_w_in, 16)
            sp.dma_start(m.kb[:, :], I["L1_ffn_kb"].rearrange("(p a) -> p a", a=1)).then_inc(m.mixer_w_in, 16)
            for tile, name in ((m.vb, "L1_ffn_vb"), (m.ob, "L1_ffn_ob"), (m.n1w, "L1_ffn_norm1_w")):
                sp.dma_start(tile[:, :], I[name].partition_broadcast(P)).then_inc(m.mixer_w_in, 16)
            load_rows(sp, 0)
            with sp.Fori(1, B) as b:
                sp.wait_ge(bias_added, b)
                load_rows(sp, b)
            with sp.Fori(1, E // 2) as i:
                for u in range(2):
                    sp.wait_ge(y_done, (i - 1) * (U * NT) + (u + 1) * NG * NT)
                    load_expert(2 * i + u, u)

        @block.gpsimd
        def _(pool):
            pool.iota(expert_i[:, :], [[1, E]], base=0, channel_multiplier=0).then_inc(iota_ready, 1)
            pool.wait_ge(xn_ready, NG * NT)
            with pool.Fori(0, B) as b:
                pool.wait_ge(rows_in, b * 16 + 16)
                take_wait(pool, m)
                xb = m.x[:, bass.ds(b * (NT * D), NT * D)].rearrange("p (t d) -> p t d", t=NT)
                pool.tensor_tensor(xb, xb, m.gate_rows[:, 3:4, :].to_broadcast([P, NT, D]), ALU.add)\
                    .then_inc(bias_added, 1)

        @block.scalar
        def _(act):
            for g in range(NG):
                act.wait_ge(hT_done, g + 1)
                act.activation(m.h0T[:, 0, g * S:(g + 1) * S], bank(m, 2 * g), ACT.Identity,
                               bias=m.mod_cols0[:, 2, 0, g:g + 1], scale=m.mod_cols0[:, 3, 0, g:g + 1])\
                    .then_inc(hT_act, 1)
            with act.Fori(0, E // 2) as i:
                for u in range(U):
                    if u >= 2:
                        act.wait_ge(y_done, i * (U * NT) + (u - 1) * NT)
                    for f in range(NF0):
                        act.wait_ge(up_done, i * (U * NF0) + u * NF0 + f + 1)
                        act.activation(actT[:, u % 2, f, :], bank(m, f % 4), ACT.Gelu).then_inc(gelu_ready, 1)

        @block.vector
        def _(dve):
            step = Steps(dve, dve_s, 0, STEPS_BEFORE)
            for g in range(NG):
                emit_layernorm(dve, step, m, [m.x[:, (g * NT + t) * D:(g * NT + t + 1) * D] for t in range(NT)],
                               xn_ready, None, (lambda: dve.wait_ge(hT_done, 1)) if g else None)
            for g in range(NG):
                dve.wait_ge(hT_done, g + 1)
                dve.tensor_scalar(m.h0T[:, 1, g * S:(g + 1) * S], bank(m, 2 * g + 1), m.mod_cols0[:, 3, 1, g:g + 1],
                                  m.mod_cols0[:, 2, 1, g:g + 1], ALU.mult, ALU.add).then_inc(hT_dve, 1)
            step(dve.memset(acc[:, :, :], 0.0))
            dve.wait_ge(route_in, 32)
            dve.wait_ge(iota_ready, 1)
            step(dve.tensor_copy(idx_f[:, :, :], idx[:, :, :]))
            step(dve.tensor_copy(expert_f[:, :], expert_i[:, :]))
            step.settle()
            for k in range(TOPK):
                step(dve.tensor_tensor(hit[:, k, :, :],
                                       expert_f[:, :].rearrange("p (e t) -> p e t", t=1).to_broadcast([P, E, NTL]),
                                       idx_f[:, :, k].rearrange("p (e t) -> p e t", e=1).to_broadcast([P, E, NTL]),
                                       ALU.is_equal))
            step.settle()
            for k in range(TOPK):
                step(dve.tensor_tensor(hit[:, k, :, :], hit[:, k, :, :],
                                       wts[:, :, k].rearrange("p (e t) -> p e t", e=1).to_broadcast([P, E, NTL]),
                                       ALU.mult))
            step.settle()
            dve.tensor_tensor(wt[:, :], hit[:, 0, :, :].rearrange("p e t -> p (e t)"),
                              hit[:, 1, :, :].rearrange("p e t -> p (e t)"), ALU.add).then_inc(acc_ready, 1)
            dve.wait_ge(acc_ready, 1)
            with dve.Fori(0, E // 2) as i:
                for u in range(U):
                    for t in range(NT):
                        tile = (u % NG) * NT + t
                        dve.wait_ge(y_done, i * (U * NT) + u * NT + t + 1)
                        dve.scalar_tensor_tensor(out=acc[:, tile, :], in0=bank(m, 4 + t)[:, 0:D],
                                                 scalar=wt[:, bass.ds((2 * i + u // NG) * NTL + tile, 1)],
                                                 in1=acc[:, tile, :], op0=ALU.mult, op1=ALU.add)\
                            .then_inc(acc_ready, 1)
            dve.wait_ge(acc_ready, 1 + (E // 2) * U * NT)
            dve.wait_ge(rows2_in, 16 * NG)
            for g in range(NG):
                a = acc[:, g * NT:(g + 1) * NT, :]
                step(dve.tensor_tensor(a, a, rows2[:, g, 2:3, :].to_broadcast([P, NT, D]), ALU.mult))
            step.settle()
            dve.wait_ge(bias_added, B)
            dve.tensor_tensor(m.x[:, 0:NTL * D], m.x[:, 0:NTL * D], acc[:, :, :].rearrange("p t d -> p (t d)"),
                              ALU.add).then_inc(x_ready, 1)

        @block.tensor
        def _(pe):
            for g in range(NG):
                emit_transpose_tiles(pe, m, m.xn, (2 * g, 2 * g + 1),
                                     lambda t: pe.wait_ge(xn_ready, g * NT + t + 1), hT_done)
            pe.wait_ge(hT_act, NG)
            pe.wait_ge(hT_dve, NG)
            with pe.Fori(0, E // 2) as i:
                def up(u):
                    if u % NG == 0:
                        pe.wait_ge(w_in[u // NG], i * 32 + 32)
                    for f in range(NF0):
                        if u or f >= 4:
                            pe.wait_ge(gelu_ready, i * (U * NF0) + u * NF0 + f - 3)
                        for c in range(C):
                            mm = pe.matmul(bank(m, f % 4), w1[:, u // NG, c, f * P:(f + 1) * P],
                                           m.h0T[:, c, (u % NG) * S:(u % NG + 1) * S],
                                           start=(c == 0), stop=(c == C - 1))
                        mm.then_inc(up_done, 1)

                def down(u):
                    pe.wait_ge(gelu_ready, i * (U * NF0) + (u + 1) * NF0)
                    for t in range(NT):
                        if u:
                            pe.wait_ge(acc_ready, i * (U * NT) + (u - 1) * NT + t + 2)
                        for f in range(NF0):
                            mm = pe.matmul(bank(m, 4 + t)[:, 0:D], actT[:, u % 2, f, t * P:(t + 1) * P],
                                           w2[:, u // NG, f, :], start=(f == 0), stop=(f == NF0 - 1))
                        mm.then_inc(y_done, 1)

                up(0)
                for u in range(1, U):
                    up(u)
                    down(u - 1)
                down(U - 1)
                pe.wait_ge(acc_ready, i * (U * NT) + U * NT + 1)


def mixer_block(nc, m, I, mods_dram, qk_dram, padded_dram, src_dram):
    ctx = ExitStack()
    with ctx:
        def sem(name):
            return ctx.enter_context(nc.semaphore("c_" + name))

        sb = tile_maker(nc, ctx)
        wq, wkv, wo, qw, kw, vw, ow, gate_w = m.wq1, m.wkv1, m.wo1, m.qw, m.kw, m.vw, m.ow, m.gate_w
        qb, kb, vb, ob, n1w = m.qb, m.kb, m.vb, m.ob, m.n1w
        block_mask = sb("block_mask", [P, HPC1, DH1])
        head_mask = sb("head_mask", [P, HPC1])
        before = sb("before", [P, P], BF16)
        ones_bf = sb("ones_bf", [P, P], BF16)
        expert_i = sb("expert_i1", [P, E], I32)
        expert_f = sb("expert_f1", [P, E])
        first_slot = sb("first_slot", [P, E])
        hT = sb("hT1", [P, C, S])
        xn = sb("xn1", [P, NT, D])
        q_exp = sb("q_exp", [P, C, S])
        q_relu = sb("q_relu", [P, C, S])
        k_exp = sb("k_exp", [P, NT, D])
        k_relu = sb("k_relu", [P, NT, D])
        v_one = sb("v_one", [P, NT, C, P + 1])
        kv_bd = sb("kv_bd", [P, C, P + HPC1])
        den = sb("den1", [P, NT, H1])
        o1 = sb("o1", [P, NT, D])
        o1T = sb("o1T", [P, 2, C, P])
        scaled = sb("scaled1", [P, NT, D])
        h2T = sb("h2T", [P, C, S])
        q_part = sb("q_part", [P, 3, C, S], BF16)
        k_part = sb("k_part", [DKV, 3, S], BF16)
        q_rest = q_relu
        q_stack = sb("q_stack", [K_FULL, HQ, S], BF16)
        k_stack = sb("k_stack", [K_FULL, HKV, S], BF16)
        v_tile = sb("v_tile", [P, NT, HKV, VW])
        negmax = sb("negmax1", [P, NT, HQ])
        max_rest = sb("max_rest", [P, NT, HQ])
        max_part = sb("max_part", [P, HKV, NT, REP, 3], BF16)
        maxT = sb("maxT", [3 * REP, HKV, S], BF16)
        pT = sb("pT", [P, 4, 2, S])
        oraw = sb("oraw", [P, HKV, S])
        k_rest = oraw[0:DKV, HKV - 1, :]
        osum = sb("osum", [P, NT, HQ])
        resid = sb("resid1", [P, NT, D])
        src = sb("src", [P, NT, D])
        probs = sb("router_probs", [P, NT, E])
        top = sb("top", [P, NT, E])
        top_i = sb("top_i", [P, NT, E], U32)
        sel = sb("sel", [P, NT, TOPK])
        wsum = sb("wsum", [P, NT, 1])
        chosen = sb("chosen", [P, TOPK, NT, E])
        load = sb("load", [P, NT, E], BF16)
        load_before = sb("load_before", [P, NT + 1, E], BF16)
        slots_e = sb("slots_e", [P, NT, E])
        over = sb("over", [P, NT, E])
        slot_k = sb("slot_k", [P, NT, TOPK])
        valid = sb("valid", [P, NT, TOPK])
        wk = sb("wk", [P, NT, TOPK])
        scatter_idx = sb("scatter_idx", [P, NT, TOPK], U32)

        consts = sem("consts")
        masks = sem("masks")
        rows_in = sem("rows_in")
        norm_s = sem("first_norm_steps")
        linear_s = sem("linear_steps")
        inputs_s = sem("inputs_steps")
        grouped_s = sem("grouped_steps")
        src_s = sem("src_steps")
        route_s = sem("route_steps")
        xn_ready = sem("xn_ready")
        hT_done = sem("hT_done")
        hT_act = sem("hT_act")
        hT_dve = sem("hT_dve")
        q_done = sem("q_done")
        kv_done = sem("kv_done")
        q_min = sem("q_min_ready")
        k_min = sem("k_min_ready")
        q_act = sem("q_act")
        k_act = sem("k_act")
        qf_ready = sem("qf_ready")
        kf_ready = sem("kf_ready")
        gram_done = sem("gram_done")
        kvbd_ready = sem("kvbd_ready")
        n_done = sem("numer_done")
        o1_ready = sem("o1_ready")
        o1T_done = sem("o1T_done")
        o1T_ready = sem("o1T_ready")
        p1_done = sem("proj1_done")
        bias_added = sem("bias_added")
        scaled_ready = sem("scaled_ready")
        x_ready = sem("x_ready")
        xn2_ready = sem("xn2_ready")
        h2_done = sem("h2_done")
        h2_act = sem("h2_act")
        h2_dve = sem("h2_dve")
        qk_done = sem("qk_done")
        v_done = sem("v_done")
        part0 = sem("part0_ready")
        rest = sem("rest_ready")
        part1 = sem("part1_ready")
        part2 = sem("part2_ready")
        v_ready = sem("v_ready")
        parts_out = sem("parts_out")
        stack_in = sem("stack_in")
        s_done = sem("max_scores_done")
        max_read = sem("max_read")
        maxp_ready = sem("max_parts_ready")
        maxT_done = sem("maxT_done")
        maxT_ready = sem("maxT_ready")
        max_in = [sem(f"max_rows_in{g}") for g in range(HKV)]
        sT_done = sem("scoresT_done")
        pT_ready = sem("probsT_ready")
        pv_done = sem("pv_done")
        oraw_ready = sem("oraw_ready")
        ot_done = sem("ot_done")
        o2_ready = sem("o2_ready")
        o2T_done = sem("o2T_done")
        o2T_ready = sem("o2T_ready")
        r_done = sem("resid_done")
        r_ready = sem("resid_ready")
        src_ready = sem("src_ready")
        srcT_done = sem("srcT_done")
        srcT_ready = sem("srcT_ready")
        logits_done = sem("logits_done")
        lexp_ready = sem("logits_exp_ready")
        load_ready = sem("load_ready")
        rank_done = sem("rank_done")
        sidx_ready = sem("scatter_idx_ready")
        scattered = sem("scattered")
        src_out = sem("src_out")
        src_free = sem("src_free")
        ROUTER_STEPS = 29
        GROUPED_STEPS = 3 * HKV + NT
        CHOOSE_STEPS = 6 + 2 * NT + 5
        MAX_AHEAD = 32
        MAX_AT = (3, 11, 19)
        NW = 14
        block = ctx.enter_context(nc.Block())

        def x_tile(b, t):
            return m.x[:, bass.ds(b * (NT * D) + t * D, D)]

        def load_rows(sp, b):
            sp.dma_start(m.gate_rows[:, :, :], mods_dram[1, bass.ds(b, 1), :, :].rearrange("a s d -> (a s) d")
                         .partition_broadcast(P)).then_inc(rows_in, 16)

        @block.sync
        def _(sp):
            load_rows(sp, 0)

            def parts(b):
                sp.wait_ge(part2, b * (C + 1) + C + 1)
                for j in range(3):
                    sp.dma_start(qk_dram[j, 0:D, :].rearrange("(c p) n -> p c n", p=P), q_part[:, j, :, :])\
                        .then_inc(parts_out, 16)
                    sp.dma_start(qk_dram[j, D:D + DKV, :], k_part[:, j, :]).then_inc(parts_out, 16)
                sp.wait_ge(parts_out, b * 96 + 96)
                for s in range(NSLOT):
                    sp.dma_start(q_stack[s * DHQ:(s + 1) * DHQ, :, :],
                                 qk_dram[Q_PARTS[s], 0:D, :].rearrange("(h d) n -> d h n", d=DHQ))\
                        .then_inc(stack_in, 16)
                    sp.dma_start(k_stack[s * DHQ:(s + 1) * DHQ, :, :],
                                 qk_dram[K_PARTS[s], D:D + DKV, :].rearrange("(h d) n -> d h n", d=DHQ))\
                        .then_inc(stack_in, 16)

            def max_rows(b):
                for g in range(HKV):
                    sp.wait_ge(maxT_ready, b * HKV + g + 1)
                    for h in range(REP):
                        sp.dma_start(q_stack[K_SCORE:K_FULL, REP * g + h, :], maxT[3 * h:3 * h + 3, g, :])\
                            .then_inc(max_in[g], 16)

            def store_src(b):
                sp.wait_ge(src_ready, b * NT + NT)
                sp.dma_start(src_dram[bass.ds(b * S, S), :].rearrange("(t p) d -> p t d", p=P), src[:, :, :])\
                    .then_inc(src_out, 16)

            def next_rows(b):
                sp.wait_ge(scaled_ready, b * NT)
                take_wait(sp, m)
                sp.wait_ge(bias_added, b)
                load_rows(sp, b)

            next_rows(1)
            parts(0)
            with sp.Fori(1, B - 1) as b:
                next_rows(b + 1)
                max_rows(b - 1)
                parts(b)
                store_src(b - 1)
            max_rows(B - 2)
            parts(B - 1)
            store_src(B - 2)
            max_rows(B - 1)
            store_src(B - 1)

        @block.gpsimd
        def _(pool):
            pool.memset(head_mask[:, :], 1.0).then_inc(masks, 1)
            pool.memset(block_mask[:, :, :], 1.0).then_inc(masks, 1)
            pool.memset(before[:, :], 1.0).then_inc(masks, 1)
            pool.memset(ones_bf[:, :], 1.0).then_inc(consts, 1)
            pool.memset(v_one[:, :, :, :], 1.0).then_inc(consts, 1)
            pool.memset(v_tile[:, :, :, :], 0.0).then_inc(masks, 1)
            pool.memset(load_before[:, :, :], 0.0).then_inc(consts, 1)
            pool.iota(expert_i[:, :], [[1, E]], base=0, channel_multiplier=0).then_inc(consts, 1)
            pool.wait_ge(masks, 4)
            pool.memset(v_tile[:, :, :, DHQ:DHQ + 1], 1.0).then_inc(consts, 1)
            pool.affine_select(out=head_mask[:, :], in_=head_mask[:, :], compare_op=ALU.is_ge, fill=0.0, base=0,
                               pattern=[[-DH1, HPC1]], channel_multiplier=1).then_inc(masks, 1)
            pool.affine_select(out=block_mask[:, :, :], in_=block_mask[:, :, :], compare_op=ALU.is_ge, fill=0.0,
                               base=0, pattern=[[-DH1, HPC1], [0, DH1]], channel_multiplier=1).then_inc(masks, 1)
            pool.affine_select(out=before[:, :], in_=before[:, :], compare_op=ALU.is_gt, fill=0.0, base=0,
                               pattern=[[1, P]], channel_multiplier=-1).then_inc(consts, 1)
            pool.wait_ge(masks, 6)
            pool.affine_select(out=head_mask[:, :], in_=head_mask[:, :], compare_op=ALU.is_ge, fill=0.0,
                               base=DH1 - 1, pattern=[[DH1, HPC1]], channel_multiplier=-1).then_inc(consts, 1)
            pool.affine_select(out=block_mask[:, :, :], in_=block_mask[:, :, :], compare_op=ALU.is_ge, fill=0.0,
                               base=DH1 - 1, pattern=[[DH1, HPC1], [0, DH1]], channel_multiplier=-1)\
                .then_inc(consts, 1)

            def add_bias(b):
                pool.wait_ge(xn_ready, b * NT + NT)
                pool.wait_ge(rows_in, b * 16 + 16)
                take_wait(pool, m)
                xb = m.x[:, bass.ds(b * (NT * D), NT * D)].rearrange("p (t d) -> p t d", t=NT)
                pool.tensor_tensor(xb, xb, m.gate_rows[:, 1:2, :].to_broadcast([P, NT, D]), ALU.add)\
                    .then_inc(bias_added, 1)

            def scatter(b):
                pool.wait_ge(sidx_ready, b + 1)
                take_wait(pool, m)
                for t in range(NT):
                    for k in range(TOPK):
                        pool.indirect_dma_start(padded_dram, bass.IndirectOffsetOnAxis(ap=scatter_idx[:, t, k:k + 1], axis=0),
                                                src[:, t, :], None, bounds_check=E * CAP - 1, oob_is_err=False)\
                            .then_inc(scattered, 16)
                pool.wait_ge(scattered, (b + 1) * (NT * TOPK * 16))
                take_wait(pool, m)
                pool.wait_ge(src_out, (b + 1) * 16)
                pool.sem_inc(src_free, 1)

            def add_branch(b):
                pool.wait_ge(scaled_ready, b * NT + NT)
                take_wait(pool, m)
                xb = m.x[:, bass.ds(b * (NT * D), NT * D)].rearrange("p (t d) -> p t d", t=NT)
                pool.tensor_tensor(xb, xb, scaled[:, :, :], ALU.add).then_inc(x_ready, 1)

            add_bias(0)
            add_branch(0)
            add_bias(1)
            add_branch(1)
            add_bias(2)
            add_branch(2)
            with pool.Fori(2, B - 1) as b:
                add_bias(b + 1)
                scatter(b - 2)
                add_branch(b + 1)
            scatter(B - 3)
            scatter(B - 2)
            scatter(B - 1)

        @block.scalar
        def _(act):
            act.wait_ge(m.mixer_w_in, 16 * NW)
            act.wait_ge(consts, 9)

            def linear_attention(b, routed=None):
                act.wait_ge(hT_done, b + 1)
                act.activation(hT[:, 0, :], bank(m, 6), ACT.Identity, bias=m.mod_cols1[:, 0, 0, bass.ds(b, 1)],
                               scale=m.mod_cols1[:, 1, 0, bass.ds(b, 1)]).then_inc(hT_act, 1)
                for c in range(C):
                    act.wait_ge(q_min, b * C + c + 1)
                    act.activation(q_exp[:, c, :], q_exp[:, c, :], ACT.Exp).then_inc(q_act, 1)
                    act.activation(q_relu[:, c, :], bank(m, 4 + c), ACT.Relu).then_inc(q_act, 1)
                for t in range(NT):
                    act.wait_ge(k_min, b * NT + t + 1)
                    act.activation(k_exp[:, t, :], k_exp[:, t, :], ACT.Exp).then_inc(k_act, 1)
                    act.activation(k_relu[:, t, :], bank(m, t)[:, 0:D], ACT.Relu).then_inc(k_act, 1)
                    act.activation(v_one[:, t, :, 0:P], bank(m, t)[:, D:2 * D].rearrange("p (c n) -> p c n", c=C),
                                   ACT.Copy).then_inc(k_act, 1)
                if routed is not None:
                    route(routed)
                for t in range(NT):
                    act.wait_ge(o1T_done, b * NT + t + 1)
                    if t >= 2:
                        act.wait_ge(p1_done, b * NT + t - 1)
                    act.activation(o1T[:, t % 2, :, :].rearrange("p c n -> p (c n)"), bank(m, 6 + t % 2)[:, 0:D],
                                   ACT.Copy).then_inc(o1T_ready, 1)

            def grouped_inputs(b):
                act.wait_ge(h2_done, b + 1)
                act.activation(h2T[:, 0, :], bank(m, 4), ACT.Identity, bias=m.mod_cols1[:, 2, 0, bass.ds(b, 1)],
                               scale=m.mod_cols1[:, 3, 0, bass.ds(b, 1)]).then_inc(h2_act, 1)
                for i in range(C + 1):
                    act.wait_ge(qk_done, b * (C + 1) + i + 1)
                    if i < C:
                        act.activation(q_part[:, 0, i, :], bank(m, i), ACT.Identity, bias=qb[:, i:i + 1])\
                            .then_inc(part0, 1)
                    else:
                        act.activation(k_part[:, 0, :], bank(m, 2)[0:DKV, :], ACT.Identity, bias=kb[:, 0:1])\
                            .then_inc(part0, 1)
                for i in range(C + 1):
                    act.wait_ge(rest, b * (C + 1) + i + 1)
                    if i < C:
                        act.activation(q_part[:, 1, i, :], q_rest[:, i, :], ACT.Copy).then_inc(part1, 1)
                    else:
                        act.activation(k_part[:, 1, :], k_rest, ACT.Copy).then_inc(part1, 1)

            def grouped_attention(b):
                def copy_max(g):
                    act.wait_ge(maxT_done, b * HKV + g + 1)
                    act.activation(maxT[:, g, :], bank(m, 6 + g % 2).bitcast(BF16)[0:3 * REP, 0:S], ACT.Copy)\
                        .then_inc(maxT_ready, 1)

                def copy_weighed(g):
                    act.wait_ge(pv_done, b * 32 + 8 * (g + 1))
                    act.activation(oraw[:, g, :], bank(m, 6 + g % 2), ACT.Copy).then_inc(oraw_ready, 1)

                copy_max(0)
                for u in range(32):
                    act.wait_ge(sT_done, b * 32 + u + 1)
                    if u >= 4:
                        act.wait_ge(pv_done, b * 32 + u - 3)
                    act.activation(pT[:, u % 4, :, :], m.psum[:, 2 + 2 * (u % 2):4 + 2 * (u % 2), :], ACT.Exp,
                                   scale=float(DHQ) ** -0.5).then_inc(pT_ready, 1)
                    if u > 8 and u % 8 == 1:
                        copy_weighed(u // 8 - 1)
                    if u in MAX_AT:
                        copy_max(1 + MAX_AT.index(u))
                copy_weighed(HKV - 1)
                for t in range(NT):
                    act.wait_ge(o2T_done, b * NT + t + 1)
                    if t >= 2:
                        act.wait_ge(r_done, b * NT + t - 1)
                    act.activation(o1T[:, t % 2, :, :].rearrange("p c n -> p (c n)"), bank(m, 4 + t % 2)[:, 0:D],
                                   ACT.Copy).then_inc(o2T_ready, 1)

            def route(b):
                act.wait_ge(srcT_done, b + 1)
                for c in range(C):
                    act.activation(oraw[:, c, :], bank(m, 6 + c), ACT.Copy).then_inc(srcT_ready, 1)
                act.wait_ge(logits_done, b + 1)
                act.activation(probs[:, :, :].rearrange("p t e -> p (t e)"), bank(m, 5)[:, 0:NT * E], ACT.Exp,
                               scale=-1.0).then_inc(lexp_ready, 1)

            linear_attention(0)
            grouped_inputs(0)
            linear_attention(1)
            with act.Fori(1, B - 1) as b:
                grouped_attention(b - 1)
                grouped_inputs(b)
                linear_attention(b + 1, routed=b - 1)
            grouped_attention(B - 2)
            grouped_inputs(B - 1)
            route(B - 2)
            grouped_attention(B - 1)
            route(B - 1)

        @block.vector
        def _(dve):
            dve.wait_ge(m.mixer_w_in, 16 * NW)
            dve.memset(k_stack[K_SCORE:K_FULL, :, :], 1.0).then_inc(consts, 1)
            dve.wait_ge(consts, 9)
            dve.tensor_copy(expert_f[:, :], expert_i[:, :]).then_inc(masks, 1)
            dve.wait_ge(masks, 7)
            dve.tensor_scalar(first_slot[:, :], expert_f[:, :], float(CAP), None, ALU.mult)\
                .then_inc(src_free, 1)

            def first_norm(b):
                step = Steps(dve, norm_s, b * LN_STEPS, LN_STEPS)
                emit_layernorm(dve, step, m, [x_tile(b, t) for t in range(NT)], xn_ready, out=xn)
                step.close()

            def second_norm(b):
                step = Steps(dve, inputs_s, b * LN_STEPS, LN_STEPS)
                emit_layernorm(dve, step, m, [x_tile(b, t) for t in range(NT)], xn2_ready,
                               lambda t: t == 0 and (dve.wait_ge(x_ready, b + 1), take_wait(dve, m)))
                step.close()

            def linear_attention(b, routed=None):
                step = Steps(dve, linear_s, b * (2 * NT), 2 * NT)
                dve.wait_ge(hT_done, b + 1)
                dve.tensor_scalar(hT[:, 1, :], bank(m, 7), m.mod_cols1[:, 1, 1, bass.ds(b, 1)],
                                  m.mod_cols1[:, 0, 1, bass.ds(b, 1)], ALU.mult, ALU.add).then_inc(hT_dve, 1)
                if routed is not None:
                    make_src(routed)
                for c in range(C):
                    dve.wait_ge(q_done, b * C + c + 1)
                    dve.tensor_scalar(q_exp[:, c, :], bank(m, 4 + c), 0.0, None, ALU.min).then_inc(q_min, 1)

                def add_k(t):
                    dve.wait_ge(k_act, b * (3 * NT) + 3 * t + 3)
                    dve.tensor_tensor(k_exp[:, t, :], k_exp[:, t, :], k_relu[:, t, :], ALU.add).then_inc(kf_ready, 1)

                for t in range(NT):
                    dve.wait_ge(kv_done, b * NT + t + 1)
                    dve.tensor_scalar(k_exp[:, t, :], bank(m, t)[:, 0:D], 0.0, None, ALU.min).then_inc(k_min, 1)
                    if t:
                        add_k(t - 1)
                add_k(NT - 1)
                for c in range(C):
                    dve.wait_ge(q_act, b * (2 * C) + 2 * c + 2)
                    dve.tensor_tensor(q_exp[:, c, :], q_exp[:, c, :], q_relu[:, c, :], ALU.add).then_inc(qf_ready, 1)
                dve.wait_ge(gram_done, b * C + C)
                for c in range(C):
                    gram = bank(m, 4)[:, c * (P + 1):(c + 1) * (P + 1)]
                    dve.tensor_tensor(kv_bd[:, c, 0:P], gram[:, 0:P],
                                      block_mask[:, :, :].rearrange("p h d -> p (h d)"), ALU.mult)\
                        .then_inc(kvbd_ready, 1)
                    dve.tensor_tensor(kv_bd[:, c, P:P + HPC1], head_mask[:, :],
                                      gram[:, P:P + 1].to_broadcast([P, HPC1]), ALU.mult)\
                        .then_inc(kvbd_ready, 1)
                for t in range(NT):
                    dve.wait_ge(n_done, b * NT + t + 1)
                    nd = bank(m, t)[:, 0:C * (P + HPC1)].rearrange("p (c n) -> p c n", c=C)
                    step(dve.tensor_scalar(den[:, t, :].rearrange("p (c h) -> p c h", c=C), nd[:, :, P:P + HPC1],
                                           EPS_DEN, None, ALU.add))
                    step.settle()
                    step(dve.reciprocal(den[:, t, :], den[:, t, :]))
                    step.settle()
                    for c in range(C):
                        ins = dve.tensor_tensor(o1[:, t, c * P:(c + 1) * P].rearrange("p (h d) -> p h d", h=HPC1),
                                                nd[:, c, 0:P].rearrange("p (h d) -> p h d", h=HPC1),
                                                den[:, t, c * HPC1:(c + 1) * HPC1].rearrange("p (h a) -> p h a", a=1)
                                                .to_broadcast([P, HPC1, DH1]), ALU.mult)
                        ins.then_inc(o1_ready, 1)
                dve.wait_ge(bias_added, b + 1)
                for t in range(NT):
                    dve.wait_ge(p1_done, b * NT + t + 1)
                    dve.tensor_tensor(scaled[:, t, :], bank(m, t)[:, 0:D], m.gate_rows[:, 0, :], ALU.mult)\
                        .then_inc(scaled_ready, 1)
                step.close()

            def grouped_inputs(b):
                dve.wait_ge(h2_done, b + 1)
                dve.tensor_scalar(h2T[:, 1, :], bank(m, 5), m.mod_cols1[:, 3, 1, bass.ds(b, 1)],
                                  m.mod_cols1[:, 2, 1, bass.ds(b, 1)], ALU.mult, ALU.add).then_inc(h2_dve, 1)
                for i in range(C + 1):
                    dve.wait_ge(part0, b * (C + 1) + i + 1)
                    if i < C:
                        dve.scalar_tensor_tensor(out=q_rest[:, i, :], in0=bank(m, i), scalar=qb[:, i:i + 1],
                                                 in1=q_part[:, 0, i, :], op0=ALU.add, op1=ALU.subtract)\
                            .then_inc(rest, 1)
                    else:
                        dve.scalar_tensor_tensor(out=k_rest, in0=bank(m, 2)[0:DKV, :], scalar=kb[:, 0:1],
                                                 in1=k_part[:, 0, :], op0=ALU.add, op1=ALU.subtract)\
                            .then_inc(rest, 1)
                for i in range(C + 1):
                    dve.wait_ge(part1, b * (C + 1) + i + 1)
                    if i < C:
                        dve.tensor_tensor(q_part[:, 2, i, :], q_rest[:, i, :], q_part[:, 1, i, :], ALU.subtract)\
                            .then_inc(part2, 1)
                    else:
                        dve.tensor_tensor(k_part[:, 2, :], k_rest, k_part[:, 1, :], ALU.subtract)\
                            .then_inc(part2, 1)
                dve.wait_ge(v_done, b + 1)
                dve.tensor_tensor(v_tile[:, :, :, 0:DHQ],
                                  bank(m, 3)[:, 0:NT * DKV].rearrange("p (t g d) -> p t g d", t=NT, g=HKV),
                                  vb[:, :].rearrange("p (t g d) -> p t g d", t=1, g=HKV)
                                  .to_broadcast([P, NT, HKV, DHQ]), ALU.add).then_inc(v_ready, 1)

            def grouped_attention(b, second=None, first=None, routed=None):
                step = Steps(dve, grouped_s, b * GROUPED_STEPS, GROUPED_STEPS)

                def row_max(g, k):
                    n = 16 * g + k
                    dve.wait_ge(s_done, b * 64 + n + 1)
                    dve.tensor_reduce(negmax[:, k // 4, REP * g + k % 4:REP * g + k % 4 + 1], bank(m, n % 2), AX.X,
                                      ALU.max, negate=True).then_inc(max_read, 1)

                def cut_max(g):
                    dve.wait_ge(max_read, b * 64 + 16 * g + 16)
                    part, head = max_part[:, g, :, :, :], slice(REP * g, REP * (g + 1))
                    step(dve.tensor_copy(part[:, :, :, 0], negmax[:, :, head]))
                    step.settle()
                    step(dve.tensor_tensor(max_rest[:, :, head], negmax[:, :, head], part[:, :, :, 0], ALU.subtract))
                    step.settle()
                    step(dve.tensor_copy(part[:, :, :, 1], max_rest[:, :, head]))
                    step.settle()
                    dve.tensor_tensor(part[:, :, :, 2], max_rest[:, :, head], part[:, :, :, 1], ALU.subtract)\
                        .then_inc(maxp_ready, 1)

                for n in range(64):
                    row_max(n // 16, n % 16)
                    if n % 16 == 15:
                        cut_max(n // 16)
                if routed is not None:
                    choose(routed)
                if second is not None:
                    second_norm(second)
                if first is not None:
                    first_norm(first)
                if routed is not None:
                    place(routed)
                for t in range(NT):
                    dve.wait_ge(ot_done, b * NT + t + 1)
                    o = bank(m, t).rearrange("p (h w) -> p h w", w=VW)
                    step(dve.reciprocal(osum[:, t, :], o[:, :, DHQ]))
                    step.settle()
                    dve.tensor_tensor(o1[:, t, :].rearrange("p (h d) -> p h d", h=HQ), o[:, :, 0:DHQ],
                                      osum[:, t, :].rearrange("p (h a) -> p h a", a=1).to_broadcast([P, HQ, DHQ]),
                                      ALU.mult).then_inc(o2_ready, 1)
                for t in range(NT):
                    dve.wait_ge(r_done, b * NT + t + 1)
                    dve.tensor_tensor(resid[:, t, :], bank(m, 6 + t % 2)[:, 0:D], ob[:, :], ALU.add)\
                        .then_inc(r_ready, 1)
                step.close()

            def make_src(b):
                step = Steps(dve, src_s, b * RMS_STEPS, RMS_STEPS)
                emit_rms_scale(dve, step, m, [resid[:, t, :] for t in range(NT)], EPS_NORM,
                               lambda t: dve.wait_ge(r_ready, b * NT + t + 1))
                dve.wait_ge(src_free, b + 1)
                for t in range(NT):
                    dve.scalar_tensor_tensor(out=src[:, t, :], in0=resid[:, t, :], scalar=m.rstd[:, t:t + 1],
                                             in1=n1w[:, :], op0=ALU.mult, op1=ALU.mult).then_inc(src_ready, 1)
                step.close()

            def choose(b):
                step = Steps(dve, route_s, b * ROUTER_STEPS, CHOOSE_STEPS)
                dve.wait_ge(lexp_ready, b + 1)
                step(dve.tensor_scalar(probs[:, :, :], probs[:, :, :], 1.0, None, ALU.add))
                step.settle()
                step(dve.reciprocal(probs[:, :, :], probs[:, :, :]))
                step.settle()
                take_wait(dve, m)
                step(dve.tensor_copy(load_before[:, 0, :], load_before[:, NT, :]))
                for t in range(NT):
                    step(dve.max(top[:, t, :], probs[:, t, :]))
                step.settle()
                take_wait(dve, m)
                step(dve.tensor_tensor(wsum[:, :, :], top[:, :, 0:1], top[:, :, 1:2], ALU.add))
                for t in range(NT):
                    step(dve.max_index(top_i[:, t, :], top[:, t, :], probs[:, t, :]))
                step.settle()
                step(dve.tensor_copy(sel[:, :, :], top_i[:, :, 0:TOPK]))
                step(dve.tensor_scalar(wsum[:, :, :], wsum[:, :, :], 1e-6, None, ALU.add))
                step.settle()
                step(dve.reciprocal(wsum[:, :, :], wsum[:, :, :]))
                for k in range(TOPK):
                    step(dve.tensor_tensor(chosen[:, k, :, :],
                                           expert_f[:, :].rearrange("p (t e) -> p t e", t=1).to_broadcast([P, NT, E]),
                                           sel[:, :, k:k + 1].to_broadcast([P, NT, E]), ALU.is_equal))
                step.settle()
                step(dve.tensor_tensor(load[:, :, :], chosen[:, 0, :, :], chosen[:, 1, :, :], ALU.add))
                step(dve.tensor_tensor(wk[:, :, :], top[:, :, 0:TOPK], wsum[:, :, :].to_broadcast([P, NT, TOPK]),
                                       ALU.mult))
                step.settle()
                for t in range(NT):
                    dve.tensor_tensor(load_before[:, t + 1, :], load_before[:, t, :], load[:, t, :], ALU.add)\
                        .then_inc(load_ready, 1)
                    dve.wait_ge(load_ready, b * NT + t + 1)
                step.close()

            def place(b):
                step = Steps(dve, route_s, b * ROUTER_STEPS + CHOOSE_STEPS, ROUTER_STEPS - CHOOSE_STEPS)
                dve.wait_ge(rank_done, b + 1)
                rank = bank(m, 0)[:, 0:NT * E].rearrange("p (t e) -> p t e", t=NT)
                step(dve.tensor_scalar(over[:, :, :], rank, float(CAP), INVALID, ALU.is_ge, ALU.mult))
                step(dve.tensor_tensor(slots_e[:, :, :], rank, first_slot[:, :].rearrange("p (t e) -> p t e", t=1)
                                       .to_broadcast([P, NT, E]), ALU.add))
                step.settle()
                step(dve.tensor_tensor(slots_e[:, :, :], slots_e[:, :, :], over[:, :, :], ALU.add))
                step.settle()
                for k in range(TOPK):
                    step(dve.tensor_tensor(chosen[:, k, :, :], chosen[:, k, :, :], slots_e[:, :, :], ALU.mult))
                step.settle()
                for k in range(TOPK):
                    step(dve.tensor_reduce(slot_k[:, :, k], chosen[:, k, :, :], AX.X, ALU.add))
                step.settle()
                step(dve.tensor_scalar(valid[:, :, :], slot_k[:, :, :], INVALID, None, ALU.is_lt))
                dve.tensor_copy(scatter_idx[:, :, :], slot_k[:, :, :]).then_inc(sidx_ready, 1)
                step.settle()
                at = bass.ds(b * (NT * TOPK), NT * TOPK)
                step(dve.tensor_tensor(m.gather_idx[:, at], slot_k[:, :, :].rearrange("p t k -> p (t k)"),
                                       valid[:, :, :].rearrange("p t k -> p (t k)"), ALU.mult))
                step(dve.tensor_tensor(m.gather_wt[:, at], wk[:, :, :].rearrange("p t k -> p (t k)"),
                                       valid[:, :, :].rearrange("p t k -> p (t k)"), ALU.mult))
                step.close()

            first_norm(0)
            linear_attention(0)
            second_norm(0)
            first_norm(1)
            grouped_inputs(0)
            linear_attention(1)
            grouped_attention(0, second=1, first=2)
            grouped_inputs(1)
            linear_attention(2, routed=0)
            with dve.Fori(2, B - 1) as b:
                grouped_attention(b - 1, second=b, first=b + 1, routed=b - 2)
                grouped_inputs(b)
                linear_attention(b + 1, routed=b - 1)
            grouped_attention(B - 2, second=B - 1, routed=B - 3)
            grouped_inputs(B - 1)
            make_src(B - 2)
            grouped_attention(B - 1, routed=B - 2)
            make_src(B - 1)
            choose(B - 1)
            place(B - 1)

        @block.tensor
        def _(pe):
            pe.wait_ge(m.mixer_w_in, 16 * NW)
            pe.wait_ge(consts, 9)

            def linear_attention(b, routed=None, after_inputs=True):
                if routed is not None:
                    pe.wait_ge(r_ready, routed * NT + NT)
                emit_transpose_tiles(pe, m, xn, (6, 7), lambda t: pe.wait_ge(xn_ready, b * NT + t + 1), hT_done)
                pe.wait_ge(hT_act, b + 1)
                pe.wait_ge(hT_dve, b + 1)
                for o in range(C):
                    for c in range(C):
                        mm = pe.matmul(bank(m, 4 + o), wq[:, c, o * P:(o + 1) * P], hT[:, c, :],
                                       start=(c == 0), stop=(c == C - 1))
                    mm.then_inc(q_done, 1)
                if after_inputs:
                    pe.wait_ge(rest, (b - 1) * (C + 1) + C + 1)
                    pe.wait_ge(v_ready, b)
                for t in range(NT):
                    for c in range(C):
                        mm = pe.matmul(bank(m, t), hT[:, c, t * P:(t + 1) * P], wkv[:, c, :],
                                       start=(c == 0), stop=(c == C - 1))
                    mm.then_inc(kv_done, 1)
                if routed is not None:
                    transpose_src(routed)
                pe.wait_ge(kf_ready, b * NT + NT)
                for c in range(C):
                    for t in range(NT):
                        mm = pe.matmul(bank(m, 4)[:, c * (P + 1):(c + 1) * (P + 1)],
                                       k_exp[:, t, c * P:(c + 1) * P], v_one[:, t, c, :],
                                       start=(t == 0), stop=(t == NT - 1))
                    mm.then_inc(gram_done, 1)
                if routed is not None:
                    logits(routed)
                pe.wait_ge(qf_ready, b * C + C)
                pe.wait_ge(kvbd_ready, b * (2 * C) + 2 * C)
                for t in range(NT):
                    for c in range(C):
                        mm = pe.matmul(bank(m, t)[:, c * (P + HPC1):(c + 1) * (P + HPC1)],
                                       q_exp[:, c, t * P:(t + 1) * P], kv_bd[:, c, :], start=True, stop=True)
                    mm.then_inc(n_done, 1)

                def transpose1(t):
                    pe.wait_ge(o1_ready, b * (C * NT) + C * t + C)
                    if t >= 2:
                        pe.wait_ge(o1T_ready, b * NT + t - 1)
                    for c in range(C):
                        mm = pe.transpose(bank(m, 6 + t % 2)[:, c * P:(c + 1) * P], o1[:, t, c * P:(c + 1) * P],
                                          m.ident[:, :])
                    mm.then_inc(o1T_done, 1)

                def project1(t):
                    pe.wait_ge(o1T_ready, b * NT + t + 1)
                    for c in range(C):
                        mm = pe.matmul(bank(m, t)[:, 0:D], o1T[:, t % 2, c, :], wo[:, c, :],
                                       start=(c == 0), stop=(c == C - 1))
                    mm.then_inc(p1_done, 1)

                transpose1(0)
                for t in range(1, NT):
                    transpose1(t)
                    project1(t - 1)
                project1(NT - 1)
                pe.wait_ge(scaled_ready, b * NT + NT)
                take_wait(pe, m)

            def grouped_inputs(b):
                emit_transpose_tiles(pe, m, m.xn, (4, 5), lambda t: pe.wait_ge(xn2_ready, b * NT + t + 1), h2_done)
                pe.wait_ge(h2_act, b + 1)
                pe.wait_ge(h2_dve, b + 1)
                for o in range(C + 1):
                    for c in range(C):
                        if o < C:
                            mm = pe.matmul(bank(m, o), qw[:, c, o * P:(o + 1) * P], h2T[:, c, :],
                                           start=(c == 0), stop=(c == C - 1))
                        else:
                            mm = pe.matmul(bank(m, 2)[0:DKV, :], kw[:, c, :], h2T[:, c, :],
                                           start=(c == 0), stop=(c == C - 1))
                    mm.then_inc(qk_done, 1)
                for t in range(NT):
                    for c in range(C):
                        mm = pe.matmul(bank(m, 3)[:, t * DKV:(t + 1) * DKV], h2T[:, c, t * P:(t + 1) * P], vw[:, c, :],
                                       start=(c == 0), stop=(c == C - 1))
                mm.then_inc(v_done, 1)

            def grouped_attention(b, routed=None):
                pe.wait_ge(rest, b * (C + 1) + C + 1)
                pe.wait_ge(v_ready, b + 1)
                pe.wait_ge(stack_in, b * (32 * NSLOT) + 32 * NSLOT)
                def max_scores(g, k):
                    n = 16 * g + k
                    if n >= 2:
                        pe.wait_ge(max_read, b * 64 + n - 1)
                    pe.matmul(bank(m, n % 2), q_stack[0:K_SCORE, REP * g + k % 4, (k // 4) * P:(k // 4 + 1) * P],
                              k_stack[0:K_SCORE, g, :], start=True, stop=True).then_inc(s_done, 1)

                def transpose_max(g):
                    if g >= 2:
                        pe.wait_ge(oraw_ready, b * HKV + g - 1)
                        take_wait(pe, m)
                    pe.wait_ge(maxp_ready, b * HKV + g + 1)
                    take_wait(pe, m)
                    for t in range(NT):
                        mm = pe.transpose(bank(m, 6 + g % 2).bitcast(BF16)[0:3 * REP, t * P:(t + 1) * P],
                                          max_part[:, g, t, :, :].rearrange("p h j -> p (h j)"), m.ident_bf[:, :])
                    mm.then_inc(maxT_done, 1)

                def unit(u):
                    return u // 8, u % 2, (u // 2) % 4

                def scoresT(u):
                    g, pair, kc = unit(u)
                    if u % 8 == 0:
                        pe.wait_ge(max_in[g], b * (16 * REP) + 16 * REP)
                    if u >= 2:
                        pe.wait_ge(pT_ready, b * 32 + u - 1)
                    for j in range(2):
                        mm = pe.matmul(bank(m, 2 + 2 * (u % 2) + j), k_stack[:, g, kc * P:(kc + 1) * P],
                                       q_stack[:, REP * g + 2 * pair + j, :], start=True, stop=True)
                    mm.then_inc(sT_done, 1)

                def weigh(u):
                    g, pair, kc = unit(u)
                    pe.wait_ge(pT_ready, b * 32 + u + 1)
                    for j in range(2):
                        q0 = 32 * (2 * pair + j)
                        mm = pe.matmul(bank(m, 6 + g % 2)[q0:q0 + VW, :], v_tile[:, kc, g, :], pT[:, u % 4, j, :],
                                       start=(kc == 0), stop=(kc == NT - 1))
                    mm.then_inc(pv_done, 1)

                for n in range(MAX_AHEAD):
                    max_scores(n // 16, n % 16)
                    if n == 19:
                        transpose_max(0)
                scoresT(0)
                scoresT(1)
                for u in range(0, 32, 2):
                    ahead = [(n // 16, n % 16) for n in range(MAX_AHEAD + 2 * u, min(MAX_AHEAD + 2 * u + 4, 64))]
                    if u + 2 < 32:
                        scoresT(u + 2)
                        for g, k in ahead[:2]:
                            max_scores(g, k)
                        scoresT(u + 3)
                    weigh(u)
                    weigh(u + 1)
                    for g, k in ahead[2:]:
                        max_scores(g, k)
                    if u + 3 in MAX_AT:
                        transpose_max(1 + MAX_AT.index(u + 3))
                    if u == 28 and routed is not None:
                        count(routed)

                if routed is not None:
                    pe.wait_ge(sidx_ready, routed + 1)
                    take_wait(pe, m)
                pe.wait_ge(oraw_ready, b * HKV + HKV)
                for t in range(NT):
                    for g in range(HKV):
                        mm = pe.transpose(bank(m, t)[:, g * P:(g + 1) * P], oraw[:, g, t * P:(t + 1) * P],
                                          m.ident[:, :])
                    mm.then_inc(ot_done, 1)

                def transpose2(t):
                    pe.wait_ge(o2_ready, b * NT + t + 1)
                    if t >= 2:
                        pe.wait_ge(o2T_ready, b * NT + t - 1)
                    for c in range(C):
                        mm = pe.transpose(bank(m, 4 + t % 2)[:, c * P:(c + 1) * P], o1[:, t, c * P:(c + 1) * P],
                                          m.ident[:, :])
                    mm.then_inc(o2T_done, 1)

                def project2(t):
                    pe.wait_ge(o2T_ready, b * NT + t + 1)
                    if t >= 2:
                        pe.wait_ge(r_ready, b * NT + t - 1)
                    out = bank(m, 6 + t % 2)
                    for c in range(C):
                        pe.matmul(out[:, 0:D], o1T[:, t % 2, c, :], ow[:, c, :], start=(c == 0), stop=False,
                                  skip_group_check=True)
                    for c in range(C):
                        mm = pe.matmul(out[:, c * P:(c + 1) * P], h2T[:, c, t * P:(t + 1) * P], m.ident[:, :],
                                       start=False, stop=True, skip_group_check=True)
                    mm.then_inc(r_done, 1)

                transpose2(0)
                for t in range(1, NT):
                    transpose2(t)
                    project2(t - 1)
                project2(NT - 1)

            def transpose_src(b):
                emit_transpose_tiles(pe, m, src, (6, 7), lambda t: pe.wait_ge(src_ready, b * NT + t + 1), srcT_done)

            def logits(b):
                pe.wait_ge(srcT_ready, b * C + C)
                for t in range(NT):
                    for c in range(C):
                        mm = pe.matmul(bank(m, 5)[:, t * E:(t + 1) * E], oraw[:, c, t * P:(t + 1) * P],
                                       gate_w[:, c, :], start=(c == 0), stop=(c == C - 1))
                mm.then_inc(logits_done, 1)

            def count(b):
                pe.wait_ge(load_ready, b * NT + NT)
                for t in range(NT):
                    pe.matmul(bank(m, 0)[:, t * E:(t + 1) * E], before[:, :], load[:, t, :], start=True, stop=False)
                    mm = pe.matmul(bank(m, 0)[:, t * E:(t + 1) * E], ones_bf[:, :], load_before[:, t, :],
                                   start=False, stop=True)
                mm.then_inc(rank_done, 1)

            linear_attention(0, after_inputs=False)
            grouped_inputs(0)
            linear_attention(1)
            grouped_attention(0)
            grouped_inputs(1)
            linear_attention(2, routed=0)
            with pe.Fori(2, B - 1) as b:
                grouped_attention(b - 1, routed=b - 2)
                grouped_inputs(b)
                linear_attention(b + 1, routed=b - 1)
            grouped_attention(B - 2, routed=B - 3)
            grouped_inputs(B - 1)
            transpose_src(B - 2)
            logits(B - 2)
            grouped_attention(B - 1, routed=B - 2)
            transpose_src(B - 1)
            logits(B - 1)
            count(B - 1)



def experts_block(nc, m, I, padded_dram, expert_out):
    U = 2 * CT
    ctx = ExitStack()
    with ctx:
        def sem(name):
            return ctx.enter_context(nc.semaphore("d_" + name))

        sb = tile_maker(nc, ctx)
        w1 = sb("w1_x", [P, 2, C, F1])
        w2 = sb("w2_x", [P, 2, NF1, D])
        xe = sb("xe", [P, 2, NT, D])
        xT = sb("xT_x", [P, C, S])
        actT = sb("actT_x", [P, NF1, S])
        ye = sb("ye", [P, 2, NT, D])
        w_in = [sem(f"w_in{u}") for u in range(2)]
        x_in = [sem(f"x_in{u}") for u in range(2)]
        stored = [sem(f"stored{u}") for u in range(2)]
        xT_done = sem("xT_done")
        xT_act = sem("xT_act")
        xT_dve = sem("xT_dve")
        up_done = sem("up_done")
        gelu_ready = sem("gelu_ready")
        y_done = sem("y_done")
        ye_ready = sem("ye_ready")
        ye_free = sem("ye_free")
        block = ctx.enter_context(nc.Block())

        @block.sync
        def _(sp):
            def load_expert(e, slot):
                sp.dma_start(w1[:, slot, :, :], I["L1_ffn_w1"][bass.ds(e, 1), :, :]
                             .rearrange("e (c p) f -> p (e c) f", p=P)).then_inc(w_in[slot], 16)
                sp.dma_start(w2[:, slot, :, :], I["L1_ffn_w2"][bass.ds(e, 1), :, :]
                             .rearrange("e (f p) d -> p (e f) d", p=P)).then_inc(w_in[slot], 16)

            def load_rows(i, u):
                sp.dma_start(xe[:, u % 2, :, :], padded_dram[bass.ds((i * U + u) * S, S), :]
                             .rearrange("(t p) d -> p t d", p=P)).then_inc(x_in[u % 2], 16)

            def store_rows(i, u):
                sp.wait_ge(ye_ready, i * (2 * U) + 2 * u + 2)
                sp.dma_start(expert_out[bass.ds((i * U + u) * S, S), :].rearrange("(t p) d -> p t d", p=P),
                             ye[:, u % 2, :, :]).then_inc(stored[u % 2], 16)

            def turn(i, last):
                for u in range(U):
                    if not (last and u + 2 >= U):
                        sp.wait_ge(xT_done, i * U + u + 1)
                        load_rows(i, u + 2)
                    if u:
                        store_rows(i, u - 1)
                    if u == CT and not last:
                        load_expert(2 * i + 2, 0)
                store_rows(i, U - 1)
                if not last:
                    load_expert(2 * i + 3, 1)

            load_rows(0, 0)
            load_expert(0, 0)
            load_rows(0, 1)
            load_expert(1, 1)
            with sp.Fori(0, E // 2 - 1) as i:
                turn(i, False)
            turn(E // 2 - 1, True)

        @block.gpsimd
        def _(pool):
            pool.sem_inc(ye_free, 2)
            with pool.Fori(0, E // 2) as i:
                for u in range(U):
                    pool.wait_ge(stored[u % 2], i * (16 * CT) + 16 * (u // 2) + 16)
                    pool.sem_inc(ye_free, 1)

        @block.scalar
        def _(act):
            with act.Fori(0, E // 2) as i:
                def evacuate(u):
                    act.wait_ge(xT_done, i * U + u + 1)
                    act.activation(xT[:, 0, :], bank(m, 0), ACT.Copy).then_inc(xT_act, 1)

                evacuate(0)
                for u in range(U):
                    for f in range(NF1):
                        act.wait_ge(up_done, i * (U * NF1) + u * NF1 + f + 1)
                        act.activation(actT[:, f, :], bank(m, 2 + f), ACT.Gelu).then_inc(gelu_ready, 1)
                    if u + 1 < U:
                        evacuate(u + 1)

        @block.vector
        def _(dve):
            with dve.Fori(0, E // 2) as i:
                def evacuate(u):
                    dve.wait_ge(xT_done, i * U + u + 1)
                    dve.tensor_copy(xT[:, 1, :], bank(m, 1)).then_inc(xT_dve, 1)

                evacuate(0)
                for u in range(U):
                    if u + 1 < U:
                        evacuate(u + 1)
                    dve.wait_ge(ye_free, i * U + u + 1)
                    take_wait(dve, m)
                    for h in range(2):
                        dve.wait_ge(y_done, i * (2 * U) + 2 * u + h + 1)
                        dve.tensor_copy(ye[:, u % 2, 2 * h:2 * h + 2, :].rearrange("p t d -> p (t d)"),
                                        bank(m, 6 + h)).then_inc(ye_ready, 1)

        @block.tensor
        def _(pe):
            with pe.Fori(0, E // 2) as i:
                def transpose(u):
                    pe.wait_ge(x_in[u % 2], i * (16 * CT) + 16 * (u // 2) + 16)
                    for t in range(NT):
                        for c in range(C):
                            mm = pe.transpose(bank(m, c)[:, t * P:(t + 1) * P], xe[:, u % 2, t, c * P:(c + 1) * P],
                                              m.ident[:, :])
                    mm.then_inc(xT_done, 1)

                def up(u):
                    pe.wait_ge(xT_act, i * U + u + 1)
                    pe.wait_ge(xT_dve, i * U + u + 1)
                    if u % CT == 0:
                        pe.wait_ge(w_in[u // CT], i * 32 + 32)
                    for f in range(NF1):
                        for c in range(C):
                            mm = pe.matmul(bank(m, 2 + f), w1[:, u // CT, c, f * P:(f + 1) * P], xT[:, c, :],
                                           start=(c == 0), stop=(c == C - 1))
                        mm.then_inc(up_done, 1)

                def down(u):
                    pe.wait_ge(gelu_ready, i * (U * NF1) + (u + 1) * NF1)
                    for h in range(2):
                        if u:
                            pe.wait_ge(ye_ready, i * (2 * U) + 2 * u - 1 + h)
                        for t in range(2 * h, 2 * h + 2):
                            for f in range(NF1):
                                mm = pe.matmul(bank(m, 6 + h)[:, (t % 2) * D:(t % 2 + 1) * D],
                                               actT[:, f, t * P:(t + 1) * P], w2[:, u // CT, f, :],
                                               start=(f == 0), stop=(f == NF1 - 1))
                        mm.then_inc(y_done, 1)

                transpose(0)
                for u in range(U):
                    up(u)
                    if u + 1 < U:
                        transpose(u + 1)
                    down(u)
                pe.wait_ge(ye_ready, i * (2 * U) + 2 * U)
                take_wait(pe, m)


def combine_block(nc, m, I, mods_dram, src_dram, expert_out, out):
    ctx = ExitStack()
    with ctx:
        def sem(name):
            return ctx.enter_context(nc.semaphore("e_" + name))

        sb = tile_maker(nc, ctx)
        src = sb("src_e", [P, 2, NT, D])
        gate2 = sb("gate2", [P, 2, D])
        gate_norm = sb("gate_norm", [P, 2, D])
        n2w = sb("n2w_rows", [P, D])
        idx_b = sb("idx_b", [P, 2, NT * TOPK], U32)
        got = sb("got", [P, 2, NT, TOPK, D])
        y = sb("y_e", [P, 2, NT, D])
        part = sb("part_e", [P, 2, NT, D])
        z = sb("z_e", [P, 2, NT, D])
        n2w_in = sem("n2w_in")
        src_in = [sem(f"src_in{u}") for u in range(2)]
        gathered = [sem(f"gathered{u}") for u in range(2)]
        idx_ready = sem("idx_ready")
        used = sem("buffers_free")
        dve_s = sem("dve_steps")
        x_ready = sem("x_ready")
        stored = sem("stored")
        block = ctx.enter_context(nc.Block())
        PER = 2 * (2 * NT + 1 + NT) + RMS_STEPS + 2 * NT
        CHUNK = NT * D

        @block.sync
        def _(sp):
            sp.dma_start(n2w[:, :], I["L1_ffn_norm2_w"].partition_broadcast(P)).then_inc(n2w_in, 16)
            with sp.Fori(0, B // 2) as i:
                for u in range(2):
                    sp.wait_ge(used, 2 * i + u + 1)
                    sp.dma_start(src[:, u, :, :], src_dram[bass.ds((2 * i + u) * S, S), :]
                                 .rearrange("(t p) d -> p t d", p=P)).then_inc(src_in[u], 16)
                    sp.dma_start(gate2[:, u, :], mods_dram[1, bass.ds(2 * i + u, 1), 2:3, :]
                                 .rearrange("a s d -> (a s d)").partition_broadcast(P)).then_inc(src_in[u], 16)

        @block.gpsimd
        def _(pool):
            with pool.Fori(0, B // 2) as i:
                for u in range(2):
                    pool.wait_ge(used, 2 * i + u + 1)
                    take_wait(pool, m)
                    pool.tensor_copy(idx_b[:, u, :], m.gather_idx[:, bass.ds((2 * i + u) * (NT * TOPK), NT * TOPK)])\
                        .then_inc(idx_ready, 1)
                    pool.wait_ge(idx_ready, 2 * i + u + 1)
                    take_wait(pool, m)
                    for t in range(NT):
                        for k in range(TOPK):
                            at = idx_b[:, u, t * TOPK + k:t * TOPK + k + 1]
                            pool.indirect_dma_start(got[:, u, t, k, :], None, expert_out,
                                                    bass.IndirectOffsetOnAxis(ap=at, axis=0),
                                                    bounds_check=E * CAP - 1, oob_is_err=False)\
                                .then_inc(gathered[u], 16)

        @block.scalar
        def _(act):
            with act.Fori(0, B) as b:
                act.wait_ge(x_ready, b + 1)
                act.dma_start(out[bass.ds(b, 1), :, :].rearrange("b (t p) d -> p (b t) d", p=P),
                              m.x[:, bass.ds(b * CHUNK, CHUNK)].rearrange("p (t d) -> p t d", t=NT))\
                    .then_inc(stored, 16)
            act.wait_ge(stored, 16 * B)

        @block.vector
        def _(dve):
            dve.sem_inc(used, 2)
            dve.wait_ge(n2w_in, 16)
            with dve.Fori(0, B // 2) as i:
                step = Steps(dve, dve_s, i * PER, PER)

                def weight(u, t, k):
                    return m.gather_wt[:, bass.ds((2 * i + u) * (NT * TOPK) + t * TOPK + k, 1)]

                for u in range(2):
                    dve.wait_ge(src_in[u], i * 32 + 32)
                    take_wait(dve, m)
                    step(dve.tensor_tensor(gate_norm[:, u, :], gate2[:, u, :], n2w[:, :], ALU.mult))
                    dve.wait_ge(gathered[u], i * (16 * NT * TOPK) + 16 * NT * TOPK)
                    take_wait(dve, m)
                    for t in range(NT):
                        step(dve.scalar_tensor_tensor(out=part[:, u, t, :], in0=got[:, u, t, 0, :],
                                                      scalar=weight(u, t, 0), in1=src[:, u, t, :],
                                                      op0=ALU.mult, op1=ALU.add))
                    step.settle()
                    take_wait(dve, m)
                    for t in range(NT):
                        step(dve.scalar_tensor_tensor(out=y[:, u, t, :], in0=got[:, u, t, 1, :],
                                                      scalar=weight(u, t, 1), in1=part[:, u, t, :],
                                                      op0=ALU.mult, op1=ALU.add))
                    step.settle()
                    dve.sem_inc(used, 1)
                emit_rms_scale(dve, step, m, [y[:, u, t, :] for u in range(2) for t in range(NT)], EPS_NORM)
                for u in range(2):
                    for t in range(NT):
                        step(dve.scalar_tensor_tensor(out=z[:, u, t, :], in0=y[:, u, t, :],
                                                      scalar=m.rstd[:, u * NT + t:u * NT + t + 1],
                                                      in1=gate_norm[:, u, :], op0=ALU.mult, op1=ALU.mult))
                    step.settle()
                    xb = m.x[:, bass.ds((2 * i + u) * CHUNK, CHUNK)]
                    dve.tensor_tensor(xb, xb, z[:, u, :, :].rearrange("p t d -> p (t d)"), ALU.add)\
                        .then_inc(x_ready, 1)
                step.close()


def build_program(nc, I, out):
    mods_dram = nc.dram_tensor("mods", (2, B, 4, D), F32, kind="Internal").ap()
    qk_dram = nc.dram_tensor("qk_parts", (3, D + DKV, S), BF16, kind="Internal").ap()
    padded_dram = nc.dram_tensor("padded", (E * CAP, D), F32, kind="Internal").ap()
    expert_out = nc.dram_tensor("expert_out", (E * CAP, D), F32, kind="Internal").ap()
    src_dram = nc.dram_tensor("src_rows", (T, D), F32, kind="Internal").ap()
    ctx = ExitStack()
    with ctx:
        m = allocate(nc, ctx)
        setup_block(nc, m, I, mods_dram)
        local_attention_block(nc, m, I, mods_dram, padded_dram)
        routed_experts_block(nc, m, I, mods_dram)
        mixer_block(nc, m, I, mods_dram, qk_dram, padded_dram, src_dram)
        experts_block(nc, m, I, padded_dram, expert_out)
        combine_block(nc, m, I, mods_dram, src_dram, expert_out, out)


_TRANSPOSED = ("L1_attn_wq", "L1_attn_wk", "L1_attn_wv", "L1_attn_wo")


def kernel(**inputs):
    import numpy as _np
    import concourse.bacc as _bacc
    from concourse import mybir as _mybir
    from concourse.bass_utils import run_bass_kernel_spmd as _run

    nc = _bacc.Bacc("TRN2", target_bir_lowering=False, num_devices=1)
    arrays, aps = {}, {}
    for name, a in inputs.items():
        a = _np.asarray(a)
        a = _np.ascontiguousarray(a.T if name in _TRANSPOSED else a)
        arrays[f"in_{name}_dram"] = a
        aps[name] = nc.dram_tensor(f"in_{name}_dram", a.shape, _mybir.dt.from_np(a.dtype), kind="ExternalInput").ap()
    out = nc.dram_tensor("out_0_dram", (B, S, D), F32, kind="ExternalOutput").ap()
    build_program(nc, aps, out)
    r = _run(nc, [arrays], core_ids=[0])
    return r.results[0]["out_0_dram"]
```
